# Optimizing a Trainium2 kernel written in Bass

```python
import numpy as np
import jax
import jax.numpy as jnp

def _softmax(x, axis=-1):
    return jax.nn.softmax(x, axis=axis)

def _gelu(x):
    return jax.nn.gelu(x, approximate=True)

def _silu(x):
    return jax.nn.silu(x)

def _sigmoid(x):
    return jax.nn.sigmoid(x)

def _layernorm(x, axis=-1, eps=1e-05):
    m = jnp.mean(x, axis=axis, keepdims=True)
    v = jnp.var(x, axis=axis, keepdims=True)
    return (x - m) / jnp.sqrt(v + eps)

def _scatter_add(tgt, idx, src, axis=0):
    return tgt.at[idx].add(src)

def _segment_sum(src, seg, n):
    return jax.ops.segment_sum(src, seg, n)
kernel_name = 'mk_audio_tower_d2_tok_audfeat768_r4_44afe1'

def setup_inputs(seed: int=0):
    np.random.seed(seed)
    _w = jnp.asarray

    def _rec_inputs():
        import jax
        import jax.numpy as jnp
        _rk = jax.random.key(seed)
        x = -0.000147625 + 0.999875 * jax.random.normal(jax.random.fold_in(_rk, 1), (64, 64, 192), jnp.float32)
        return x
    x = _rec_inputs()

    def _L0_tok_setup():
        import jax, jax.numpy as jnp
        import numpy as np
        T = 16
        N = 196
        B = 16
        D = 192
        key = jax.random.key(seed)
        k1, k2, k3, k4, k5 = jax.random.split(key, 5)
        return {'x': jax.random.normal(k1, (N, B * T, D), dtype=jnp.float32), 'Wq': jax.random.normal(k2, (T // 2, T), dtype=jnp.float32) * 0.25, 'bq': jax.random.normal(k3, (T // 2,), dtype=jnp.float32) * 0.02, 'Wkv': jax.random.normal(k4, (T, T), dtype=jnp.float32) * 0.25, 'bkv': jax.random.normal(k5, (T // 2,), dtype=jnp.float32) * 0.02}
    _L0_tok_all = _L0_tok_setup()
    _L0_tok_in = {k: v for k, v in _L0_tok_all.items() if k in ('Wq', 'bq', 'Wkv', 'bkv')}
    del _L0_tok_all

    def _L0_attn_setup():
        import jax, jax.numpy as jnp
        import numpy as np
        D_MODEL = 192
        D_STATE = 128
        EXPAND = 2
        HEADDIM = 64
        D_INNER = D_MODEL * EXPAND
        NHEADS = D_INNER // HEADDIM
        CONV_K = 4
        D_IN_PROJ = 2 * D_INNER + 2 * D_STATE + NHEADS
        EPS = 1e-05

        def _layernorm(x, w, b):
            mu = jnp.mean(x, -1, keepdims=True)
            var = jnp.mean(jnp.square(x - mu), -1, keepdims=True)
            return (x - mu) * jax.lax.rsqrt(var + EPS) * w + b

        def _causal_dw_conv(x, w, b):
            xt = jnp.transpose(x, (0, 2, 1))
            xt = jnp.pad(xt, ((0, 0), (0, 0), (CONV_K - 1, 0)))
            y = jax.lax.conv_general_dilated(xt, w, window_strides=(1,), padding='VALID', dimension_numbers=('NCH', 'OIH', 'NCH'), feature_group_count=x.shape[-1])
            return jnp.transpose(y, (0, 2, 1)) + b

        def _mamba_core(u, W_in, conv_w, conv_b, A_log, D, dt_bias, norm_w, W_out):
            Bsz, L, _ = u.shape
            zxbcdt = u @ W_in
            z = zxbcdt[..., :D_INNER]
            xBC = zxbcdt[..., D_INNER:D_INNER + D_INNER + 2 * D_STATE]
            dt = zxbcdt[..., -NHEADS:]
            xBC = jax.nn.silu(_causal_dw_conv(xBC, conv_w, conv_b))
            xs = xBC[..., :D_INNER].reshape(Bsz, L, NHEADS, HEADDIM)
            Bmat = xBC[..., D_INNER:D_INNER + D_STATE]
            Cmat = xBC[..., D_INNER + D_STATE:]
            dt = jax.nn.softplus(dt + dt_bias)
            A = -jnp.exp(A_log)
            dA = jnp.exp(dt * A)

            def step(h, inputs):
                dA_t, dt_t, B_t, C_t, x_t = inputs
                h = dA_t[:, :, None, None] * h + (dt_t[:, :, None] * x_t)[..., None] * B_t[:, None, None, :]
                y = jnp.einsum('bhpn,bn->bhp', h, C_t)
                return (h, y)
            h0 = jnp.zeros((Bsz, NHEADS, HEADDIM, D_STATE), u.dtype)
            seq = (jnp.moveaxis(dA, 1, 0), jnp.moveaxis(dt, 1, 0), jnp.moveaxis(Bmat, 1, 0), jnp.moveaxis(Cmat, 1, 0), jnp.moveaxis(xs, 1, 0))
            _, ys = jax.lax.scan(step, h0, seq)
            y = jnp.moveaxis(ys, 0, 1) + D[None, None, :, None] * xs
            y = y.reshape(Bsz, L, D_INNER)
            yg = y * jax.nn.silu(z)
            yn = yg * jax.lax.rsqrt(jnp.mean(jnp.square(yg), -1, keepdims=True) + EPS) * norm_w
            return yn @ W_out
        key = jax.random.key(seed)
        ks = jax.random.split(key, 12)
        B, L = (4, 1024)
        conv_ch = D_INNER + 2 * D_STATE
        inp = {'x': jax.random.normal(ks[0], (B, L, D_MODEL), dtype=jnp.float32), 'ln_w': jnp.ones((D_MODEL,), jnp.float32), 'ln_b': jnp.zeros((D_MODEL,), jnp.float32), 'W_in': jax.random.normal(ks[1], (D_MODEL, D_IN_PROJ), jnp.float32) * D_MODEL ** (-0.5), 'conv_w': jax.random.normal(ks[2], (conv_ch, 1, CONV_K), jnp.float32) * CONV_K ** (-0.5), 'conv_b': jnp.zeros((conv_ch,), jnp.float32), 'A_log': jnp.log(jnp.arange(1, NHEADS + 1, dtype=jnp.float32)), 'D': jnp.ones((NHEADS,), jnp.float32), 'dt_bias': jnp.log(jnp.expm1(jax.random.uniform(ks[3], (NHEADS,), jnp.float32, 0.001, 0.1))), 'norm_w': jnp.ones((D_INNER,), jnp.float32), 'W_out': jax.random.normal(ks[4], (D_INNER, D_MODEL), jnp.float32) * D_INNER ** (-0.5)}
        return inp
    _L0_attn_all = _L0_attn_setup()
    _L0_attn_in = {k: v for k, v in _L0_attn_all.items() if k in ('ln_w', 'ln_b', 'W_in', 'conv_w', 'conv_b', 'A_log', 'D', 'dt_bias', 'norm_w', 'W_out')}
    del _L0_attn_all

    def _L0_ffn_setup():
        import jax, jax.numpy as jnp
        import numpy as np
        B, T, C = (2, 256, 192)
        H, NE, K = (768, 8, 2)
        key = jax.random.key(seed)
        k1, k2, k3, k4 = jax.random.split(key, 4)
        x = jax.random.normal(k1, (B, T, C), dtype=jnp.float32)
        w_fc = jax.random.normal(k2, (C, H * NE), dtype=jnp.float32) * 0.02
        w_proj = jax.random.normal(k3, (H * NE, C), dtype=jnp.float32) * (0.02 * (2 * 12) ** (-0.5))
        w_gate = jax.random.normal(k4, (C, NE), dtype=jnp.float32) * 0.02
        return {'x': x, 'w_fc': w_fc, 'w_proj': w_proj, 'w_gate': w_gate}
    _L0_ffn_all = _L0_ffn_setup()
    _L0_ffn_in = {k: v for k, v in _L0_ffn_all.items() if k in ('w_fc', 'w_proj', 'w_gate')}
    del _L0_ffn_all

    def _L1_attn_setup():
        import jax, jax.numpy as jnp
        import numpy as np
        EMBED_DIM = 192
        SEQ_LEN = 256
        BATCH = 32
        ALPHA = 0.99

        def _decay_mask(sl: int, alpha: float) -> jnp.ndarray:
            i = jnp.arange(sl, dtype=jnp.float32)
            diff = i[:, None] - i[None, :]
            return jnp.where(diff >= 0, jnp.float32(alpha) ** diff, 0.0)
        key = jax.random.key(seed)
        k1, k2 = jax.random.split(key)
        x = jax.random.normal(k1, (BATCH, SEQ_LEN, EMBED_DIM), dtype=jnp.float32)
        W_qkv = jax.random.normal(k2, (EMBED_DIM, 3 * EMBED_DIM), dtype=jnp.float32) * EMBED_DIM ** (-0.5)
        b_qkv = jnp.zeros((3 * EMBED_DIM,), dtype=jnp.float32)
        return {'x': x, 'W_qkv': W_qkv, 'b_qkv': b_qkv}
    _L1_attn_all = _L1_attn_setup()
    _L1_attn_in = {k: v for k, v in _L1_attn_all.items() if k in ('W_qkv', 'b_qkv')}
    del _L1_attn_all

    def _L1_ffn_setup():
        import jax, jax.numpy as jnp
        import numpy as np
        B, T, H, F, E = (128, 32, 192, 768, 3)
        key = jax.random.key(seed)
        ks = jax.random.split(key, 4)
        s = 0.02
        return {'x': jax.random.normal(ks[0], (B, T, H), jnp.float32), 'Wg': jax.random.normal(ks[1], (E, H), jnp.float32) * s, 'W1': jax.random.normal(ks[2], (E, H, F), jnp.float32) * s, 'b1': jnp.zeros((E, F), jnp.float32), 'W2': jax.random.normal(ks[3], (E, F, H), jnp.float32) * s, 'b2': jnp.zeros((E, H), jnp.float32)}
    _L1_ffn_all = _L1_ffn_setup()
    _L1_ffn_in = {k: v for k, v in _L1_ffn_all.items() if k in ('Wg', 'W1', 'b1', 'W2', 'b2')}
    del _L1_ffn_all
    return {'x': x, 'L0_tok_Wq': _L0_tok_in['Wq'], 'L0_tok_bq': _L0_tok_in['bq'], 'L0_tok_Wkv': _L0_tok_in['Wkv'], 'L0_tok_bkv': _L0_tok_in['bkv'], 'L0_attn_ln_w': _L0_attn_in['ln_w'], 'L0_attn_ln_b': _L0_attn_in['ln_b'], 'L0_attn_W_in': _L0_attn_in['W_in'], 'L0_attn_conv_w': _L0_attn_in['conv_w'], 'L0_attn_conv_b': _L0_attn_in['conv_b'], 'L0_attn_A_log': _L0_attn_in['A_log'], 'L0_attn_D': _L0_attn_in['D'], 'L0_attn_dt_bias': _L0_attn_in['dt_bias'], 'L0_attn_norm_w': _L0_attn_in['norm_w'], 'L0_attn_W_out': _L0_attn_in['W_out'], 'L0_ffn_w_fc': _L0_ffn_in['w_fc'], 'L0_ffn_w_proj': _L0_ffn_in['w_proj'], 'L0_ffn_w_gate': _L0_ffn_in['w_gate'], 'L1_attn_W_qkv': _L1_attn_in['W_qkv'], 'L1_attn_b_qkv': _L1_attn_in['b_qkv'], 'L1_ffn_Wg': _L1_ffn_in['Wg'], 'L1_ffn_W1': _L1_ffn_in['W1'], 'L1_ffn_b1': _L1_ffn_in['b1'], 'L1_ffn_W2': _L1_ffn_in['W2'], 'L1_ffn_b2': _L1_ffn_in['b2']}

def reference(x, L0_tok_Wq, L0_tok_bq, L0_tok_Wkv, L0_tok_bkv, L0_attn_ln_w, L0_attn_ln_b, L0_attn_W_in, L0_attn_conv_w, L0_attn_conv_b, L0_attn_A_log, L0_attn_D, L0_attn_dt_bias, L0_attn_norm_w, L0_attn_W_out, L0_ffn_w_fc, L0_ffn_w_proj, L0_ffn_w_gate, L1_attn_W_qkv, L1_attn_b_qkv, L1_ffn_Wg, L1_ffn_W1, L1_ffn_b1, L1_ffn_W2, L1_ffn_b2):
    import jax
    import jax.numpy as jnp

    def _L0_tok_ref(x, Wq, bq, Wkv, bkv):
        import jax, jax.numpy as jnp
        import numpy as np
        T = 16
        N = 196
        B = 16
        D = 192
        n, bt, d = x.shape
        t = Wkv.shape[0]
        b = bt // t
        t2 = t // 2
        scale = 1.0 / np.sqrt(d).astype(np.float32)
        xv = x.reshape(n, b, t, d).transpose(1, 0, 3, 2)
        q = jnp.einsum('bndt,st->bnds', xv, Wq) + bq
        kv_bias = jnp.concatenate([jnp.zeros_like(bkv), bkv])
        kv = jnp.einsum('bndt,st->bnds', xv, Wkv) + kv_bias
        kv = kv.reshape(b, n, d, 2, t2)
        k = kv[:, :, :, 0, :]
        v = kv[:, :, :, 1, :]
        q = q * scale
        attn = jax.nn.softmax(jnp.einsum('bnds,bndr->bnsr', q, k), axis=-1)
        out = q.transpose(0, 1, 3, 2) + jnp.einsum('bnsr,bndr->bnsd', attn, v)
        return out.transpose(1, 0, 2, 3).reshape(n, b * t2, d)

    def _L0_attn_ref(x, ln_w, ln_b, W_in, conv_w, conv_b, A_log, D, dt_bias, norm_w, W_out):
        import jax, jax.numpy as jnp
        import numpy as np
        D_MODEL = 192
        D_STATE = 128
        EXPAND = 2
        HEADDIM = 64
        D_INNER = D_MODEL * EXPAND
        NHEADS = D_INNER // HEADDIM
        CONV_K = 4
        D_IN_PROJ = 2 * D_INNER + 2 * D_STATE + NHEADS
        EPS = 1e-05

        def _layernorm(x, w, b):
            mu = jnp.mean(x, -1, keepdims=True)
            var = jnp.mean(jnp.square(x - mu), -1, keepdims=True)
            return (x - mu) * jax.lax.rsqrt(var + EPS) * w + b

        def _causal_dw_conv(x, w, b):
            xt = jnp.transpose(x, (0, 2, 1))
            xt = jnp.pad(xt, ((0, 0), (0, 0), (CONV_K - 1, 0)))
            y = jax.lax.conv_general_dilated(xt, w, window_strides=(1,), padding='VALID', dimension_numbers=('NCH', 'OIH', 'NCH'), feature_group_count=x.shape[-1])
            return jnp.transpose(y, (0, 2, 1)) + b

        def _mamba_core(u, W_in, conv_w, conv_b, A_log, D, dt_bias, norm_w, W_out):
            Bsz, L, _ = u.shape
            zxbcdt = u @ W_in
            z = zxbcdt[..., :D_INNER]
            xBC = zxbcdt[..., D_INNER:D_INNER + D_INNER + 2 * D_STATE]
            dt = zxbcdt[..., -NHEADS:]
            xBC = jax.nn.silu(_causal_dw_conv(xBC, conv_w, conv_b))
            xs = xBC[..., :D_INNER].reshape(Bsz, L, NHEADS, HEADDIM)
            Bmat = xBC[..., D_INNER:D_INNER + D_STATE]
            Cmat = xBC[..., D_INNER + D_STATE:]
            dt = jax.nn.softplus(dt + dt_bias)
            A = -jnp.exp(A_log)
            dA = jnp.exp(dt * A)

            def step(h, inputs):
                dA_t, dt_t, B_t, C_t, x_t = inputs
                h = dA_t[:, :, None, None] * h + (dt_t[:, :, None] * x_t)[..., None] * B_t[:, None, None, :]
                y = jnp.einsum('bhpn,bn->bhp', h, C_t)
                return (h, y)
            h0 = jnp.zeros((Bsz, NHEADS, HEADDIM, D_STATE), u.dtype)
            seq = (jnp.moveaxis(dA, 1, 0), jnp.moveaxis(dt, 1, 0), jnp.moveaxis(Bmat, 1, 0), jnp.moveaxis(Cmat, 1, 0), jnp.moveaxis(xs, 1, 0))
            _, ys = jax.lax.scan(step, h0, seq)
            y = jnp.moveaxis(ys, 0, 1) + D[None, None, :, None] * xs
            y = y.reshape(Bsz, L, D_INNER)
            yg = y * jax.nn.silu(z)
            yn = yg * jax.lax.rsqrt(jnp.mean(jnp.square(yg), -1, keepdims=True) + EPS) * norm_w
            return yn @ W_out
        u = _layernorm(x, ln_w, ln_b)
        out = _mamba_core(u, W_in, conv_w, conv_b, A_log, D, dt_bias, norm_w, W_out)
        return out + x

    def _L0_ffn_ref(x, w_fc, w_proj, w_gate):
        import jax, jax.numpy as jnp
        import numpy as np
        B, T, C = (2, 256, 192)
        H, NE, K = (768, 8, 2)
        router_logits = jnp.einsum('btc,ce->bte', x, w_gate)
        router_probs = jax.nn.softmax(router_logits, axis=-1)
        top_p, top_i = jax.lax.top_k(router_probs, K)
        top_p = top_p / jnp.sum(top_p, axis=-1, keepdims=True)
        wf = w_fc.reshape(C, H, NE)
        h_all = jnp.einsum('btc,che->bthe', x, wf)
        h = jnp.take_along_axis(h_all, top_i[:, :, None, :], axis=-1)
        h = jax.nn.gelu(h, approximate=True)
        wp = w_proj.reshape(H, C, NE)
        o_all = jnp.einsum('bthk,hce->btcke', h, wp)
        o = jnp.take_along_axis(o_all, top_i[:, :, None, :, None], axis=-1)[..., 0]
        o = jnp.einsum('btck,btk->btc', o, top_p)
        return o

    def _L1_attn_ref(x, W_qkv, b_qkv):
        import jax, jax.numpy as jnp
        import numpy as np
        EMBED_DIM = 192
        SEQ_LEN = 256
        BATCH = 32
        ALPHA = 0.99

        def _decay_mask(sl: int, alpha: float) -> jnp.ndarray:
            i = jnp.arange(sl, dtype=jnp.float32)
            diff = i[:, None] - i[None, :]
            return jnp.where(diff >= 0, jnp.float32(alpha) ** diff, 0.0)
        bs, sl, d = x.shape
        qkv = x @ W_qkv + b_qkv
        q, k, v = jnp.split(qkv, 3, axis=-1)
        M = _decay_mask(sl, ALPHA)
        dim_sqrt = jnp.sqrt(jnp.float32(d))
        scores = jnp.einsum('bsd,btd->bst', q, k) / dim_sqrt * M
        return jnp.einsum('bst,btd->bsd', scores, v)

    def _L1_ffn_ref(x, Wg, W1, b1, W2, b2):
        import jax, jax.numpy as jnp
        import numpy as np
        B, T, H, F, E = (128, 32, 192, 768, 3)
        scores = jax.nn.softmax(jnp.mean(x, axis=1) @ Wg.T, axis=-1)
        _, idx = jax.lax.top_k(scores, 1)
        sel = idx[:, 0]
        h = jax.nn.gelu(jnp.einsum('bth,ehf->betf', x, W1) + b1[None, :, None, :], approximate=False)
        y = jnp.einsum('betf,efh->beth', h, W2) + b2[None, :, None, :]
        w = scores * jax.nn.one_hot(sel, E, dtype=scores.dtype)
        out = jnp.einsum('beth,be->bth', y, w)
        return out
    h = _L0_tok_ref(x, L0_tok_Wq, L0_tok_bq, L0_tok_Wkv, L0_tok_bkv)
    h = h + _L0_attn_ref(_layernorm(h, axis=-1), L0_attn_ln_w, L0_attn_ln_b, L0_attn_W_in, L0_attn_conv_w, L0_attn_conv_b, L0_attn_A_log, L0_attn_D, L0_attn_dt_bias, L0_attn_norm_w, L0_attn_W_out)
    h = h + _L0_ffn_ref(_layernorm(h, axis=-1), L0_ffn_w_fc, L0_ffn_w_proj, L0_ffn_w_gate)
    h = h + _L1_attn_ref(_layernorm(h, axis=-1), L1_attn_W_qkv, L1_attn_b_qkv)
    h = h + _L1_ffn_ref(_layernorm(h, axis=-1), L1_ffn_Wg, L1_ffn_W1, L1_ffn_b1, L1_ffn_W2, L1_ffn_b2)
    return h

_drawn_inputs = setup_inputs


def setup_inputs(seed=0):
    import zlib

    import numpy as np

    out = dict(_drawn_inputs(seed))
    spreads = {'L0_attn_ln_w': (1.0, 0.2),
     'L0_attn_ln_b': (0.0, 0.1),
     'L0_attn_conv_b': (0.0, 0.1),
     'L0_attn_D': (1.0, 0.2),
     'L0_attn_norm_w': (1.0, 0.2),
     'L1_attn_b_qkv': (0.0, 0.1),
     'L1_ffn_b1': (0.0, 0.8),
     'L1_ffn_b2': (0.0, 0.8)}
    factors = {'L0_tok_bq': 3.405,
     'L0_tok_bkv': 8.0,
     'L0_ffn_w_fc': 5.962,
     'L0_ffn_w_proj': 5.813,
     'L0_ffn_w_gate': 6.973,
     'L1_ffn_Wg': 7.888,
     'L1_ffn_W1': 8.0,
     'L1_ffn_W2': 8.0}
    for name, (base, spread) in spreads.items():
        noise = np.random.default_rng([zlib.crc32(name.encode()), seed]).standard_normal(out[name].shape)
        drawn = base * np.exp(spread * noise) if base else spread * noise
        out[name] = jnp.asarray(drawn.astype(out[name].dtype))
    for name, factor in factors.items():
        out[name] = (out[name] * factor).astype(out[name].dtype)
    return out
```

```python
from contextlib import ExitStack

import concourse.bass as bass
import numpy as np
from concourse import mybir

F32 = mybir.dt.float32
I32 = mybir.dt.int32
U32 = mybir.dt.uint32
ALU = mybir.AluOpType
ACT = mybir.ActivationFunctionType
AX_X = mybir.AxisListType.X

P = 128
BLK = 32
D = 192
HD = 96
N_TOK = 2048
TILES = N_TOK // P
FR, FR2 = 16, 8
NH, HP = 6, 64
DI = NH * HP
DS = 128
CONV = DI + 2 * DS
KC = 4
NIN = 2 * DI + 2 * DS + NH
SB = 512
HID = 768
HC = HID // P
E1, E2 = 8, 3
T1 = (2 * N_TOK + E1 * (P - 1)) // P
T2 = (N_TOK + E2 * (P - BLK)) // P
EPS = 1e-5
SC = float(1.0 / np.sqrt(np.float32(D)))


def constant_table():
    p = np.arange(P)
    same32 = p[:, None] // BLK == p[None, :] // BLK
    diff = p[None, :] - p[:, None]
    decay = np.where(same32 & (diff >= 0), np.float32(0.99) ** np.maximum(diff, 0).astype(np.float32), 0) / np.sqrt(np.float32(D))
    parts = {
        "ident": np.eye(P),
        "group_bar": np.where(p[:, None] // FR2 == p[None, :] // FR2, 0.0, -1e30),
        "frame_sel": np.tile((p[:, None] // FR == np.arange(64)[None, :] // FR2), (1, 3)),
        "after": same32 & (p[:, None] > p[None, :]),
        "upto": (p[:, None] % BLK) <= np.arange(BLK)[None, :],
        "before": p[:, None] < p[None, :],
        "ones": np.ones((P, P)),
        "decay": decay,
        "seq_mean": same32 / float(BLK),
        "iota": np.tile(np.arange(64)[None, :], (P, 1)),
        "minus_half": np.full((P, 1), -0.5),
        "eps": np.full((P, 1), EPS),
    }
    at, n = {}, 0
    for name, a in parts.items():
        at[name] = (n, a.shape[1])
        n += a.shape[1]
    return np.concatenate([a.astype(np.float32) for a in parts.values()], axis=1), at


PARAMS = [("bq", 1), ("bkv", 1), ("ln_w", 2), ("ln_b", 2), ("conv_w", 20), ("conv_b", 5), ("skip", 3), ("norm_w", 3),
          ("b_qk", 4), ("A_log", NH), ("dt_bias", NH), ("bq_row", P), ("b_v", D), ("wq", 64), ("wk", 64), ("wv", 64)]


def param_places():
    at, n = {}, 0
    for name, w in PARAMS:
        at[name] = (n, w)
        n += w
    return at, n


class Tile:
    def __init__(self, k, odd):
        self.k, self.odd, self.i = k, odd, k * 2 + odd


def pipelined(eng, n, stages, depth, straight=False):
    first = depth + 1
    first += (n - first) % 2

    def step(t, turn=0):
        for s in reversed(range(depth)):
            i = t - s
            if stages.get(s) and 0 <= i and (i < n or not isinstance(turn, int)):
                stages[s](Tile(turn + i // 2, i % 2))

    if straight or first >= n:
        for t in range(n + depth - 1):
            step(t)
        return
    for t in range(first):
        step(t)
    with eng.Fori(0, (n - first) // 2) as turn:
        step(first, turn)
        step(first + 1, turn)
    for t in range(n, n + depth - 1):
        step(t)


def need(eng, sem, value):
    if not (isinstance(value, int) and value <= 0):
        eng.wait_ge(sem, value)


def need_alone(eng, m, *counts):
    counts = [(sem, value if isinstance(value, int) else eng.snap(value)) for sem, value in counts]
    if not all(isinstance(value, int) for _, value in counts):
        eng.wait_ge(m.loaded, 32)
    for sem, value in counts:
        need(eng, sem, value)


def after_first(eng, sem, turn, value):
    if not (isinstance(turn, int) and turn == 0):
        eng.wait_ge(sem, value)


def build(nc, dram):
    with ExitStack() as ctx:
        def sb(name, shape, dt=F32):
            return ctx.enter_context(nc.sbuf_tensor(name, shape, dt))

        m = Memory(nc, ctx, sb)
        ps = ctx.enter_context(nc.psum_tensor("psum", [P, 8, 512], F32))
        banks = [ps[:, n, :] for n in range(8)]
        with ExitStack() as early:
            s = SsmMemory(nc, early)
            merge_frames(nc, dram, m, s, banks)
            project_in(nc, dram, m, s, banks)
            state_space(nc, dram, m, s, ps)
            nc.clear_and_free_semaphores(s.semaphores)
            nc.all_engine_barrier()
        with ExitStack() as late:
            w = ExpertMemory(nc, late)
            load_weights(nc, dram, m, w)
            dispatch(nc, m, banks, 1, E1, 2 * TILES, m.pick[:, :], m.slot1, m.expert1, T1, True)
            scatter_rows(nc, m, 1, 2, m.slot1, dram["x1"], [(m.zeros_sent, 32)])
            experts(nc, m, ps, 1, E1, T1, m.expert1, dram["x1"], dram["y1"], m.w_fc, w.w_proj, None, None, ACT.Gelu_apprx_tanh,
                    [(m.w_fc_loaded, 16), (w.w_proj_loaded, 16)])
            linear_attention(nc, dram, m, ps)
            choose_one(nc, m, banks)
            dispatch(nc, m, banks, 2, E2, TILES, m.pick2[:, :], m.slot2, m.expert2, T2, False)
            scatter_rows(nc, m, 2, 1, m.slot2, dram["x2"], [(m.zeros_sent, 32)])
            experts(nc, m, ps, 2, E2, T2, m.expert2, dram["x2"], dram["y2"], w.w1, w.w2, w.b1, w.b2, ACT.Gelu, [(w.second_loaded, 64)])
            finish(nc, dram, m)


def load_weights(nc, dram, m, w):
    with nc.Block() as block:
        @block.sync
        def _(sp):
            sp.dma_start(w.w_proj[:, :], dram["w_proj"]).then_inc(w.w_proj_loaded, 16)
            for tile, name in ((w.w1, "w1"), (w.w2, "w2"), (w.b1, "b1"), (w.b2, "b2")):
                sp.dma_start(tile[:, :], dram[name]).then_inc(w.second_loaded, 16)


class Memory:

    def __init__(self, nc, ctx, sb):
        table, at = constant_table()
        places, width = param_places()
        self.const = sb("const", [P, table.shape[1]])
        self.param = sb("param", [P, width])
        self.c = {n: self.const[:, a:a + w] for n, (a, w) in at.items()}
        self.p = {n: self.param[:, a:a + w] for n, (a, w) in places.items()}
        self.h = sb("h", [P, TILES, D])
        self.dt = sb("dt", [P, TILES * NH])
        self.dt_a = sb("dt_a", [P, TILES * NH])
        self.top = sb("top", [P, TILES * 2])
        self.pick = sb("pick", [P, TILES * 2])
        self.w_out = sb("w_out", [P, 3, D])
        self.w_gate = sb("w_gate", [HD, 2, E1])
        self.w_fc = sb("w_fc", [HD, E1 * 2 * HID])
        self.w_qkv = sb("w_qkv", [HD, 2, 3 * D])
        self.wg = sb("wg", [HD, 2, E2])
        self.gate = sb("gate", [P, TILES, 2])
        self.slot1 = sb("slot1", [P, 2 * TILES], U32)
        self.expert1 = sb("expert1", [P, T1], I32)
        self.logits2 = sb("logits2", [P, TILES * E2])
        self.pick2 = sb("pick2", [P, TILES])
        self.score2 = sb("score2", [P, TILES])
        self.slot2 = sb("slot2", [P, TILES], U32)
        self.expert2 = sb("expert2", [P, T2], I32)
        self.zeros = sb("zeros", [P, D])
        self.rows = sb("rows", [P, TILES, D])
        self.loaded = ctx.enter_context(nc.semaphore("constants_loaded"))
        self.w_in_loaded = ctx.enter_context(nc.semaphore("w_in_loaded"))
        self.w_out_loaded = ctx.enter_context(nc.semaphore("w_out_loaded"))
        self.w_gate_loaded = ctx.enter_context(nc.semaphore("w_gate_loaded"))
        self.w_fc_loaded = ctx.enter_context(nc.semaphore("w_fc_loaded"))
        self.w_qkv_loaded = ctx.enter_context(nc.semaphore("w_qkv_loaded"))
        self.wg_loaded = ctx.enter_context(nc.semaphore("wg_loaded"))
        self.zeros_ready = ctx.enter_context(nc.semaphore("zeros_ready"))
        self.zeros_sent = ctx.enter_context(nc.semaphore("pad_rows_zeroed"))
        self.tables = ctx.enter_context(nc.semaphore("gelu_table_loaded"))


class ExpertMemory:

    def __init__(self, nc, ctx):
        def sb(name, shape):
            return ctx.enter_context(nc.sbuf_tensor(name, shape, F32))

        self.w_proj = sb("w_proj", [P, E1 * HC * D])
        self.w1 = sb("w1", [HD, E2 * 2 * HID])
        self.w2 = sb("w2", [P, E2 * HC * D])
        self.b1 = sb("b1", [1, E2 * HID])
        self.b2 = sb("b2", [1, E2 * D])
        self.w_proj_loaded = ctx.enter_context(nc.semaphore("w_proj_loaded"))
        self.second_loaded = ctx.enter_context(nc.semaphore("second_weights_loaded"))


class SsmMemory:

    def __init__(self, nc, ctx):
        def sb(name, shape):
            return ctx.enter_context(nc.sbuf_tensor(name, shape, F32))

        self.nc, self.semaphores = nc, []
        self.w_in = sb("w_in", [HD, 2, NIN])
        self.ut = sb("ut", [HD, 2, N_TOK])
        self.xbc = sb("xbc", [P, 5, N_TOK])
        self.sz = sb("sz", [P, 3, N_TOK])

    def semaphore(self, name):
        self.semaphores.append(self.nc.alloc_semaphore(name))
        return self.semaphores[-1]


def merge_frames(nc, dram, m, s, banks):
    with ExitStack() as ctx:
        def sb(name, shape, dt=F32):
            return ctx.enter_context(nc.sbuf_tensor(name, shape, dt))

        def sem(name):
            return s.semaphore(name)

        c, p = m.c, m.p
        x = sb("x_frames", [P, 2, 2, D])
        w_tok = sb("w_tok", [P, 3, 64])
        bq_sc = sb("bq_scaled", [P, 1])
        ones_row = c["ones"][0:1, 0:HD]
        qk = sb("qk", [HD, 2, 2, 2, P])
        s_m = sb("scores", [P, 2, P])
        mx = sb("row_max", [P, 2, 2])
        pr = sb("probs", [P, 2, P])
        rs = sb("row_sum", [P, 2, 2])
        pt = sb("probs_t", [P, 2, P])
        st = sb("bn_sums", [P, 2, 2, 6])
        mv = sb("bn_mean_var", [P, 2, 2, 2])
        ve = sb("var_eps", [P, 2, 2])
        rstd = sb("rstd", [P, 2, 2])
        a = sb("normed", [P, 2, D])
        u = sb("normed_twice", [P, 2, D])
        ut = sb("ut_tile", [HD, 2, 2, P])
        ps_qk = [banks[o][0:HD, :].rearrange("p (w c t) -> p w c t", w=2, c=2) for o in range(2)]
        ps_qv = banks[2][:, 0:2 * D].rearrange("p (w d) -> p w d", w=2)
        ps_s, ps_pt, ps_o = banks[3][:, 0:P], banks[4][:, 0:P], banks[5][:, 0:D]
        ps_u = banks[6][0:HD, 0:256].rearrange("p (c t) -> p c t", c=2)
        ps_dt = banks[7][:, 0:NH]

        x_in = [sem("x_in_even"), sem("x_in_odd")]
        w_ready, b_ready = sem("w_tok_ready"), sem("bq_scaled_ready")
        qk_mm, qv_mm, s_mm, pt_mm, o_mm, u_mm, dt_mm = (sem(n) for n in (
            "qk_product", "qv_product", "score_product", "probs_transposed", "attended", "u_transposed", "dt_product"))
        qk_ev, qn_ev, vn_ev = sem("qk_out"), sem("q_rows_out"), sem("v_rows_out")
        s_bar, s_max, n_max, p_exp, pt_ev = sem("scores_barred"), sem("scores_maxed"), sem("neg_max_ready"), sem("probs_ready"), sem("probs_t_out")
        r_inv, h_out, st1, mv1, ve1, rstd1 = (sem(n) for n in ("sum_inverted", "h_ready", "sums1", "mean_var1", "var_eps1", "rstd1"))
        a_out, st2, mv2, ve2, rstd2, ha = (sem(n) for n in ("a_ready", "sums2", "mean_var2", "var_eps2", "rstd2", "h_plus_a"))
        u_out, ut_ev, ut_copy, dt_out = sem("u_ready"), sem("ut_out"), sem("ut_copied"), sem("dt_out")

        x_rows = dram["x"].rearrange("(i h p) d -> i p h d", h=2, p=P)

        def row(t, i):
            return t[:, bass.ds(i, 1), :].rearrange("p a d -> p (a d)")

        with nc.Block() as block:
            @block.sync
            def _(sp):
                sp.dma_start(m.const[:, :], dram["const"]).then_inc(m.loaded, 16)
                sp.dma_start(m.param[:, :], dram["param"]).then_inc(m.loaded, 16)

                def load(t):
                    need(sp, qk_mm, t.i - 1)
                    need(sp, qv_mm, t.i - 1)
                    sp.dma_start(x[:, t.odd, :, :], x_rows[bass.ds(t.i, 1), :, :, :].rearrange("a p h d -> (a p) h d")).then_inc(x_in[t.odd], 16)

                pipelined(sp, TILES, {0: load}, 1)
                sp.dma_start(m.w_fc[:, :], dram["w_fc"]).then_inc(m.w_fc_loaded, 16)
                sp.dma_start(m.w_qkv[:, :, :], dram["w_qkv"].rearrange("(c p) n -> p c n", p=HD)).then_inc(m.w_qkv_loaded, 16)
                sp.dma_start(m.wg[:, :, :], dram["wg"].rearrange("(c p) e -> p c e", p=HD)).then_inc(m.wg_loaded, 16)
                sp.wait_ge(m.zeros_ready, 1)
                for name, tiles in (("x1", T1), ("x2", T2)):
                    sp.dma_start(dram[name].rearrange("(t p) d -> p t d", p=P), m.zeros[:, :].unsqueeze(1).to_broadcast([P, tiles, D])).then_inc(m.zeros_sent, 16)

            @block.tensor
            def _(pe):
                pe.wait_ge(m.loaded, 32)
                pe.wait_ge(w_ready, 1)

                def project(t):
                    pe.wait_ge(x_in[t.odd], 16 * (t.k + 1))
                    need(pe, qk_ev, t.i - 1)
                    for ch in range(2):
                        nc.tensor.matmul(ps_qk[t.odd][:, 0, ch, :], ones_row, p["bq_row"][0:1, :], start=True, stop=False)
                        for half in range(2):
                            nc.tensor.matmul(ps_qk[t.odd][:, 0, ch, half * 64:half * 64 + 64], x[:, t.odd, half, ch * HD:(ch + 1) * HD],
                                             w_tok[:, 0, :], start=False, stop=half == 1)
                    for ch in range(2):
                        for half in range(2):
                            last = nc.tensor.matmul(ps_qk[t.odd][:, 1, ch, half * 64:half * 64 + 64], x[:, t.odd, half, ch * HD:(ch + 1) * HD],
                                                    w_tok[:, 1, :], start=True, stop=True)
                    last.then_inc(qk_mm, 1)
                    need(pe, qn_ev, t.i)
                    need(pe, vn_ev, t.i)
                    for w, col in ((0, 0), (1, 2)):
                        for half in range(2):
                            last = nc.tensor.matmul(ps_qv[half * 64:half * 64 + 64, w, :], w_tok[:, col, :],
                                                    x[:, t.odd, half, :], start=True, stop=True)
                    last.then_inc(qv_mm, 1)

                def score(t):
                    pe.wait_ge(qk_ev, t.i + 1)
                    need(pe, s_bar, t.i)
                    for ch in range(2):
                        last = nc.tensor.matmul(ps_s, qk[:, t.odd, 0, ch, :], qk[:, t.odd, 1, ch, :], start=ch == 0, stop=ch == 1)
                    last.then_inc(s_mm, 1)

                def turn_probs(t):
                    pe.wait_ge(p_exp, t.i + 1)
                    need(pe, pt_ev, t.i)
                    nc.tensor.transpose(ps_pt, pr[:, t.odd, :], c["ident"]).then_inc(pt_mm, 1)

                def attend(t):
                    pe.wait_ge(pt_ev, t.i + 1)
                    pe.wait_ge(vn_ev, t.i + 1)
                    need(pe, h_out, t.i)
                    nc.tensor.matmul(ps_o, pt[:, t.odd, :], row(m.rows, t.i), start=True, stop=True).then_inc(o_mm, 1)

                def turn_u(t):
                    pe.wait_ge(u_out, t.i + 1)
                    need(pe, ut_ev, 2 * t.i)
                    for ch in range(2):
                        last = nc.tensor.transpose(ps_u[:, ch, :], u[:, t.odd, ch * HD:(ch + 1) * HD], c["ident"])
                    last.then_inc(u_mm, 1)

                def steps(t):
                    if isinstance(t.i, int) and t.i == 0:
                        pe.wait_ge(m.w_in_loaded, 16)
                    pe.wait_ge(ut_ev, 2 * (t.i + 1))
                    need(pe, dt_out, t.i)
                    for ch in range(2):
                        last = nc.tensor.matmul(ps_dt, ut[:, t.odd, ch, :], s.w_in[:, ch, NIN - NH:NIN], start=ch == 0, stop=ch == 1)
                    last.then_inc(dt_mm, 1)

                pipelined(pe, TILES, {0: project, 1: score, 2: turn_probs, 3: attend, 5: turn_u, 6: steps}, 7)

            @block.scalar
            def _(act):
                act.dma_start(s.w_in[:, :, :], dram["w_in"].rearrange("(c p) n -> p c n", p=HD)).then_inc(m.w_in_loaded, 16)
                act.dma_start(m.w_out[:, :, :], dram["w_out"].rearrange("(c p) n -> p c n", p=P)).then_inc(m.w_out_loaded, 16)
                act.dma_start(m.w_gate[:, :, :], dram["w_gate"].rearrange("(c p) e -> p c e", p=HD)).then_inc(m.w_gate_loaded, 16)
                act.wait_ge(m.loaded, 32)
                act.wait_ge(b_ready, 1)
                act.activation(rs[:, 0, 1:2], c["ones"][:, 0:1], ACT.Exp)

                def take_rows(t):
                    act.wait_ge(qv_mm, t.i + 1)
                    act.activation(row(m.h, t.i), ps_qv[:, 0, :], ACT.Identity, bias=bq_sc[:, 0:1], scale=SC).then_inc(qn_ev, 1)
                    act.activation(row(m.rows, t.i), ps_qv[:, 1, :], ACT.Identity, bias=p["bkv"]).then_inc(vn_ev, 1)

                def exponent(t):
                    act.wait_ge(n_max, t.i + 1)
                    need(act, pt_mm, t.i - 1)
                    act.activation(pr[:, t.odd, :], s_m[:, t.odd, :], ACT.Exp, bias=mx[:, t.odd, 1:2], scale=SC,
                                   accum_out=rs[:, t.odd, 0:1]).then_inc(p_exp, 1)

                def take_u(t):
                    act.wait_ge(u_mm, t.i + 1)
                    need(act, dt_mm, t.i - 1)
                    need(act, ut_copy, t.i - 1)
                    for ch in range(2):
                        act.activation(ut[:, t.odd, ch, :], ps_u[:, ch, :], ACT.Identity, bias=p["ln_b"][0:HD, ch:ch + 1],
                                       scale=p["ln_w"][0:HD, ch:ch + 1]).then_inc(ut_ev, 1)

                pipelined(act, TILES, {0: take_rows, 1: exponent, 5: take_u}, 7)

            @block.vector
            def _(dve):
                dve.wait_ge(m.loaded, 32)
                for w, name in enumerate(("wq", "wk", "wv")):
                    last = nc.vector.tensor_tensor(w_tok[:, w, :], p[name], c["frame_sel"][:, w * 64:(w + 1) * 64], ALU.mult)
                last.then_inc(w_ready, 1)
                nc.vector.tensor_scalar(bq_sc[:, :], p["bq"], SC, None, ALU.mult).then_inc(b_ready, 1)

                def take_qk(t):
                    dve.wait_ge(qk_mm, t.i + 1)
                    need(dve, s_mm, t.i - 1)
                    nc.vector.tensor_copy(qk[:, t.odd, :, :, :], ps_qk[t.odd]).then_inc(qk_ev, 1)

                def maxima(t):
                    dve.wait_ge(s_mm, t.i + 1)
                    need(dve, p_exp, t.i - 1)
                    nc.vector.tensor_tensor(s_m[:, t.odd, :], ps_s, c["group_bar"], ALU.add).then_inc(s_bar, 1)
                    dve.wait_ge(s_bar, t.i + 1)
                    nc.vector.reduce_max(mx[:, t.odd, 0:1], s_m[:, t.odd, :], AX_X).then_inc(s_max, 1)
                    dve.wait_ge(s_max, t.i + 1)
                    nc.vector.tensor_scalar(mx[:, t.odd, 1:2], mx[:, t.odd, 0:1], -SC, None, ALU.mult).then_inc(n_max, 1)

                def take_probs(t):
                    dve.wait_ge(pt_mm, t.i + 1)
                    need(dve, o_mm, t.i - 1)
                    nc.vector.tensor_copy(pt[:, t.odd, :], ps_pt).then_inc(pt_ev, 1)
                    nc.vector.reciprocal(rs[:, t.odd, 1:2], rs[:, t.odd, 0:1]).then_inc(r_inv, 1)

                def merge(t):
                    dve.wait_ge(o_mm, t.i + 1)
                    dve.wait_ge(r_inv, t.i + 1)
                    dve.wait_ge(qn_ev, t.i + 1)
                    nc.vector.scalar_tensor_tensor(row(m.h, t.i), ps_o, rs[:, t.odd, 1:2], row(m.h, t.i), ALU.mult, ALU.add).then_inc(h_out, 1)
                    need_alone(dve, m, (h_out, t.i + 1))
                    nc.vector.bn_stats(st[:, t.odd, 0, :], row(m.h, t.i)).then_inc(st1, 1)
                    need_alone(dve, m, (st1, t.i + 1))
                    need(dve, a_out, t.i - 1)
                    nc.vector.bn_aggr(mv[:, t.odd, 0, :], st[:, t.odd, 0, :]).then_inc(mv1, 1)

                def norm_once(t):
                    dve.wait_ge(rstd1, t.i + 1)
                    need(dve, ha, t.i - 1)
                    need(dve, u_out, t.i - 1)
                    nc.vector.tensor_scalar(a[:, t.odd, :], row(m.h, t.i), mv[:, t.odd, 0, 0:1], rstd[:, t.odd, 0:1], ALU.subtract, ALU.mult).then_inc(a_out, 1)
                    need_alone(dve, m, (a_out, t.i + 1))
                    nc.vector.bn_stats(st[:, t.odd, 1, :], a[:, t.odd, :]).then_inc(st2, 1)
                    need_alone(dve, m, (st2, t.i + 1))
                    nc.vector.bn_aggr(mv[:, t.odd, 1, :], st[:, t.odd, 1, :]).then_inc(mv2, 1)

                def norm_twice(t):
                    dve.wait_ge(rstd2, t.i + 1)
                    need(dve, u_mm, t.i - 1)
                    nc.vector.tensor_scalar(u[:, t.odd, :], a[:, t.odd, :], mv[:, t.odd, 1, 0:1], rstd[:, t.odd, 1:2], ALU.subtract, ALU.mult).then_inc(u_out, 1)

                def take_dt(t):
                    dve.wait_ge(dt_mm, t.i + 1)
                    nc.vector.tensor_tensor(m.dt[:, bass.ds(t.i * NH, NH)], ps_dt, p["dt_bias"], ALU.add).then_inc(dt_out, 1)

                pipelined(dve, TILES, {0: take_qk, 1: maxima, 2: take_probs, 3: merge, 4: norm_once, 5: norm_twice, 6: take_dt}, 7)

            @block.gpsimd
            def _(pool):
                nc.gpsimd.memset(m.zeros[:, :], 0.0).then_inc(m.zeros_ready, 1)
                pool.wait_ge(m.loaded, 32)

                def inverse_root(t, n, known, eps_done, done):
                    pool.wait_ge(known, t.i + 1)
                    nc.gpsimd.tensor_tensor(ve[:, t.odd, n:n + 1], mv[:, t.odd, n, 1:2], c["eps"], ALU.add).then_inc(eps_done, 1)
                    pool.wait_ge(eps_done, t.i + 1)
                    nc.gpsimd.tensor_tensor(rstd[:, t.odd, n:n + 1], ve[:, t.odd, n:n + 1], c["minus_half"], ALU.pow).then_inc(done, 1)

                def roots(t):
                    inverse_root(t, 0, mv1, ve1, rstd1)

                def roots_and_residual(t):
                    inverse_root(t, 1, mv2, ve2, rstd2)
                    nc.gpsimd.tensor_tensor(row(m.h, t.i), row(m.h, t.i), a[:, t.odd, :], ALU.add).then_inc(ha, 1)

                def keep_u(t):
                    pool.wait_ge(ut_ev, 2 * (t.i + 1))
                    nc.gpsimd.tensor_copy(s.ut[:, :, bass.ds(t.i * P, P)], ut[:, t.odd, :, :]).then_inc(ut_copy, 1)

                pipelined(pool, TILES, {3: roots, 4: roots_and_residual, 5: keep_u}, 7)


def project_in(nc, dram, m, s, banks):
    with ExitStack() as ctx:
        def sb(name, shape, dt=F32):
            return ctx.enter_context(nc.sbuf_tensor(name, shape, dt))

        def sem(name):
            return s.semaphore(name)

        p = m.p
        n_dt = TILES * NH
        mag, ex, one_ex, ln1, back = (sb(n, [P, n_dt]) for n in ("dt_mag", "dt_exp", "dt_one_exp", "dt_log", "dt_back"))
        e_a = sb("exp_A", [P, NH])
        pre = sb("conv_out", [P, 5, SB])
        mag_done, exp_done, one_done, log_done, back1, back2, back3, sp_done, ea_done, a_done = (sem(n) for n in (
            "dt_mag_ready", "dt_exp_ready", "dt_one_exp_ready", "dt_log_ready", "dt_rounded", "dt_lost_ready",
            "dt_log_mended", "dt_softplus_ready", "exp_A_ready", "dt_A_ready"))
        proj, gate_out, tap3, taps, conv_silu = (sem(n) for n in ("projected", "gate_ready", "last_tap_done", "taps_done", "conv_ready"))

        chunks = [("conv", c, 3 + c) for c in range(5)] + [("gate", c, c) for c in range(3)]

        with nc.Block() as block:
            @block.tensor
            def _(pe):
                def superblock(j):
                    for n, (kind, c, ch) in enumerate(chunks):
                        if kind == "conv":
                            after_first(pe, taps, j, 3 * (5 * (j - 1) + c + 1))
                        else:
                            after_first(pe, gate_out, j, 3 * (j - 1) + c + 1)
                        for half in range(2):
                            last = nc.tensor.matmul(banks[n][:, :], s.w_in[:, half, ch * P:(ch + 1) * P], s.ut[:, half, bass.ds(j * SB, SB)],
                                                    start=half == 0, stop=half == 1)
                        last.then_inc(proj, 1)

                superblock(0)
                with pe.Fori(1, N_TOK // SB) as j:
                    superblock(j)

            @block.scalar
            def _(act):
                act.activation(e_a[:, :], p["A_log"], ACT.Exp).then_inc(ea_done, 1)
                act.wait_ge(mag_done, 1)
                act.activation(ex[:, :], mag[:, :], ACT.Exp, scale=-1.0).then_inc(exp_done, 1)
                act.wait_ge(one_done, 1)
                act.activation(ln1[:, :], one_ex[:, :], ACT.Ln).then_inc(log_done, 1)
                act.wait_ge(ea_done, 1)
                act.wait_ge(a_done, 1)
                act.activation(e_a[:, :], p["A_log"], ACT.Silu).then_inc(ea_done, 1)

                def first_tap(j, c):
                    act.wait_ge(proj, 8 * j + c + 1)
                    after_first(act, conv_silu, j, 5 * (j - 1) + c + 1)
                    act.activation(pre[:, c, :], banks[c][:, :], ACT.Identity, bias=p["conv_b"][:, c:c + 1],
                                   scale=p["conv_w"][:, 4 * c + 3:4 * c + 4]).then_inc(tap3, 1)

                def silu(j, c):
                    act.wait_ge(taps, 3 * (5 * j + c + 1))
                    act.activation(s.xbc[:, c, bass.ds(j * SB, SB)], pre[:, c, :], ACT.Silu).then_inc(conv_silu, 1)

                def gate(j, c):
                    act.wait_ge(proj, 8 * j + 5 + c + 1)
                    act.activation(s.sz[:, c, bass.ds(j * SB, SB)], banks[5 + c][:, :], ACT.Silu).then_inc(gate_out, 1)

                def superblock(j):
                    first_tap(j, 0)
                    for c in range(1, 5):
                        first_tap(j, c)
                        silu(j, c - 1)
                    gate(j, 0)
                    silu(j, 4)
                    gate(j, 1)
                    gate(j, 2)

                superblock(0)
                with act.Fori(1, N_TOK // SB) as j:
                    superblock(j)

            @block.vector
            def _(dve):
                nc.vector.scalar_tensor_tensor(mag[:, :], m.dt[:, :], -1.0, m.dt[:, :], ALU.mult, ALU.max).then_inc(mag_done, 1)
                dve.wait_ge(exp_done, 1)
                nc.vector.tensor_scalar(one_ex[:, :], ex[:, :], 1.0, None, ALU.add).then_inc(one_done, 1)
                dve.wait_ge(one_done, 1)
                nc.vector.tensor_scalar(back[:, :], one_ex[:, :], -1.0, None, ALU.add).then_inc(back1, 1)
                dve.wait_ge(back1, 1)
                nc.vector.tensor_tensor(mag[:, :], ex[:, :], back[:, :], ALU.subtract).then_inc(back2, 1)
                dve.wait_ge(back2, 1)
                dve.wait_ge(log_done, 1)
                nc.vector.tensor_tensor(one_ex[:, :], ln1[:, :], mag[:, :], ALU.add).then_inc(back3, 1)
                dve.wait_ge(back3, 1)
                nc.vector.scalar_tensor_tensor(m.dt[:, :], m.dt[:, :], 0.0, one_ex[:, :], ALU.max, ALU.add).then_inc(sp_done, 1)
                dve.wait_ge(sp_done, 1)
                dve.wait_ge(ea_done, 1)
                nc.vector.scalar_tensor_tensor(m.dt_a[:, :].rearrange("p (i h) -> p i h", h=NH), m.dt[:, :].rearrange("p (i h) -> p i h", h=NH), -1.0,
                                               e_a[:, :].unsqueeze(1).to_broadcast([P, TILES, NH]), ALU.mult, ALU.mult).then_inc(a_done, 1)

                def superblock(j):
                    for c in range(5):
                        full = pre[:, c, :].rearrange("p (b t) -> p b t", t=BLK)
                        src = banks[c][:, :].rearrange("p (b t) -> p b t", t=BLK)
                        for back_by in range(1, KC):
                            if back_by == 1:
                                dve.wait_ge(tap3, 5 * j + c + 1)
                            else:
                                dve.wait_ge(taps, 3 * (5 * j + c) + back_by - 1)
                            nc.vector.scalar_tensor_tensor(full[:, :, back_by:], src[:, :, :BLK - back_by], p["conv_w"][:, 4 * c + 3 - back_by:4 * c + 4 - back_by],
                                                           full[:, :, back_by:], ALU.mult, ALU.add).then_inc(taps, 1)

                superblock(0)
                with dve.Fori(1, N_TOK // SB) as j:
                    superblock(j)


def state_space(nc, dram, m, s, ps):
    with ExitStack() as ctx:
        def sb(name, shape, dt=F32):
            return ctx.enter_context(nc.sbuf_tensor(name, shape, dt))

        def sem(name):
            return s.semaphore(name)

        c, p = m.c, m.p
        xb = sb("xbc_tile", [P, 2, 5, P])
        a_upto = sb("dt_a_upto", [P, 2, NH, BLK])
        ex = sb("decays", [P, 2, NH, BLK])
        gm = sb("bc_masked", [P, 2, BLK])
        mix = sb("mix", [P, 2, NH, BLK])
        xt = sb("x_dt", [P, 2, DI])
        y = sb("y", [P, 2, 3, P])
        yg = sb("y_gated", [P, 2, 3, P])
        sq = sb("y_squares", [P, 2, 3, P])
        col = sb("columns", [P, 2, 8])
        st = sb("bn_sums2", [P, 2, 6])
        mv = sb("bn_mean_var2", [P, 2, 2])
        xf = sb("xf_tile", [P, 2, D])
        xft = sb("xf_turned", [HD, 2, 2, P])
        lg = sb("logits", [P, 2, E1])
        top = sb("top8", [P, 2, 8])
        ix = sb("top8_index", [P, 2, 8], U32)
        ps_d = ps[:, 0, 0:NH * BLK]
        ps_g = ps[:, 1, 0:BLK]
        ps_x = ps[:, 1, P:P + DI]
        ps_o = ps[:, 6, 0:D]
        ps_q = ps[:, 6, D:D + 1]
        ps_u = ps[0:HD, 7, 0:256].rearrange("p (c t) -> p c t", c=2)
        ps_l = ps[:, 7, 256:256 + E1]

        xb_in = [sem("xbc_in_even"), sem("xbc_in_odd")]
        (wo_ready, upto_done, d_mm, gx_mm, exp_done, g_done, x_done, mix_done, y_mm, skip_done, gate_done, sq_done, q_mm, ms_done, rms_done,
         h_done, sums, mean_var, eps_done, rstd_done, xf_done, u_mm, u_out, l_mm, l_out, top_done, ix_done, kept, picked, row_kept) = (sem(n) for n in (
            "w_out_scaled", "dt_a_spread", "decay_sums", "bc_and_x_turned", "decays_ready", "bc_masked_ready", "x_dt_ready", "mix_ready", "y_product",
            "skip_added", "y_gated_ready", "squares_ready", "out_product", "mean_square_ready", "rms_ready", "h2_ready", "sums3", "mean_var3", "var_eps3",
            "rstd3", "xf_ready", "xf_turned_mm", "xf_turned_out", "logit_product", "logits_out", "top_ready", "index_ready", "top_kept", "index_kept", "xf_kept"))

        def row(t, i):
            return t[:, bass.ds(i, 1), :].rearrange("p a d -> p (a d)")

        with nc.Block() as block:
            @block.sync
            def _(sp):
                def copy_tile(t):
                    need(sp, skip_done, 3 * (t.i - 1))
                    need(sp, gx_mm, t.i - 1)
                    sp.dma_start(xb[:, t.odd, :, :], s.xbc[:, :, bass.ds(t.i * P, P)]).then_inc(xb_in[t.odd], 16)

                pipelined(sp, TILES, {0: copy_tile}, 7)

            @block.tensor
            def _(pe):
                pe.wait_ge(wo_ready, 3)
                pe.wait_ge(m.w_gate_loaded, 16)

                def decay_and_bc(t):
                    pe.wait_ge(upto_done, t.i + 1)
                    need(pe, exp_done, t.i)
                    nc.tensor.matmul(ps_d, c["after"], a_upto[:, t.odd, :, :].rearrange("p h t -> p (h t)"), start=True, stop=True).then_inc(d_mm, 1)
                    pe.wait_ge(xb_in[t.odd], 16 * (t.k + 1))
                    need(pe, g_done, t.i)
                    need(pe, x_done, t.i)
                    for b in range(4):
                        seq = slice(b * BLK, (b + 1) * BLK)
                        nc.tensor.matmul(ps_g[seq, :], xb[:, t.odd, 3, seq], xb[:, t.odd, 4, seq], start=True, stop=True)
                    for ch in range(3):
                        last = nc.tensor.transpose(ps_x[:, ch * P:(ch + 1) * P], xb[:, t.odd, ch, :], c["ident"])
                    last.then_inc(gx_mm, 1)

                def mix_time(t):
                    pe.wait_ge(mix_done, t.i + 1)
                    pe.wait_ge(x_done, t.i + 1)
                    need(pe, skip_done, 3 * t.i)
                    for h in range(NH):
                        for b in range(4):
                            seq = slice(b * BLK, (b + 1) * BLK)
                            half = slice((h % 2) * HP, (h % 2 + 1) * HP)
                            last = nc.tensor.matmul(ps[half, 2 + b, (h // 2) * BLK:(h // 2 + 1) * BLK], xt[seq, t.odd, h * HP:(h + 1) * HP],
                                                    mix[seq, t.odd, h, :], start=True, stop=True)
                    last.then_inc(y_mm, 1)

                def project_out(t):
                    pe.wait_ge(sq_done, t.i + 1)
                    need(pe, h_done, t.i)
                    for ch in range(3):
                        nc.tensor.matmul(ps_q, sq[:, t.odd, ch, :], c["ones"][:, 0:1], start=ch == 0, stop=ch == 2)
                    for ch in range(3):
                        last = nc.tensor.matmul(ps_o, yg[:, t.odd, ch, :], m.w_out[:, ch, :], start=ch == 0, stop=ch == 2)
                    last.then_inc(q_mm, 1)

                def turn(t):
                    pe.wait_ge(xf_done, t.i + 1)
                    need(pe, l_out, t.i)
                    for ch in range(2):
                        last = nc.tensor.transpose(ps_u[:, ch, :], xf[:, t.odd, ch * HD:(ch + 1) * HD], c["ident"])
                    last.then_inc(u_mm, 1)

                def route(t):
                    pe.wait_ge(u_out, t.i + 1)
                    for ch in range(2):
                        last = nc.tensor.matmul(ps_l, xft[:, t.odd, ch, :], m.w_gate[:, ch, :], start=ch == 0, stop=ch == 1)
                    last.then_inc(l_mm, 1)

                pipelined(pe, TILES, {1: decay_and_bc, 2: mix_time, 3: project_out, 5: turn, 6: route}, 7)

            @block.scalar
            def _(act):
                act.activation(col[:, 0, 7:8], c["ones"][:, 0:1], ACT.Exp)

                def decays(t):
                    act.wait_ge(d_mm, t.i + 1)
                    need(act, mix_done, t.i - 1)
                    act.activation(ex[:, t.odd, :, :].rearrange("p h t -> p (h t)"), ps_d, ACT.Exp).then_inc(exp_done, 1)

                def squares(t):
                    act.wait_ge(gate_done, t.i + 1)
                    need(act, q_mm, t.i - 1)
                    act.activation(sq[:, t.odd, :, :], yg[:, t.odd, :, :], ACT.Square).then_inc(sq_done, 1)

                def take_turned(t):
                    act.wait_ge(u_mm, t.i + 1)
                    need(act, l_mm, t.i - 1)
                    act.activation(xft[:, t.odd, :, :], ps_u, ACT.Identity).then_inc(u_out, 1)

                pipelined(act, TILES, {1: decays, 2: squares, 5: take_turned}, 7)

            @block.vector
            def _(dve):
                dve.wait_ge(m.w_out_loaded, 16)
                for ch in range(3):
                    nc.vector.tensor_scalar(m.w_out[:, ch, :], m.w_out[:, ch, :], p["norm_w"][:, ch:ch + 1], None, ALU.mult).then_inc(wo_ready, 1)

                def mixing(t):
                    dve.wait_ge(gx_mm, t.i + 1)
                    nc.vector.tensor_tensor(gm[:, t.odd, :], ps_g, c["upto"], ALU.mult).then_inc(g_done, 1)
                    need(dve, y_mm, t.i - 1)
                    nc.vector.tensor_tensor(xt[:, t.odd, :].rearrange("p (h c) -> p h c", h=NH), ps_x.rearrange("p (h c) -> p h c", h=NH),
                                            m.dt[:, bass.ds(t.i * NH, NH)].unsqueeze(2).to_broadcast([P, NH, HP]), ALU.mult).then_inc(x_done, 1)
                    dve.wait_ge(exp_done, t.i + 1)
                    dve.wait_ge(g_done, t.i + 1)
                    nc.vector.tensor_tensor(mix[:, t.odd, :, :], ex[:, t.odd, :, :], gm[:, t.odd, :].unsqueeze(1).to_broadcast([P, NH, BLK]), ALU.mult).then_inc(mix_done, 1)

                def skip_and_gate(t):
                    dve.wait_ge(y_mm, t.i + 1)
                    need(dve, gate_done, t.i - 1)
                    for ch in range(3):
                        nc.vector.scalar_tensor_tensor(y[:, t.odd, ch, :].rearrange("p (b t) -> p b t", b=4), xb[:, t.odd, ch, :].rearrange("p (b t) -> p b t", b=4),
                                                       p["skip"][:, ch:ch + 1], ps[:, 2:6, ch * BLK:(ch + 1) * BLK], ALU.mult, ALU.add).then_inc(skip_done, 1)
                    dve.wait_ge(skip_done, 3 * (t.i + 1))
                    need(dve, q_mm, t.i - 1)
                    nc.vector.tensor_tensor(yg[:, t.odd, :, :], y[:, t.odd, :, :], s.sz[:, :, bass.ds(t.i * P, P)], ALU.mult).then_inc(gate_done, 1)

                def mean_square(t):
                    dve.wait_ge(q_mm, t.i + 1)
                    need(dve, rms_done, t.i - 1)
                    nc.vector.tensor_scalar(col[:, t.odd, 0:1], ps_q, 1.0 / DI, EPS, ALU.mult, ALU.add).then_inc(ms_done, 1)

                def residual(t):
                    dve.wait_ge(rms_done, t.i + 1)
                    need(dve, xf_done, t.i - 1)
                    nc.vector.scalar_tensor_tensor(row(m.h, t.i), ps_o, col[:, t.odd, 1:2], row(m.h, t.i), ALU.mult, ALU.add).then_inc(h_done, 1)
                    need_alone(dve, m, (h_done, t.i + 1))
                    nc.vector.bn_stats(st[:, t.odd, :], row(m.h, t.i)).then_inc(sums, 1)
                    need_alone(dve, m, (sums, t.i + 1))
                    nc.vector.bn_aggr(mv[:, t.odd, :], st[:, t.odd, :]).then_inc(mean_var, 1)

                def norm(t):
                    dve.wait_ge(rstd_done, t.i + 1)
                    need(dve, u_mm, t.i - 1)
                    need(dve, row_kept, t.i - 1)
                    nc.vector.tensor_scalar(xf[:, t.odd, :], row(m.h, t.i), mv[:, t.odd, 0:1], col[:, t.odd, 3:4], ALU.subtract, ALU.mult).then_inc(xf_done, 1)

                def best_two(t):
                    dve.wait_ge(l_mm, t.i + 1)
                    need(dve, ix_done, t.i - 1)
                    need(dve, kept, t.i - 1)
                    need(dve, picked, t.i - 1)
                    nc.vector.tensor_copy(lg[:, t.odd, :], ps_l).then_inc(l_out, 1)
                    need_alone(dve, m, (l_out, t.i + 1))
                    nc.vector.max(top[:, t.odd, :], lg[:, t.odd, :]).then_inc(top_done, 1)
                    need_alone(dve, m, (top_done, t.i + 1))
                    nc.vector.max_index(ix[:, t.odd, :], top[:, t.odd, :], lg[:, t.odd, :]).then_inc(ix_done, 1)
                    nc.vector.tensor_copy(m.top[:, bass.ds(t.i * 2, 2)], top[:, t.odd, 0:2]).then_inc(kept, 1)
                    dve.wait_ge(ix_done, t.i + 1)
                    nc.vector.tensor_copy(m.pick[:, bass.ds(t.i * 2, 2)], ix[:, t.odd, 0:2]).then_inc(picked, 1)

                pipelined(dve, TILES, {1: mixing, 2: skip_and_gate, 3: mean_square, 4: residual, 5: norm, 6: best_two}, 7)

            @block.gpsimd
            def _(pool):
                def spread(t):
                    need(pool, d_mm, t.i - 1)
                    nc.gpsimd.tensor_tensor(a_upto[:, t.odd, :, :], c["upto"].unsqueeze(1).to_broadcast([P, NH, BLK]),
                                            m.dt_a[:, bass.ds(t.i * NH, NH)].unsqueeze(2).to_broadcast([P, NH, BLK]), ALU.mult).then_inc(upto_done, 1)

                def root_of_mean_square(t):
                    pool.wait_ge(ms_done, t.i + 1)
                    need(pool, h_done, t.i - 1)
                    nc.gpsimd.tensor_tensor(col[:, t.odd, 1:2], col[:, t.odd, 0:1], c["minus_half"], ALU.pow).then_inc(rms_done, 1)

                def root_of_variance(t):
                    pool.wait_ge(mean_var, t.i + 1)
                    need(pool, xf_done, t.i - 1)
                    nc.gpsimd.tensor_tensor(col[:, t.odd, 2:3], mv[:, t.odd, 1:2], c["eps"], ALU.add).then_inc(eps_done, 1)
                    pool.wait_ge(eps_done, t.i + 1)
                    nc.gpsimd.tensor_tensor(col[:, t.odd, 3:4], col[:, t.odd, 2:3], c["minus_half"], ALU.pow).then_inc(rstd_done, 1)

                def keep(t):
                    pool.wait_ge(xf_done, t.i + 1)
                    nc.gpsimd.tensor_copy(row(m.rows, t.i), xf[:, t.odd, :]).then_inc(row_kept, 1)

                pipelined(pool, TILES, {0: spread, 3: root_of_mean_square, 4: root_of_variance, 5: keep}, 7)


def dispatch(nc, m, banks, tag, n_exp, cols, pick, slot, tile_expert, n_tiles, logits_to_gates):
    with ExitStack() as ctx:
        def sb(name, shape, dt=F32):
            return ctx.enter_context(nc.sbuf_tensor(f"{name}_{tag}", shape, dt))

        def sem(name):
            return ctx.enter_context(nc.semaphore(f"{name}_{tag}"))

        c = m.c
        n = n_exp * cols
        one_hot = sb("one_hot", [P, n_exp, cols])
        counts = sb("counts", [P, n_exp, cols + 1])
        run = sb("running", [P, n_exp, cols + 1])
        ones = sb("scan_ones", [P, n_exp * (cols + 1)])
        total = sb("totals", [P, 4, n_exp])
        total_i = sb("totals_int", [P, 2, n_exp], I32)
        place = sb("places", [P, n_exp, cols])
        slot_f = sb("slots", [P, cols])
        ended = sb("ended", [P, n_tiles, n_exp])
        expert_f = sb("tile_experts", [P, n_tiles])
        picked, counted, step, gate_exp = sem("picked"), sem("counted"), sem("dispatch_step"), sem("gate_exp")
        flat = "p e a -> p (e a)"
        ps_before, ps_count = banks[0][:, 0:n], banks[1][:, 0:n]

        with nc.Block() as block:
            @block.tensor
            def _(pe):
                pe.wait_ge(picked, 1)
                nc.tensor.matmul(ps_before, c["before"], one_hot[:, :, :].rearrange(flat), start=True, stop=True)
                nc.tensor.matmul(ps_count, c["ones"], one_hot[:, :, :].rearrange(flat), start=True, stop=True).then_inc(counted, 1)

            @block.scalar
            def _(act):
                if logits_to_gates:
                    act.wait_ge(step, 1)
                    act.activation(m.gate[:, :, 1], m.gate[:, :, 1], ACT.Exp).then_inc(gate_exp, 1)

            @block.vector
            def _(dve):
                done = [0]

                def then(ins):
                    done[0] += 1
                    ins.then_inc(step, 1)
                    dve.wait_ge(step, done[0])

                if logits_to_gates:
                    top = m.top[:, :].rearrange("p (i k) -> p i k", k=2)
                    then(nc.vector.tensor_tensor(m.gate[:, :, 1], top[:, :, 1], top[:, :, 0], ALU.subtract))
                nc.vector.tensor_tensor(one_hot[:, :, :], pick.unsqueeze(1).to_broadcast([P, n_exp, cols]),
                                        c["iota"][:, 0:n_exp].unsqueeze(2).to_broadcast([P, n_exp, cols]), ALU.is_equal).then_inc(picked, 1)
                then(nc.vector.memset(ones[:, :], 1.0))
                dve.wait_ge(counted, 1)
                then(nc.vector.tensor_copy(counts[:, :, 0:cols], ps_count.rearrange("p (e a) -> p e a", e=n_exp)))
                then(nc.vector.reduce_sum(total[:, 0, :], counts[:, :, 0:cols], AX_X))
                then(nc.vector.tensor_scalar(total_i[:, 0, :], total[:, 0, :], float(P - 1), None, ALU.add))
                then(nc.vector.tensor_scalar(total_i[:, 1, :], total_i[:, 0, :], 7, None, ALU.logical_shift_right))
                then(nc.vector.tensor_copy(total[:, 1, :], total_i[:, 1, :]))
                then(nc.vector.scalar_tensor_tensor(counts[:, :, cols], total[:, 1, :], float(P), total[:, 0, :], ALU.mult, ALU.subtract))
                then(nc.vector.tensor_tensor_scan(run[:, :, :].rearrange(flat), ones[:, :], counts[:, :, :].rearrange(flat), 0.0, ALU.mult, ALU.add))
                then(nc.vector.tensor_tensor(place[:, :, :], run[:, :, 0:cols], counts[:, :, 0:cols], ALU.subtract))
                then(nc.vector.tensor_tensor(place[:, :, :], place[:, :, :], ps_before.rearrange("p (e a) -> p e a", e=n_exp), ALU.add))
                then(nc.vector.tensor_tensor(place[:, :, :], place[:, :, :], one_hot[:, :, :], ALU.mult))
                then(nc.vector.reduce_sum(slot_f[:, :], place[:, :, :].rearrange("p e a -> p a e"), AX_X))
                then(nc.vector.tensor_copy(slot[:, :], slot_f[:, :]))
                then(nc.vector.tensor_scalar(total[:, 2, :], run[:, :, cols], 1.0 / P, None, ALU.mult))
                then(nc.vector.tensor_tensor(ended[:, :, :], c["iota"][:, 0:n_tiles].unsqueeze(2).to_broadcast([P, n_tiles, n_exp]),
                                             total[:, 2, :].unsqueeze(1).to_broadcast([P, n_tiles, n_exp]), ALU.is_ge))
                then(nc.vector.reduce_sum(expert_f[:, :], ended[:, :, :], AX_X))
                then(nc.vector.tensor_scalar(expert_f[:, :], expert_f[:, :], float(n_exp - 1), None, ALU.min))
                then(nc.vector.tensor_copy(tile_expert[:, :], expert_f[:, :]))
                if logits_to_gates:
                    dve.wait_ge(gate_exp, 1)
                    then(nc.vector.tensor_scalar(m.gate[:, :, 0], m.gate[:, :, 1], 1.0, None, ALU.add))
                    then(nc.vector.reciprocal(m.gate[:, :, 0], m.gate[:, :, 0]))
                    then(nc.vector.tensor_tensor(m.gate[:, :, 1], m.gate[:, :, 1], m.gate[:, :, 0], ALU.mult))


def scatter_rows(nc, m, tag, picks, slot, dst, before):
    with ExitStack() as ctx:
        rows = ctx.enter_context(nc.sbuf_tensor(f"scatter_rows_{tag}", [P, 2, D], F32))
        index = ctx.enter_context(nc.sbuf_tensor(f"scatter_index_{tag}", [P, 2, picks], U32))
        ready = ctx.enter_context(nc.semaphore(f"scatter_ready_{tag}"))
        sent = [ctx.enter_context(nc.semaphore(f"scattered_{n}_{tag}")) for n in range(2)]
        with nc.Block() as block:
            @block.vector
            def _(dve):
                def stage(t):
                    need(dve, sent[t.odd], 16 * picks * t.k)
                    nc.vector.tensor_copy(rows[:, t.odd, :], m.rows[:, bass.ds(t.i, 1), :].rearrange("p a d -> p (a d)")).then_inc(ready, 1)
                    nc.vector.tensor_copy(index[:, t.odd, :], slot[:, bass.ds(t.i * picks, picks)]).then_inc(ready, 1)

                pipelined(dve, TILES, {0: stage}, 2)

            @block.gpsimd
            def _(pool):
                for sem, value in before:
                    pool.wait_ge(sem, value)

                def send(t):
                    pool.wait_ge(ready, 2 * (t.i + 1))
                    for k in range(picks):
                        nc.gpsimd.indirect_dma_start(out=dst, out_offset=bass.IndirectOffsetOnAxis(ap=index[:, t.odd, k:k + 1], axis=0),
                                                     in_=rows[:, t.odd, :], in_offset=None).then_inc(sent[t.odd], 16)

                pipelined(pool, TILES, {1: send}, 2, straight=True)
                for o in range(2):
                    pool.wait_ge(sent[o], 16 * picks * TILES // 2)


def experts(nc, m, ps, tag, n_exp, n_tiles, tile_expert, src, dst, w_up, w_down, b_up, b_down, gelu, weights_in):
    with ExitStack() as ctx:
        def sb(name, shape, dt=F32):
            return ctx.enter_context(nc.sbuf_tensor(f"{name}_{tag}", shape, dt))

        def sem(name):
            return ctx.enter_context(nc.semaphore(f"{name}_{tag}"))

        c = m.c
        x = sb("rows_in", [P, 2, D])
        xt = sb("rows_turned", [HD, 2, 2, P])
        hid = sb("hidden", [P, 2, 2, HID // 2])
        ht = sb("hidden_turned", [P, 2, HC, P])
        y = sb("rows_out", [P, 2, D])
        x_in = [sem("rows_in_even"), sem("rows_in_odd")]
        y_sent = [sem("rows_sent_even"), sem("rows_sent_odd")]
        x_mm, x_out, up_mm, act_done, t_mm, t_out, down_mm, y_out = (sem(n) for n in (
            "rows_turned_mm", "rows_turned_out", "up_product", "gelu_ready", "hidden_turned_mm", "hidden_turned_out", "down_product", "rows_ready"))
        ps_x = ps[0:HD, 0, 0:256].rearrange("p (c t) -> p c t", c=2)
        ps_h = [ps[:, 1:3, 0:HID // 2], ps[:, 6:8, 0:HID // 2]]
        ps_t = [ps[:, 3, :], ps[:, 4, 0:256]]
        ps_y = ps[:, 5, 0:D]

        def rows(t, i):
            return t[bass.ds(i * P, P), :]

        with nc.Block() as block:
            @block.sync
            def _(sp):
                def load(t):
                    need(sp, x_mm, t.i - 1)
                    sp.dma_start(x[:, t.odd, :], rows(src, t.i)).then_inc(x_in[t.odd], 16)

                def store(t):
                    sp.wait_ge(y_out, t.i + 1)
                    sp.dma_start(rows(dst, t.i), y[:, t.odd, :]).then_inc(y_sent[t.odd], 16)

                pipelined(sp, n_tiles, {0: load, 4: store}, 5)
                sp.wait_ge(y_sent[0], 16 * ((n_tiles + 1) // 2))
                sp.wait_ge(y_sent[1], 16 * (n_tiles // 2))

            @block.tensor
            def _(pe):
                for s, value in weights_in:
                    pe.wait_ge(s, value)

                def turn_rows(t):
                    pe.wait_ge(x_in[t.odd], 16 * (t.k + 1))
                    need(pe, x_out, t.i)
                    for ch in range(2):
                        last = nc.tensor.transpose(ps_x[:, ch, :], x[:, t.odd, ch * HD:(ch + 1) * HD], c["ident"])
                    last.then_inc(x_mm, 1)

                def expert_of(t):
                    return pe.value_load(tile_expert[0:1, bass.ds(t.i, 1)], min_val=0, max_val=n_exp - 1)

                def up(t):
                    e = expert_of(t)
                    pe.wait_ge(x_out, t.i + 1)
                    need(pe, act_done, t.i - 1)
                    for half in range(2):
                        if b_up is not None:
                            nc.tensor.matmul(ps_h[t.odd][:, half, :], c["ones"][0:1, :], b_up[0:1, bass.ds(e * HID + half * (HID // 2), HID // 2)], start=True, stop=False)
                        for ch in range(2):
                            last = nc.tensor.matmul(ps_h[t.odd][:, half, :], xt[:, t.odd, ch, :], w_up[:, bass.ds((e * 2 + ch) * HID + half * (HID // 2), HID // 2)],
                                                    start=ch == 0 and b_up is None, stop=ch == 1)
                    last.then_inc(up_mm, 1)

                def turn_hidden(t):
                    pe.wait_ge(act_done, t.i + 1)
                    need(pe, t_out, 2 * t.i)
                    for ch in range(HC):
                        half, at = ch // 3, ch % 3
                        last = nc.tensor.transpose(ps_t[ch // 4][:, (ch % 4) * P:(ch % 4 + 1) * P], hid[:, t.odd, half, at * P:(at + 1) * P], c["ident"])
                        if ch in (3, 5):
                            last.then_inc(t_mm, 1)

                def down(t):
                    e = expert_of(t)
                    pe.wait_ge(t_out, 2 * (t.i + 1))
                    need(pe, y_out, t.i)
                    if b_down is not None:
                        nc.tensor.matmul(ps_y, c["ones"][0:1, :], b_down[0:1, bass.ds(e * D, D)], start=True, stop=False)
                    for ch in range(HC):
                        last = nc.tensor.matmul(ps_y, ht[:, t.odd, ch, :], w_down[:, bass.ds((e * HC + ch) * D, D)], start=ch == 0 and b_down is None, stop=ch == HC - 1)
                    last.then_inc(down_mm, 1)

                pipelined(pe, n_tiles, {1: turn_rows, 2: up, 3: turn_hidden, 4: down}, 5)

            @block.scalar
            def _(act):
                act.activation(y[:, 0, 0:1], c["ones"][:, 0:1], gelu).then_inc(m.tables, 1)

                def take_rows(t):
                    act.wait_ge(x_mm, t.i + 1)
                    need(act, up_mm, t.i - 1)
                    act.activation(xt[:, t.odd, :, :], ps_x, ACT.Identity).then_inc(x_out, 1)

                def activate(t):
                    act.wait_ge(up_mm, t.i + 1)
                    need(act, t_mm, 2 * (t.i - 1))
                    act.activation(hid[:, t.odd, :, :], ps_h[t.odd], gelu).then_inc(act_done, 1)

                pipelined(act, n_tiles, {1: take_rows, 2: activate}, 5)

            @block.vector
            def _(dve):
                dve.wait_ge(m.tables, tag)

                def take_hidden(t):
                    need(dve, down_mm, t.i - 1)
                    dve.wait_ge(t_mm, 2 * t.i + 1)
                    nc.vector.tensor_copy(ht[:, t.odd, 0:4, :], ps_t[0]).then_inc(t_out, 1)
                    dve.wait_ge(t_mm, 2 * t.i + 2)
                    nc.vector.tensor_copy(ht[:, t.odd, 4:6, :], ps_t[1]).then_inc(t_out, 1)

                def take_rows(t):
                    need(dve, y_sent[t.odd], 16 * t.k)
                    dve.wait_ge(down_mm, t.i + 1)
                    nc.vector.tensor_copy(y[:, t.odd, :], ps_y).then_inc(y_out, 1)

                pipelined(dve, n_tiles, {3: take_hidden, 4: take_rows}, 5)


def linear_attention(nc, dram, m, ps):
    with ExitStack() as ctx:
        def sb(name, shape, dt=F32):
            return ctx.enter_context(nc.sbuf_tensor(name, shape, dt))

        def sem(name):
            return ctx.enter_context(nc.semaphore(name))

        c, p = m.c, m.p
        index = sb("gather_index", [P, 2, 2], U32)
        gate = sb("gate_tile", [P, 2, 2])
        y = sb("expert_rows", [P, 2, 2, D])
        st = sb("bn_sums4", [P, 2, 2, 6])
        mv = sb("bn_mean_var4", [P, 2, 2, 2])
        col = sb("columns4", [P, 2, 4])
        xn = sb("xn", [P, 2, 2, D])
        xt = sb("xn_turned", [HD, 2, 2, 2, P])
        qk = sb("qk_turned", [HD, 2, 4, P])
        v = sb("v_rows", [P, 2, D])
        w = sb("weights_t", [P, 2, P])
        ps_t = [ps[0:HD, b, 0:256].rearrange("p (c t) -> p c t", c=2) for b in (0, 5)]
        ps_qk = ps[0:HD, 1, :].rearrange("p (n t) -> p n t", n=4)
        ps_v, ps_s, ps_o, ps_l = ps[:, 2, 0:D], ps[:, 3, 0:P], ps[:, 4, 0:D], ps[:, 6, 0:E2]

        y_in = [sem("expert_rows_even"), sem("expert_rows_odd")]
        (index_set, gate_set, first_added, h3, sums_a, mv_a, eps_a, rstd_a, xn_a, t_mm_a, t_out_a, qk_mm, v_mm, qk_out, v_out, s_mm, w_out, o_mm, h4,
         sums_b, mv_b, eps_b, rstd_b, xn_b, t_mm_b, t_out_b, row_kept, l_mm, l_out) = (sem(n) for n in (
            "index_set", "gate_set", "first_expert_added", "h3_ready", "sums_a", "mean_var_a", "var_eps_a", "rstd_a", "xn_a_ready", "turned_a_mm",
            "turned_a_out", "qk2_product", "v2_product", "qk2_out", "v2_out", "score2_product", "weights_ready", "attended2", "h4_ready", "sums_b",
            "mean_var_b", "var_eps_b", "rstd_b", "xn_b_ready", "turned_b_mm", "turned_b_out", "xn_b_kept", "logit2_product", "logits2_out"))

        def row(t, i):
            return t[:, bass.ds(i, 1), :].rearrange("p a d -> p (a d)")

        with nc.Block() as block:
            @block.gpsimd
            def _(pool):
                def gather(t):
                    pool.wait_ge(index_set, t.i + 1)
                    need(pool, h3, t.i - 1)
                    for k in range(2):
                        nc.gpsimd.indirect_dma_start(out=y[:, t.odd, k, :], out_offset=None, in_=dram["y1"],
                                                     in_offset=bass.IndirectOffsetOnAxis(ap=index[:, t.odd, k:k + 1], axis=0)).then_inc(y_in[t.odd], 16)

                def root(t, n, known, eps_done, done, used):
                    pool.wait_ge(known, t.i + 1)
                    need(pool, used, t.i - 1)
                    nc.gpsimd.tensor_tensor(col[:, t.odd, 2 * n:2 * n + 1], mv[:, t.odd, n, 1:2], c["eps"], ALU.add).then_inc(eps_done, 1)
                    pool.wait_ge(eps_done, t.i + 1)
                    nc.gpsimd.tensor_tensor(col[:, t.odd, 2 * n + 1:2 * n + 2], col[:, t.odd, 2 * n:2 * n + 1], c["minus_half"], ALU.pow).then_inc(done, 1)

                def root_a(t):
                    root(t, 0, mv_a, eps_a, rstd_a, xn_a)

                def root_b(t):
                    root(t, 1, mv_b, eps_b, rstd_b, xn_b)

                def keep(t):
                    pool.wait_ge(xn_b, t.i + 1)
                    nc.gpsimd.tensor_copy(row(m.rows, t.i), xn[:, t.odd, 1, :]).then_inc(row_kept, 1)

                pipelined(pool, TILES, {0: gather, 2: root_a, 6: root_b, 7: keep}, 9, straight=True)

            @block.vector
            def _(dve):
                def set_index(t):
                    need(dve, y_in[t.odd], 32 * t.k)
                    nc.vector.tensor_copy(index[:, t.odd, :], m.slot1[:, bass.ds(t.i * 2, 2)]).then_inc(index_set, 1)
                    need(dve, h3, t.i - 1)
                    nc.vector.tensor_copy(gate[:, t.odd, :], m.gate[:, bass.ds(t.i, 1), :].rearrange("p a k -> p (a k)")).then_inc(gate_set, 1)

                def combine(t):
                    dve.wait_ge(y_in[t.odd], 32 * (t.k + 1))
                    dve.wait_ge(gate_set, t.i + 1)
                    nc.vector.scalar_tensor_tensor(row(m.h, t.i), y[:, t.odd, 0, :], gate[:, t.odd, 0:1], row(m.h, t.i), ALU.mult, ALU.add).then_inc(first_added, 1)
                    dve.wait_ge(first_added, t.i + 1)
                    nc.vector.scalar_tensor_tensor(row(m.h, t.i), y[:, t.odd, 1, :], gate[:, t.odd, 1:2], row(m.h, t.i), ALU.mult, ALU.add).then_inc(h3, 1)
                    moments(t, 0, h3, sums_a, mv_a)

                def moments(t, n, ready, sums, done):
                    need_alone(dve, m, (ready, t.i + 1))
                    nc.vector.bn_stats(st[:, t.odd, n, :], row(m.h, t.i)).then_inc(sums, 1)
                    need_alone(dve, m, (sums, t.i + 1))
                    nc.vector.bn_aggr(mv[:, t.odd, n, :], st[:, t.odd, n, :]).then_inc(done, 1)

                def norm_a(t):
                    dve.wait_ge(rstd_a, t.i + 1)
                    need(dve, t_mm_a, t.i - 1)
                    nc.vector.tensor_scalar(xn[:, t.odd, 0, :], row(m.h, t.i), mv[:, t.odd, 0, 0:1], col[:, t.odd, 1:2], ALU.subtract, ALU.mult).then_inc(xn_a, 1)

                def take_qkv(t):
                    dve.wait_ge(qk_mm, t.i + 1)
                    need(dve, s_mm, t.i - 1)
                    nc.vector.tensor_tensor(qk[:, t.odd, :, :], ps_qk, p["b_qk"][0:HD, :].unsqueeze(2).to_broadcast([HD, 4, P]), ALU.add).then_inc(qk_out, 1)
                    dve.wait_ge(v_mm, t.i + 1)
                    need(dve, o_mm, t.i - 1)
                    nc.vector.tensor_tensor(v[:, t.odd, :], ps_v, p["b_v"], ALU.add).then_inc(v_out, 1)

                def decay(t):
                    dve.wait_ge(s_mm, t.i + 1)
                    need(dve, o_mm, t.i - 1)
                    nc.vector.tensor_tensor(w[:, t.odd, :], ps_s, c["decay"], ALU.mult).then_inc(w_out, 1)

                def residual(t):
                    dve.wait_ge(o_mm, t.i + 1)
                    need(dve, xn_b, t.i - 1)
                    nc.vector.tensor_tensor(row(m.h, t.i), row(m.h, t.i), ps_o, ALU.add).then_inc(h4, 1)
                    moments(t, 1, h4, sums_b, mv_b)

                def norm_b(t):
                    dve.wait_ge(rstd_b, t.i + 1)
                    need(dve, t_mm_b, t.i - 1)
                    need(dve, row_kept, t.i - 1)
                    nc.vector.tensor_scalar(xn[:, t.odd, 1, :], row(m.h, t.i), mv[:, t.odd, 1, 0:1], col[:, t.odd, 3:4], ALU.subtract, ALU.mult).then_inc(xn_b, 1)

                def take_logits(t):
                    dve.wait_ge(l_mm, t.i + 1)
                    nc.vector.tensor_copy(m.logits2[:, bass.ds(t.i * E2, E2)], ps_l).then_inc(l_out, 1)

                pipelined(dve, TILES, {0: set_index, 2: combine, 3: norm_a, 4: take_qkv, 5: decay, 6: residual, 7: norm_b, 8: take_logits}, 9)

            @block.scalar
            def _(act):
                def take_a(t):
                    act.wait_ge(t_mm_a, t.i + 1)
                    need(act, v_mm, t.i - 1)
                    act.activation(xt[:, t.odd, 0, :, :], ps_t[0], ACT.Identity).then_inc(t_out_a, 1)

                def take_b(t):
                    act.wait_ge(t_mm_b, t.i + 1)
                    need(act, l_mm, t.i - 1)
                    act.activation(xt[:, t.odd, 1, :, :], ps_t[1], ACT.Identity).then_inc(t_out_b, 1)

                pipelined(act, TILES, {3: take_a, 7: take_b}, 9)

            @block.tensor
            def _(pe):
                pe.wait_ge(m.w_qkv_loaded, 16)
                pe.wait_ge(m.wg_loaded, 16)

                def turn(t, n, ready, freed, done):
                    pe.wait_ge(ready, t.i + 1)
                    need(pe, freed, t.i)
                    for ch in range(2):
                        last = nc.tensor.transpose(ps_t[n][:, ch, :], xn[:, t.odd, n, ch * HD:(ch + 1) * HD], c["ident"])
                    last.then_inc(done, 1)

                def turn_a(t):
                    turn(t, 0, xn_a, t_out_a, t_mm_a)

                def turn_b(t):
                    turn(t, 1, xn_b, t_out_b, t_mm_b)

                def project(t):
                    pe.wait_ge(t_out_a, t.i + 1)
                    need(pe, qk_out, t.i)
                    for n in range(4):
                        for ch in range(2):
                            last = nc.tensor.matmul(ps_qk[:, n, :], m.w_qkv[:, ch, n * HD:(n + 1) * HD], xt[:, t.odd, 0, ch, :], start=ch == 0, stop=ch == 1)
                    last.then_inc(qk_mm, 1)
                    need(pe, v_out, t.i)
                    for ch in range(2):
                        last = nc.tensor.matmul(ps_v, xt[:, t.odd, 0, ch, :], m.w_qkv[:, ch, 2 * D:3 * D], start=ch == 0, stop=ch == 1)
                    last.then_inc(v_mm, 1)

                def score(t):
                    pe.wait_ge(qk_out, t.i + 1)
                    need(pe, w_out, t.i)
                    for ch in range(2):
                        last = nc.tensor.matmul(ps_s, qk[:, t.odd, 2 + ch, :], qk[:, t.odd, ch, :], start=ch == 0, stop=ch == 1)
                    last.then_inc(s_mm, 1)

                def attend(t):
                    pe.wait_ge(w_out, t.i + 1)
                    pe.wait_ge(v_out, t.i + 1)
                    need(pe, h4, t.i)
                    nc.tensor.matmul(ps_o, w[:, t.odd, :], v[:, t.odd, :], start=True, stop=True).then_inc(o_mm, 1)

                def route(t):
                    pe.wait_ge(t_out_b, t.i + 1)
                    need(pe, l_out, t.i)
                    for ch in range(2):
                        last = nc.tensor.matmul(ps_l, xt[:, t.odd, 1, ch, :], m.wg[:, ch, :], start=ch == 0, stop=ch == 1)
                    last.then_inc(l_mm, 1)

                pipelined(pe, TILES, {3: turn_a, 4: project, 5: score, 6: attend, 7: turn_b, 8: route}, 9)


def choose_one(nc, m, banks):
    with ExitStack() as ctx:
        def sb(name, shape, dt=F32):
            return ctx.enter_context(nc.sbuf_tensor(name, shape, dt))

        z = sb("seq_logits", [P, TILES, E2])
        e = sb("seq_exp", [P, TILES, E2])
        best = sb("seq_best", [P, TILES])
        mean_mm = ctx.enter_context(nc.semaphore("logits_averaged"))
        exp_done = ctx.enter_context(nc.semaphore("seq_exp_ready"))
        step = ctx.enter_context(nc.semaphore("choice_step"))
        wide = [P, TILES, E2]
        with nc.Block() as block:
            @block.tensor
            def _(pe):
                nc.tensor.matmul(banks[0][:, 0:TILES * E2], m.c["seq_mean"], m.logits2[:, :], start=True, stop=True).then_inc(mean_mm, 1)

            @block.scalar
            def _(act):
                act.wait_ge(step, 3)
                act.activation(e[:, :, :], e[:, :, :], ACT.Exp).then_inc(exp_done, 1)

            @block.vector
            def _(dve):
                done = [0]

                def then(ins):
                    done[0] += 1
                    ins.then_inc(step, 1)
                    dve.wait_ge(step, done[0])

                dve.wait_ge(mean_mm, 1)
                then(nc.vector.tensor_copy(z[:, :, :].rearrange("p i e -> p (i e)"), banks[0][:, 0:TILES * E2]))
                then(nc.vector.reduce_max(best[:, :], z[:, :, :], AX_X))
                then(nc.vector.tensor_tensor(e[:, :, :], z[:, :, :], best[:, :].unsqueeze(2).to_broadcast(wide), ALU.subtract))
                then(nc.vector.tensor_tensor(z[:, :, :], z[:, :, :], best[:, :].unsqueeze(2).to_broadcast(wide), ALU.is_equal))
                then(nc.vector.scalar_tensor_tensor(z[:, :, :], z[:, :, :], -float(E2), m.c["iota"][:, 0:E2].unsqueeze(1).to_broadcast(wide), ALU.mult, ALU.add))
                then(nc.vector.tensor_reduce(best[:, :], z[:, :, :], AX_X, ALU.min))
                then(nc.vector.tensor_scalar(m.pick2[:, :], best[:, :], float(E2), None, ALU.add))
                dve.wait_ge(exp_done, 1)
                then(nc.vector.reduce_sum(best[:, :], e[:, :, :], AX_X))
                then(nc.vector.reciprocal(m.score2[:, :], best[:, :]))


def finish(nc, dram, m):
    with ExitStack() as ctx:
        def sb(name, shape, dt=F32):
            return ctx.enter_context(nc.sbuf_tensor(name, shape, dt))

        def sem(name):
            return ctx.enter_context(nc.semaphore(name))

        index, score = sb("gather_index_last", [P, 2], U32), sb("score_tile", [P, 2])
        y, o = sb("expert_rows_last", [P, 2, D]), sb("out_rows", [P, 2, D])
        index_set, score_set, o_done = sem("index_set_last"), sem("score_set_last"), sem("out_ready")
        y_in = [sem("expert_rows_last_even"), sem("expert_rows_last_odd")]
        sent = [sem("out_sent_even"), sem("out_sent_odd")]
        with nc.Block() as block:
            @block.gpsimd
            def _(pool):
                def gather(t):
                    pool.wait_ge(index_set, t.i + 1)
                    need(pool, o_done, t.i - 1)
                    nc.gpsimd.indirect_dma_start(out=y[:, t.odd, :], out_offset=None, in_=dram["y2"],
                                                 in_offset=bass.IndirectOffsetOnAxis(ap=index[:, t.odd:t.odd + 1], axis=0)).then_inc(y_in[t.odd], 16)

                pipelined(pool, TILES, {0: gather}, 2, straight=True)

            @block.vector
            def _(dve):
                def set_index(t):
                    need(dve, y_in[t.odd], 16 * t.k)
                    nc.vector.tensor_copy(index[:, t.odd:t.odd + 1], m.slot2[:, bass.ds(t.i, 1)]).then_inc(index_set, 1)
                    need(dve, o_done, t.i - 1)
                    nc.vector.tensor_copy(score[:, t.odd:t.odd + 1], m.score2[:, bass.ds(t.i, 1)]).then_inc(score_set, 1)

                def add(t):
                    dve.wait_ge(y_in[t.odd], 16 * (t.k + 1))
                    dve.wait_ge(score_set, t.i + 1)
                    need(dve, sent[t.odd], 16 * t.k)
                    nc.vector.scalar_tensor_tensor(o[:, t.odd, :], y[:, t.odd, :], score[:, t.odd:t.odd + 1], m.h[:, bass.ds(t.i, 1), :].rearrange("p a d -> p (a d)"),
                                                   ALU.mult, ALU.add).then_inc(o_done, 1)

                pipelined(dve, TILES, {0: set_index, 1: add}, 2)

            @block.sync
            def _(sp):
                def store(t):
                    sp.wait_ge(o_done, t.i + 1)
                    sp.dma_start(dram["out"][bass.ds(t.i * P, P), :], o[:, t.odd, :]).then_inc(sent[t.odd], 16)

                pipelined(sp, TILES, {1: store}, 2)
                for half in range(2):
                    sp.wait_ge(sent[half], 16 * TILES // 2)


def host_layout(v):
    def chunks(a, n):
        a = np.asarray(a).reshape(n, -1).T
        return np.concatenate([a, np.zeros((P - a.shape[0], n), a.dtype)]) if a.shape[0] < P else a

    wkv = v["L0_tok_Wkv"]
    rows = {
        "bq": np.tile(v["L0_tok_bq"], 16)[:, None], "bkv": np.tile(v["L0_tok_bkv"], 16)[:, None],
        "ln_w": chunks(v["L0_attn_ln_w"], 2), "ln_b": chunks(v["L0_attn_ln_b"], 2),
        "conv_w": v["L0_attn_conv_w"].reshape(5, P, KC).transpose(1, 0, 2).reshape(P, 20),
        "conv_b": chunks(v["L0_attn_conv_b"], 5), "skip": chunks(np.repeat(v["L0_attn_D"], HP), 3),
        "norm_w": chunks(v["L0_attn_norm_w"], 3), "b_qk": chunks(v["L1_attn_b_qkv"][:2 * D], 4),
        "A_log": np.tile(v["L0_attn_A_log"], (P, 1)), "dt_bias": np.tile(v["L0_attn_dt_bias"], (P, 1)),
        "bq_row": np.tile(v["L0_tok_bq"], (P, 16)), "b_v": np.tile(v["L1_attn_b_qkv"][2 * D:], (P, 1)),
        "wq": np.tile(v["L0_tok_Wq"].T, (8, 8)), "wk": np.tile(wkv[:8].T, (8, 8)), "wv": np.tile(wkv[8:].T, (8, 8)),
    }
    return {
        "x": v["x"].reshape(2 * N_TOK, D),
        "param": np.concatenate([rows[n] for n, _ in PARAMS], axis=1),
        "const": constant_table()[0],
        "w_in": v["L0_attn_W_in"],
        "w_out": v["L0_attn_W_out"],
        "w_fc": v["L0_ffn_w_fc"].reshape(2, HD, HID, E1).transpose(1, 3, 0, 2).reshape(HD, E1 * 2 * HID),
        "w_proj": v["L0_ffn_w_proj"].reshape(HC, P, D, E1).transpose(1, 3, 0, 2).reshape(P, E1 * HC * D),
        "w_gate": v["L0_ffn_w_gate"],
        "w_qkv": v["L1_attn_W_qkv"],
        "wg": v["L1_ffn_Wg"].T,
        "w1": v["L1_ffn_W1"].reshape(E2, 2, HD, HID).transpose(2, 0, 1, 3).reshape(HD, E2 * 2 * HID),
        "b1": v["L1_ffn_b1"].reshape(1, E2 * HID),
        "w2": v["L1_ffn_W2"].reshape(E2, HC, P, D).transpose(2, 0, 1, 3).reshape(P, E2 * HC * D),
        "b2": v["L1_ffn_b2"].reshape(1, E2 * D),
    }


OUTPUTS = {"out": (N_TOK, D)}
DEBUG = {}
SCRATCH = {"x1": (T1 * P, D), "y1": (T1 * P, D), "x2": (T2 * P, D), "y2": (T2 * P, D)}


def kernel(**inputs):
    import concourse.bacc as bacc
    from concourse.bass_utils import run_bass_kernel_spmd

    arrays = {n: np.ascontiguousarray(a) for n, a in host_layout({n: np.asarray(a) for n, a in inputs.items()}).items()}
    nc = bacc.Bacc("TRN2", target_bir_lowering=False, num_devices=1)
    dram = {n: nc.dram_tensor("in_" + n, a.shape, F32, kind="ExternalInput").ap() for n, a in arrays.items()}
    for n, shape in {**OUTPUTS, **DEBUG}.items():
        dram[n] = nc.dram_tensor(n, shape, F32, kind="ExternalOutput").ap()
    for n, shape in SCRATCH.items():
        dram[n] = nc.dram_tensor(n, shape, F32, kind="Internal").ap()
    build(nc, dram)
    got = run_bass_kernel_spmd(nc, [{"in_" + n: a for n, a in arrays.items()}], core_ids=[0]).results[0]
    return got["out"].reshape(64, BLK, D)
```

```python
from contextlib import ExitStack

import concourse.bass as bass
import numpy as np
from concourse import mybir

F32 = mybir.dt.float32
BF16 = mybir.dt.bfloat16
F32R = mybir.dt.float32r
I32 = mybir.dt.int32
U32 = mybir.dt.uint32
ALU = mybir.AluOpType
ACT = mybir.ActivationFunctionType
AX_X = mybir.AxisListType.X

P = 128
BLK = 32
D = 192
HD = 96
N_TOK = 2048
TILES = N_TOK // P
FR, FR2 = 16, 8
NH, HP = 6, 64
DI = NH * HP
DS = 128
CONV = DI + 2 * DS
KC = 4
NIN = 2 * DI + 2 * DS + NH
SB = 512
HID = 768
HC = HID // P
E1, E2 = 8, 3
T1 = (2 * N_TOK + E1 * (P - 1)) // P
T2 = (N_TOK + E2 * (P - BLK)) // P
EPS = 1e-5
SC = float(1.0 / np.sqrt(np.float32(D)))


def constant_table():
    p = np.arange(P)
    same32 = p[:, None] // BLK == p[None, :] // BLK
    diff = p[None, :] - p[:, None]
    decay = np.where(same32 & (diff >= 0), np.float32(0.99) ** np.maximum(diff, 0).astype(np.float32), 0) / np.sqrt(np.float32(D))
    parts = {
        "ident": np.eye(P),
        "group_bar": np.where(p[:, None] // FR2 == p[None, :] // FR2, 0.0, -1e30),
        "frame_sel": np.tile((p[:, None] // FR == np.arange(64)[None, :] // FR2), (1, 3)),
        "after": same32 & (p[:, None] > p[None, :]),
        "upto_all": same32 & (p[:, None] <= p[None, :]),
        "upto": (p[:, None] % BLK) <= np.arange(BLK)[None, :],
        "before": p[:, None] < p[None, :],
        "ones": np.ones((P, P)),
        "decay": decay,
        "seq_mean": same32 / float(BLK),
        "iota": np.tile(p[None, :], (P, 1)),
        "row_index": p[:, None],
        "minus_half": np.full((P, 1), -0.5),
        "eps": np.full((P, 1), EPS),
    }
    at, n = {}, 0
    for name, a in parts.items():
        at[name] = (n, a.shape[1])
        n += a.shape[1]
    return np.concatenate([a.astype(np.float32) for a in parts.values()], axis=1), at


PARAMS = [("bq", 1), ("bkv", 1), ("ln_w", 2), ("ln_b", 2), ("conv_w", 20), ("conv_b", 5), ("skip", 3), ("norm_w", 3),
          ("b_qk", 4), ("A_log", NH), ("dt_bias", NH), ("bq_row", P), ("b_v", D), ("wq", 64), ("wk", 64), ("wv", 64)]


def param_places():
    at, n = {}, 0
    for name, w in PARAMS:
        at[name] = (n, w)
        n += w
    return at, n


class Tile:
    def __init__(self, k, odd):
        self.k, self.odd, self.i = k, odd, k * 2 + odd


def pipelined(eng, n, stages, depth, straight=False):
    first = depth + 1
    first += (n - first) % 2

    def step(t, turn=0):
        for lag, stage in stages:
            i = t - lag
            if 0 <= i and (i < n or not isinstance(turn, int)):
                stage(Tile(turn + i // 2, i % 2))

    if straight or first >= n:
        for t in range(n + depth - 1):
            step(t)
        return
    for t in range(first):
        step(t)
    with eng.Fori(0, (n - first) // 2) as turn:
        step(first, turn)
        step(first + 1, turn)
    for t in range(n, n + depth - 1):
        step(t)


def need(eng, sem, value):
    if not (isinstance(value, int) and value <= 0):
        eng.wait_ge(sem, value)


def need_alone(eng, m, *counts):
    counts = [(sem, value if isinstance(value, int) else eng.snap(value)) for sem, value in counts]
    if not all(isinstance(value, int) for _, value in counts):
        eng.wait_ge(m.loaded, 32)
    for sem, value in counts:
        need(eng, sem, value)


def after_first(eng, sem, turn, value):
    if not (isinstance(turn, int) and turn == 0):
        eng.wait_ge(sem, value)


def build(nc, dram):
    with ExitStack() as ctx:
        def sb(name, shape, dt=F32):
            return ctx.enter_context(nc.sbuf_tensor(name, shape, dt))

        m = Memory(nc, ctx, sb)
        ps = ctx.enter_context(nc.psum_tensor("psum", [P, 8, 512], F32))
        banks = [ps[:, n, :] for n in range(8)]
        with ExitStack() as early:
            s = SsmMemory(nc, early)
            with ExitStack() as inputs:
                s.hold_inputs(inputs)
                merge_frames(nc, dram, m, s, banks)
                project_in(nc, dram, m, s, banks)
            state_space(nc, dram, m, s, ps)
            nc.clear_and_free_semaphores(s.semaphores)
            nc.all_engine_barrier()
        with ExitStack() as late:
            w = ExpertMemory(nc, late)
            w.load(nc, dram)
            dispatch(nc, m, banks, 1, E1, 2 * TILES, m.pick[:, :], m.slot1, m.expert1, m.token1, T1, True)
            experts(nc, m, ps, 1, E1, T1, m.expert1, m.token1, dram["x1"], dram["y1"], m.w_fc, w.w_proj, None, ACT.Gelu_apprx_tanh,
                    [(m.w_fc_loaded, 16), (w.w_proj_loaded, 16)])
            linear_attention(nc, dram, m, ps)
            choose_one(nc, m, banks)
            dispatch(nc, m, banks, 2, E2, TILES, m.pick2[:, :], m.slot2, m.expert2, m.token2, T2, False)
            experts(nc, m, ps, 2, E2, T2, m.expert2, m.token2, dram["x2"], dram["y2"], w.w1, w.w2, w.b2, ACT.Gelu, [(w.second_loaded, 48)])
            finish(nc, dram, m)


class Memory:

    def __init__(self, nc, ctx, sb):
        table, at = constant_table()
        places, width = param_places()
        self.const = sb("const", [P, table.shape[1]])
        self.param = sb("param", [P, width])
        self.c = {n: self.const[:, a:a + w] for n, (a, w) in at.items()}
        self.p = {n: self.param[:, a:a + w] for n, (a, w) in places.items()}
        self.h = sb("h", [P, TILES, D])
        self.dt = sb("dt", [P, TILES * NH])
        self.dt_a = sb("dt_a", [P, TILES * NH])
        self.top = sb("top", [P, TILES * 2])
        self.pick = sb("pick", [P, TILES * 2])
        self.w_out = sb("w_out", [P, 3, D])
        self.w_gate = sb("w_gate", [HD, 2, E1])
        self.w_fc = sb("w_fc", [HD, E1 * 2 * HID])
        self.w_qkv = sb("w_qkv", [HD, 2, 3 * D])
        self.wg = sb("wg", [HD, 2, E2])
        self.gate = sb("gate", [P, TILES, 2])
        self.slot1 = sb("slot1", [P, 2 * TILES], U32)
        self.expert1 = sb("expert1", [P, T1], I32)
        self.token1 = sb("token1", [P, T1], U32)
        self.logits2 = sb("logits2", [P, TILES * E2])
        self.pick2 = sb("pick2", [P, TILES])
        self.score2 = sb("score2", [P, TILES])
        self.slot2 = sb("slot2", [P, TILES], U32)
        self.expert2 = sb("expert2", [P, T2], I32)
        self.token2 = sb("token2", [P, T2], U32)
        self.loaded = ctx.enter_context(nc.semaphore("constants_loaded"))
        self.w_in_loaded = ctx.enter_context(nc.semaphore("w_in_loaded"))
        self.w_out_loaded = ctx.enter_context(nc.semaphore("w_out_loaded"))
        self.w_gate_loaded = ctx.enter_context(nc.semaphore("w_gate_loaded"))
        self.w_fc_loaded = ctx.enter_context(nc.semaphore("w_fc_loaded"))
        self.w_qkv_loaded = ctx.enter_context(nc.semaphore("w_qkv_loaded"))
        self.wg_loaded = ctx.enter_context(nc.semaphore("wg_loaded"))
        self.tables = ctx.enter_context(nc.semaphore("gelu_table_loaded"))


class ExpertMemory:

    def __init__(self, nc, ctx):
        def sb(name, shape):
            return ctx.enter_context(nc.sbuf_tensor(name, shape, F32))

        self.w_proj = sb("w_proj", [P, E1 * HC * D])
        self.w1 = sb("w1", [HD + 1, E2 * 2 * HID])
        self.w2 = sb("w2", [P, E2 * HC * D])
        self.b2 = sb("b2", [1, E2 * D])
        self.w_proj_loaded = ctx.enter_context(nc.semaphore("w_proj_loaded"))
        self.second_loaded = ctx.enter_context(nc.semaphore("second_weights_loaded"))

    def load(self, nc, dram):
        with nc.Block() as block:
            @block.sync
            def _(sp):
                sp.dma_start(self.w_proj[:, :], dram["w_proj"]).then_inc(self.w_proj_loaded, 16)
                for tile, name in ((self.w1, "w1"), (self.w2, "w2"), (self.b2, "b2")):
                    sp.dma_start(tile[:, :], dram[name]).then_inc(self.second_loaded, 16)


class SsmMemory:

    def __init__(self, nc, ctx):
        def sb(name, shape):
            return ctx.enter_context(nc.sbuf_tensor(name, shape, F32))

        self.nc, self.semaphores = nc, []
        self.xbc = sb("xbc", [P, 5, N_TOK])
        self.sz = sb("sz", [P, 3, N_TOK])

    def hold_inputs(self, ctx):
        def sb(name, shape):
            return ctx.enter_context(self.nc.sbuf_tensor(name, shape, F32R))

        self.w_parts = sb("w_in_parts", [HD, 2, 2, NIN - NH])
        self.ut_parts = sb("ut_parts", [HD, 2, 2, N_TOK])

    def semaphore(self, name):
        self.semaphores.append(self.nc.alloc_semaphore(name))
        return self.semaphores[-1]


def merge_frames(nc, dram, m, s, banks):
    with ExitStack() as ctx:
        def sb(name, shape, dt=F32):
            return ctx.enter_context(nc.sbuf_tensor(name, shape, dt))

        def sem(name):
            return s.semaphore(name)

        c, p = m.c, m.p
        x = sb("x_frames", [P, 2, 2, D])
        w_tok = sb("w_tok", [P, 3, 64])
        bq_sc = sb("bq_scaled", [P, 1])
        ones_row = c["ones"][0:1, 0:HD]
        qk = sb("qk", [HD, 2, 2, 2, P])
        s_m = sb("scores", [P, 2, P])
        mx = sb("row_max", [P, 2, 2])
        pr = sb("probs", [P, 2, P])
        rs = sb("row_sum", [P, 2, 2])
        pt = sb("probs_t", [P, 2, P])
        v = s.sz[:, :, :].rearrange("p c t -> p (c t)")[:, 0:TILES * D].rearrange("p (i d) -> p i d", d=D)
        w_in = s.xbc[0:HD, :, :].rearrange("p c t -> p (c t)")[:, 0:2 * NIN].rearrange("p (c n) -> p c n", c=2)
        st = sb("bn_sums", [P, 2, 2, 6])
        mv = sb("bn_mean_var", [P, 2, 2, 2])
        ve = sb("var_eps", [P, 2, 2])
        rstd = sb("rstd", [P, 2, 2])
        a = sb("normed", [P, 2, D])
        u = sb("normed_twice", [P, 2, D])
        ut = sb("ut_tile", [HD, 2, 2, P])
        ps_qk = [banks[o][0:HD, :].rearrange("p (w c t) -> p w c t", w=2, c=2) for o in range(2)]
        ps_qv = banks[2][:, 0:2 * D].rearrange("p (w d) -> p w d", w=2)
        ps_s, ps_pt, ps_o = banks[3][:, 0:P], banks[4][:, 0:P], banks[5][:, 0:D]
        ps_u = banks[6][0:HD, 0:256].rearrange("p (c t) -> p c t", c=2)
        ps_dt = banks[7][:, 0:NH]

        x_in = [sem("x_in_even"), sem("x_in_odd")]
        w_ready, b_ready = sem("w_tok_ready"), sem("bq_scaled_ready")
        qk_mm, qv_mm, s_mm, pt_mm, o_mm, u_mm, dt_mm = (sem(n) for n in (
            "qk_product", "qv_product", "score_product", "probs_transposed", "attended", "u_transposed", "dt_product"))
        qk_ev, qn_ev, vn_ev = sem("qk_out"), sem("q_rows_out"), sem("v_rows_out")
        s_bar, s_max, n_max, p_exp, pt_ev = sem("scores_barred"), sem("scores_maxed"), sem("neg_max_ready"), sem("probs_ready"), sem("probs_t_out")
        r_inv, h_out, st1, mv1, ve1, rstd1 = (sem(n) for n in ("sum_inverted", "h_ready", "sums1", "mean_var1", "var_eps1", "rstd1"))
        a_out, st2, mv2, ve2, rstd2, ha = (sem(n) for n in ("a_ready", "sums2", "mean_var2", "var_eps2", "rstd2", "h_plus_a"))
        u_out, ut_ev, ut_kept, ut_low, dt_out, w_high = (sem(n) for n in ("u_ready", "ut_out", "ut_high_ready", "ut_low_ready", "dt_out", "w_in_high_ready"))

        x_rows = dram["x"].rearrange("(i h p) d -> i p h d", h=2, p=P)

        def row(t, i):
            return t[:, bass.ds(i, 1), :].rearrange("p a d -> p (a d)")

        with nc.Block() as block:
            @block.sync
            def _(sp):
                sp.dma_start(m.const[:, :], dram["const"]).then_inc(m.loaded, 16)
                sp.dma_start(m.param[:, :], dram["param"]).then_inc(m.loaded, 16)

                def load(t):
                    need(sp, qk_mm, t.i - 1)
                    need(sp, qv_mm, t.i - 1)
                    sp.dma_start(x[:, t.odd, :, :], x_rows[bass.ds(t.i, 1), :, :, :].rearrange("a p h d -> (a p) h d")).then_inc(x_in[t.odd], 16)

                pipelined(sp, TILES, [(0, load)], 1)
                sp.dma_start(m.w_fc[:, :], dram["w_fc"]).then_inc(m.w_fc_loaded, 16)
                sp.dma_start(m.w_qkv[:, :, :], dram["w_qkv"].rearrange("(c p) n -> p c n", p=HD)).then_inc(m.w_qkv_loaded, 16)
                sp.dma_start(m.wg[:, :, :], dram["wg"].rearrange("(c p) e -> p c e", p=HD)).then_inc(m.wg_loaded, 16)

            @block.tensor
            def _(pe):
                pe.wait_ge(m.loaded, 32)
                pe.wait_ge(w_ready, 1)

                def project(t):
                    pe.wait_ge(x_in[t.odd], 16 * (t.k + 1))
                    need(pe, qk_ev, t.i - 1)
                    for ch in range(2):
                        nc.tensor.matmul(ps_qk[t.odd][:, 0, ch, :], ones_row, p["bq_row"][0:1, :], start=True, stop=False)
                        for half in range(2):
                            nc.tensor.matmul(ps_qk[t.odd][:, 0, ch, half * 64:half * 64 + 64], x[:, t.odd, half, ch * HD:(ch + 1) * HD],
                                             w_tok[:, 0, :], start=False, stop=half == 1)
                    for ch in range(2):
                        for half in range(2):
                            last = nc.tensor.matmul(ps_qk[t.odd][:, 1, ch, half * 64:half * 64 + 64], x[:, t.odd, half, ch * HD:(ch + 1) * HD],
                                                    w_tok[:, 1, :], start=True, stop=True)
                    last.then_inc(qk_mm, 1)
                    need(pe, qn_ev, t.i)
                    need(pe, vn_ev, t.i)
                    for w, col in ((0, 0), (1, 2)):
                        for half in range(2):
                            last = nc.tensor.matmul(ps_qv[half * 64:half * 64 + 64, w, :], w_tok[:, col, :],
                                                    x[:, t.odd, half, :], start=True, stop=True)
                    last.then_inc(qv_mm, 1)

                def score(t):
                    pe.wait_ge(qk_ev, t.i + 1)
                    need(pe, s_bar, t.i)
                    for ch in range(2):
                        last = nc.tensor.matmul(ps_s, qk[:, t.odd, 0, ch, :], qk[:, t.odd, 1, ch, :], start=ch == 0, stop=ch == 1)
                    last.then_inc(s_mm, 1)

                def turn_probs(t):
                    pe.wait_ge(p_exp, t.i + 1)
                    need(pe, pt_ev, t.i)
                    nc.tensor.transpose(ps_pt, pr[:, t.odd, :], c["ident"]).then_inc(pt_mm, 1)

                def attend(t):
                    pe.wait_ge(pt_ev, t.i + 1)
                    pe.wait_ge(vn_ev, t.i + 1)
                    need(pe, h_out, t.i)
                    nc.tensor.matmul(ps_o, pt[:, t.odd, :], row(v, t.i), start=True, stop=True).then_inc(o_mm, 1)

                def turn_u(t):
                    pe.wait_ge(u_out, t.i + 1)
                    need(pe, ut_kept, 2 * t.i)
                    for ch in range(2):
                        last = nc.tensor.transpose(ps_u[:, ch, :], u[:, t.odd, ch * HD:(ch + 1) * HD], c["ident"])
                    last.then_inc(u_mm, 1)

                def steps(t):
                    if isinstance(t.i, int) and t.i == 0:
                        pe.wait_ge(m.w_in_loaded, 16)
                    pe.wait_ge(ut_ev, 2 * (t.i + 1))
                    need(pe, dt_out, t.i)
                    for ch in range(2):
                        last = nc.tensor.matmul(ps_dt, ut[:, t.odd, ch, :], w_in[:, ch, NIN - NH:NIN], start=ch == 0, stop=ch == 1)
                    last.then_inc(dt_mm, 1)

                pipelined(pe, TILES, [(2, score), (3, turn_probs), (4, attend), (8, steps), (7, turn_u), (0, project)], 9)

            @block.scalar
            def _(act):
                act.dma_start(w_in, dram["w_in"].rearrange("(c p) n -> p c n", p=HD)).then_inc(m.w_in_loaded, 16)
                act.dma_start(m.w_out[:, :, :], dram["w_out"].rearrange("(c p) n -> p c n", p=P)).then_inc(m.w_out_loaded, 16)
                act.dma_start(m.w_gate[:, :, :], dram["w_gate"].rearrange("(c p) e -> p c e", p=HD)).then_inc(m.w_gate_loaded, 16)
                act.wait_ge(m.loaded, 32)
                act.wait_ge(b_ready, 1)
                act.activation(rs[:, 0, 1:2], c["ones"][:, 0:1], ACT.Exp)
                act.wait_ge(m.w_in_loaded, 16)
                act.activation(s.w_parts[:, 0, :, :], w_in[:, :, 0:NIN - NH], ACT.Identity).then_inc(w_high, 1)

                def take_rows(t):
                    act.wait_ge(qv_mm, t.i + 1)
                    act.activation(row(m.h, t.i), ps_qv[:, 0, :], ACT.Identity, bias=bq_sc[:, 0:1], scale=SC).then_inc(qn_ev, 1)
                    act.activation(row(v, t.i), ps_qv[:, 1, :], ACT.Identity, bias=p["bkv"]).then_inc(vn_ev, 1)

                def exponent(t):
                    act.wait_ge(n_max, t.i + 1)
                    need(act, pt_mm, t.i - 1)
                    act.activation(pr[:, t.odd, :], s_m[:, t.odd, :], ACT.Exp, bias=mx[:, t.odd, 1:2], scale=SC,
                                   accum_out=rs[:, t.odd, 0:1]).then_inc(p_exp, 1)

                def take_u(t):
                    act.wait_ge(u_mm, t.i + 1)
                    need(act, dt_mm, t.i - 1)
                    need(act, ut_low, t.i - 1)
                    for to, done in ((ut[:, t.odd, :, :], ut_ev), (s.ut_parts[:, 0, :, bass.ds(t.i * P, P)], ut_kept)):
                        for ch in range(2):
                            act.activation(to[:, ch, :], ps_u[:, ch, :], ACT.Identity, bias=p["ln_b"][0:HD, ch:ch + 1],
                                           scale=p["ln_w"][0:HD, ch:ch + 1]).then_inc(done, 1)

                pipelined(act, TILES, [(1, take_rows), (2, exponent), (7, take_u)], 9)

            @block.vector
            def _(dve):
                dve.wait_ge(m.loaded, 32)
                for w, name in enumerate(("wq", "wk", "wv")):
                    last = nc.vector.tensor_tensor(w_tok[:, w, :], p[name], c["frame_sel"][:, w * 64:(w + 1) * 64], ALU.mult)
                last.then_inc(w_ready, 1)
                nc.vector.tensor_scalar(bq_sc[:, :], p["bq"], SC, None, ALU.mult).then_inc(b_ready, 1)
                dve.wait_ge(m.w_in_loaded, 16)
                dve.wait_ge(w_high, 1)
                nc.vector.tensor_tensor(s.w_parts[:, 1, :, :], w_in[:, :, 0:NIN - NH], s.w_parts[:, 0, :, :], ALU.subtract)

                def take_qk(t):
                    dve.wait_ge(qk_mm, t.i + 1)
                    need(dve, s_mm, t.i - 1)
                    nc.vector.tensor_copy(qk[:, t.odd, :, :, :], ps_qk[t.odd]).then_inc(qk_ev, 1)

                def bar(t):
                    dve.wait_ge(s_mm, t.i + 1)
                    need(dve, p_exp, t.i - 1)
                    nc.vector.tensor_tensor(s_m[:, t.odd, :], ps_s, c["group_bar"], ALU.add).then_inc(s_bar, 1)

                def maxima(t):
                    dve.wait_ge(s_bar, t.i + 1)
                    nc.vector.reduce_max(mx[:, t.odd, 0:1], s_m[:, t.odd, :], AX_X).then_inc(s_max, 1)

                def negate(t):
                    dve.wait_ge(s_max, t.i + 1)
                    nc.vector.tensor_scalar(mx[:, t.odd, 1:2], mx[:, t.odd, 0:1], -SC, None, ALU.mult).then_inc(n_max, 1)

                def take_probs(t):
                    dve.wait_ge(pt_mm, t.i + 1)
                    need(dve, o_mm, t.i - 1)
                    nc.vector.tensor_copy(pt[:, t.odd, :], ps_pt).then_inc(pt_ev, 1)
                    nc.vector.reciprocal(rs[:, t.odd, 1:2], rs[:, t.odd, 0:1]).then_inc(r_inv, 1)

                def merge(t):
                    dve.wait_ge(o_mm, t.i + 1)
                    dve.wait_ge(r_inv, t.i + 1)
                    need(dve, a_out, t.i - 1)
                    dve.wait_ge(qn_ev, t.i + 1)
                    nc.vector.scalar_tensor_tensor(row(m.h, t.i), ps_o, rs[:, t.odd, 1:2], row(m.h, t.i), ALU.mult, ALU.add).then_inc(h_out, 1)

                def sums_once(t):
                    need_alone(dve, m, (h_out, t.i + 1))
                    nc.vector.bn_stats(st[:, t.odd, 0, :], row(m.h, t.i)).then_inc(st1, 1)

                def moments_once(t):
                    need_alone(dve, m, (st1, t.i + 1))
                    nc.vector.bn_aggr(mv[:, t.odd, 0, :], st[:, t.odd, 0, :]).then_inc(mv1, 1)

                def norm_once(t):
                    dve.wait_ge(rstd1, t.i + 1)
                    need(dve, ha, t.i - 1)
                    need(dve, u_out, t.i - 1)
                    nc.vector.tensor_scalar(a[:, t.odd, :], row(m.h, t.i), mv[:, t.odd, 0, 0:1], rstd[:, t.odd, 0:1], ALU.subtract, ALU.mult).then_inc(a_out, 1)

                def sums_twice(t):
                    need_alone(dve, m, (a_out, t.i + 1))
                    nc.vector.bn_stats(st[:, t.odd, 1, :], a[:, t.odd, :]).then_inc(st2, 1)

                def moments_twice(t):
                    need_alone(dve, m, (st2, t.i + 1))
                    nc.vector.bn_aggr(mv[:, t.odd, 1, :], st[:, t.odd, 1, :]).then_inc(mv2, 1)

                def norm_twice(t):
                    dve.wait_ge(rstd2, t.i + 1)
                    need(dve, u_mm, t.i - 1)
                    nc.vector.tensor_scalar(u[:, t.odd, :], a[:, t.odd, :], mv[:, t.odd, 1, 0:1], rstd[:, t.odd, 1:2], ALU.subtract, ALU.mult).then_inc(u_out, 1)

                def take_dt(t):
                    dve.wait_ge(dt_mm, t.i + 1)
                    nc.vector.tensor_tensor(m.dt[:, bass.ds(t.i * NH, NH)], ps_dt, p["dt_bias"], ALU.add).then_inc(dt_out, 1)

                pipelined(dve, TILES, [(2, bar), (1, take_qk), (2, maxima), (6, norm_twice), (2, negate), (5, norm_once), (3, take_probs), (5, sums_twice),
                                       (4, merge), (5, moments_twice), (4, sums_once), (8, take_dt), (4, moments_once)], 9)

            @block.gpsimd
            def _(pool):
                pool.wait_ge(m.loaded, 32)

                def low_part(t):
                    pool.wait_ge(ut_kept, 2 * (t.i + 1))
                    at = bass.ds(t.i * P, P)
                    nc.gpsimd.tensor_tensor(s.ut_parts[:, 1, :, at], ut[:, t.odd, :, :], s.ut_parts[:, 0, :, at], ALU.subtract).then_inc(ut_low, 1)

                def inverse_root(t, n, known, eps_done, done):
                    pool.wait_ge(known, t.i + 1)
                    nc.gpsimd.tensor_tensor(ve[:, t.odd, n:n + 1], mv[:, t.odd, n, 1:2], c["eps"], ALU.add).then_inc(eps_done, 1)
                    pool.wait_ge(eps_done, t.i + 1)
                    nc.gpsimd.tensor_tensor(rstd[:, t.odd, n:n + 1], ve[:, t.odd, n:n + 1], c["minus_half"], ALU.pow).then_inc(done, 1)

                def roots(t):
                    inverse_root(t, 0, mv1, ve1, rstd1)

                def roots_and_residual(t):
                    inverse_root(t, 1, mv2, ve2, rstd2)
                    nc.gpsimd.tensor_tensor(row(m.h, t.i), row(m.h, t.i), a[:, t.odd, :], ALU.add).then_inc(ha, 1)

                pipelined(pool, TILES, [(8, low_part), (5, roots_and_residual), (4, roots)], 9)


def project_in(nc, dram, m, s, banks):
    with ExitStack() as ctx:
        def sb(name, shape, dt=F32):
            return ctx.enter_context(nc.sbuf_tensor(name, shape, dt))

        def sem(name):
            return s.semaphore(name)

        p = m.p
        n_dt = TILES * NH
        mag, ex, one_ex, ln1, back = (sb(n, [P, n_dt]) for n in ("dt_mag", "dt_exp", "dt_one_exp", "dt_log", "dt_back"))
        e_a = sb("exp_A", [P, NH])
        pre = sb("conv_out", [P, 5, SB])
        mag_done, exp_done, one_done, log_done, back1, back2, back3, sp_done, ea_done, a_done = (sem(n) for n in (
            "dt_mag_ready", "dt_exp_ready", "dt_one_exp_ready", "dt_log_ready", "dt_rounded", "dt_lost_ready",
            "dt_log_mended", "dt_softplus_ready", "exp_A_ready", "dt_A_ready"))
        proj, gate_out, tap3, taps, conv_silu = (sem(n) for n in ("projected", "gate_ready", "last_tap_done", "taps_done", "conv_ready"))

        chunks = [("conv", 0, 3), ("conv", 1, 4), ("gate", 0, 0), ("conv", 2, 5), ("conv", 3, 6), ("gate", 1, 1), ("conv", 4, 7), ("gate", 2, 2)]
        at = {(kind, c): n for n, (kind, c, _) in enumerate(chunks)}
        bank_of = {"conv": banks[0:5], "gate": banks[5:8]}

        with nc.Block() as block:
            @block.tensor
            def _(pe):
                def superblock(j):
                    for kind, c, ch in chunks:
                        if kind == "conv":
                            after_first(pe, taps, j, 3 * (5 * (j - 1) + c + 1))
                        else:
                            after_first(pe, gate_out, j, 3 * (j - 1) + c + 1)
                        terms = [(half, w, u) for w, u in ((0, 1), (1, 0), (0, 0)) for half in range(2)]
                        for half, w, u in terms:
                            last = nc.tensor.matmul(bank_of[kind][c][:, :], s.w_parts[:, w, half, ch * P:(ch + 1) * P], s.ut_parts[:, u, half, bass.ds(j * SB, SB)],
                                                    start=(half, w, u) == terms[0], stop=(half, w, u) == terms[-1])
                        last.then_inc(proj, 1)

                superblock(0)
                with pe.Fori(1, N_TOK // SB) as j:
                    superblock(j)

            @block.scalar
            def _(act):
                act.activation(e_a[:, :], p["A_log"], ACT.Exp).then_inc(ea_done, 1)
                act.wait_ge(mag_done, 1)
                act.activation(ex[:, :], mag[:, :], ACT.Exp, scale=-1.0).then_inc(exp_done, 1)
                act.wait_ge(one_done, 1)
                act.activation(ln1[:, :], one_ex[:, :], ACT.Ln).then_inc(log_done, 1)
                act.wait_ge(ea_done, 1)
                act.wait_ge(a_done, 1)
                act.activation(e_a[:, :], p["A_log"], ACT.Silu).then_inc(ea_done, 1)

                def first_tap(j, c):
                    act.wait_ge(proj, 8 * j + at["conv", c] + 1)
                    after_first(act, conv_silu, j, 5 * (j - 1) + c + 1)
                    act.activation(pre[:, c, :], banks[c][:, :], ACT.Identity, bias=p["conv_b"][:, c:c + 1],
                                   scale=p["conv_w"][:, 4 * c + 3:4 * c + 4]).then_inc(tap3, 1)

                def silu(j, c):
                    act.wait_ge(taps, 3 * (5 * j + c + 1))
                    act.activation(s.xbc[:, c, bass.ds(j * SB, SB)], pre[:, c, :], ACT.Silu).then_inc(conv_silu, 1)

                def gate(j, c):
                    act.wait_ge(proj, 8 * j + at["gate", c] + 1)
                    act.activation(s.sz[:, c, bass.ds(j * SB, SB)], banks[5 + c][:, :], ACT.Silu).then_inc(gate_out, 1)

                def superblock(j):
                    first_tap(j, 0)
                    first_tap(j, 1)
                    silu(j, 0)
                    gate(j, 0)
                    first_tap(j, 2)
                    silu(j, 1)
                    first_tap(j, 3)
                    silu(j, 2)
                    gate(j, 1)
                    first_tap(j, 4)
                    silu(j, 3)
                    gate(j, 2)
                    silu(j, 4)

                superblock(0)
                with act.Fori(1, N_TOK // SB) as j:
                    superblock(j)

            @block.vector
            def _(dve):
                nc.vector.scalar_tensor_tensor(mag[:, :], m.dt[:, :], -1.0, m.dt[:, :], ALU.mult, ALU.max).then_inc(mag_done, 1)
                dve.wait_ge(exp_done, 1)
                nc.vector.tensor_scalar(one_ex[:, :], ex[:, :], 1.0, None, ALU.add).then_inc(one_done, 1)
                dve.wait_ge(one_done, 1)
                nc.vector.tensor_scalar(back[:, :], one_ex[:, :], -1.0, None, ALU.add).then_inc(back1, 1)
                dve.wait_ge(back1, 1)
                nc.vector.tensor_tensor(mag[:, :], ex[:, :], back[:, :], ALU.subtract).then_inc(back2, 1)
                dve.wait_ge(back2, 1)
                dve.wait_ge(log_done, 1)
                nc.vector.tensor_tensor(one_ex[:, :], ln1[:, :], mag[:, :], ALU.add).then_inc(back3, 1)
                dve.wait_ge(back3, 1)
                nc.vector.scalar_tensor_tensor(m.dt[:, :], m.dt[:, :], 0.0, one_ex[:, :], ALU.max, ALU.add).then_inc(sp_done, 1)
                dve.wait_ge(sp_done, 1)
                dve.wait_ge(ea_done, 1)
                nc.vector.scalar_tensor_tensor(m.dt_a[:, :].rearrange("p (i h) -> p i h", h=NH), m.dt[:, :].rearrange("p (i h) -> p i h", h=NH), -1.0,
                                               e_a[:, :].unsqueeze(1).to_broadcast([P, TILES, NH]), ALU.mult, ALU.mult).then_inc(a_done, 1)

                def superblock(j):
                    for c in range(5):
                        full = pre[:, c, :].rearrange("p (b t) -> p b t", t=BLK)
                        src = banks[c][:, :].rearrange("p (b t) -> p b t", t=BLK)
                        for back_by in range(1, KC):
                            if back_by == 1:
                                dve.wait_ge(tap3, 5 * j + c + 1)
                            else:
                                dve.wait_ge(taps, 3 * (5 * j + c) + back_by - 1)
                            nc.vector.scalar_tensor_tensor(full[:, :, back_by:], src[:, :, :BLK - back_by], p["conv_w"][:, 4 * c + 3 - back_by:4 * c + 4 - back_by],
                                                           full[:, :, back_by:], ALU.mult, ALU.add).then_inc(taps, 1)

                superblock(0)
                with dve.Fori(1, N_TOK // SB) as j:
                    superblock(j)


def state_space(nc, dram, m, s, ps):
    with ExitStack() as ctx:
        def sb(name, shape, dt=F32):
            return ctx.enter_context(nc.sbuf_tensor(name, shape, dt))

        def sem(name):
            return s.semaphore(name)

        c, p = m.c, m.p
        xb = sb("xbc_tile", [P, 2, 5, P])
        a_upto = sb("dt_a_upto", [P, 2, NH, BLK])
        ex = sb("decays", [P, 2, NH, BLK])
        gm = sb("bc_masked", [P, 2, P])
        mix = sb("mix", [P, 2, NH, 4, BLK])
        xt = sb("x_dt", [P, 2, DI])
        xd = sb("x_skip", [P, 2, 3, P])
        yg = sb("y_gated", [P, 2, 3, P])
        sq = sb("y_squares", [P, 2, 3, P])
        sqs = sb("y_squares_summed", [P, 2, 2, P])
        col = sb("columns", [P, 2, 8])
        st = sb("bn_sums2", [P, 2, 6])
        mv = sb("bn_mean_var2", [P, 2, 2])
        xf = sb("xf_tile", [P, 2, D])
        xft = sb("xf_turned", [HD, 2, 2, P])
        lg = sb("logits", [P, 2, E1])
        top = sb("top8", [P, 2, 8])
        ix = sb("top8_index", [P, 2, 8], U32)
        ps_d = ps[:, 0, 0:NH * BLK]
        ps_g = ps[:, 1, 0:P]
        ps_x = ps[:, 1, P:P + DI]
        ps_y = [ps[:, 2 + o, 0:DI].rearrange("p (c t) -> p c t", c=3) for o in range(2)]
        ps_o = [ps[:, 4 + o, 0:D] for o in range(2)]
        ps_q = [ps[:, 4 + o, D:D + 1] for o in range(2)]
        ps_u = ps[0:HD, 6, 0:256].rearrange("p (c t) -> p c t", c=2)
        ps_l = ps[:, 7, 0:E1]

        xb_in = [sem("xbc_in_even"), sem("xbc_in_odd")]
        (wo_ready, upto_done, d_mm, gx_mm, exp_done, g_done, x_done, mix_done, y_mm, xd_done, skip_done, gate_done, sq_done, sum2, sum3, q_mm, ms_done, rms_done,
         o_mm, h_done, sums, mean_var, eps_done, rstd_done, xf_done, u_mm, u_out, l_mm, l_out, top_done, ix_done, kept, picked) = (sem(n) for n in (
            "w_out_scaled", "dt_a_spread", "decay_sums", "bc_and_x_turned", "decays_ready", "bc_masked_ready", "x_dt_ready", "mix_ready", "y_product",
            "skip_ready", "skip_added", "y_gated_ready", "squares_ready", "two_squares_summed", "squares_summed", "mean_square_product", "mean_square_ready", "rms_ready", "y_out_product", "h2_ready", "sums3", "mean_var3", "var_eps3",
            "rstd3", "xf_ready", "xf_turned_mm", "xf_turned_out", "logit_product", "logits_out", "top_ready", "index_ready", "top_kept", "index_kept"))
        row_sent = [sem("xf_sent_even"), sem("xf_sent_odd")]

        def row(t, i):
            return t[:, bass.ds(i, 1), :].rearrange("p a d -> p (a d)")

        with nc.Block() as block:
            @block.sync
            def _(sp):
                def copy_tile(t):
                    need(sp, gx_mm, t.i - 1)
                    sp.dma_start(xb[:, t.odd, :, :], s.xbc[:, :, bass.ds(t.i * P, P)]).then_inc(xb_in[t.odd], 16)

                def store(t):
                    sp.wait_ge(xf_done, t.i + 1)
                    sp.dma_start(dram["x1"][bass.ds(t.i * P, P), :], xf[:, t.odd, :]).then_inc(row_sent[t.odd], 16)

                pipelined(sp, TILES, [(8, store), (0, copy_tile)], 12)
                for sent in row_sent:
                    sp.wait_ge(sent, 16 * TILES // 2)

            @block.tensor
            def _(pe):
                pe.wait_ge(wo_ready, 3)
                pe.wait_ge(m.w_gate_loaded, 16)

                def decay_and_bc(t):
                    pe.wait_ge(upto_done, t.i + 1)
                    need(pe, exp_done, t.i)
                    nc.tensor.matmul(ps_d, c["after"], a_upto[:, t.odd, :, :].rearrange("p h t -> p (h t)"), start=True, stop=True).then_inc(d_mm, 1)
                    pe.wait_ge(xb_in[t.odd], 16 * (t.k + 1))
                    need(pe, g_done, t.i)
                    need(pe, x_done, t.i)
                    nc.tensor.matmul(ps_g, xb[:, t.odd, 3, :], xb[:, t.odd, 4, :], start=True, stop=True)
                    for ch in range(3):
                        last = nc.tensor.transpose(ps_x[:, ch * P:(ch + 1) * P], xb[:, t.odd, ch, :], c["ident"])
                    last.then_inc(gx_mm, 1)

                def mix_time(t):
                    pe.wait_ge(mix_done, t.i + 1)
                    pe.wait_ge(x_done, t.i + 1)
                    need(pe, skip_done, t.i - 1)
                    for h in range(NH):
                        last = nc.tensor.matmul(ps_y[t.odd][(h % 2) * HP:(h % 2 + 1) * HP, h // 2, :], xt[:, t.odd, h * HP:(h + 1) * HP],
                                                mix[:, t.odd, h, :, :].rearrange("p b t -> p (b t)"), start=True, stop=True)
                    last.then_inc(y_mm, 1)

                def project_out(t):
                    pe.wait_ge(gate_done, t.i + 1)
                    need(pe, h_done, t.i - 1)
                    need(pe, ms_done, t.i - 1)
                    for ch in range(3):
                        last = nc.tensor.matmul(ps_o[t.odd], yg[:, t.odd, ch, :], m.w_out[:, ch, :], start=ch == 0, stop=ch == 2)
                    last.then_inc(o_mm, 1)

                def add_squares(t):
                    pe.wait_ge(sum3, t.i + 1)
                    nc.tensor.matmul(ps_q[t.odd], sqs[:, t.odd, 1, :], c["ones"][:, 0:1], start=True, stop=True).then_inc(q_mm, 1)

                def turn(t):
                    pe.wait_ge(xf_done, t.i + 1)
                    need(pe, u_out, t.i)
                    for ch in range(2):
                        last = nc.tensor.transpose(ps_u[:, ch, :], xf[:, t.odd, ch * HD:(ch + 1) * HD], c["ident"])
                    last.then_inc(u_mm, 1)

                def route(t):
                    pe.wait_ge(u_out, t.i + 1)
                    need(pe, l_out, t.i)
                    for ch in range(2):
                        last = nc.tensor.matmul(ps_l, xft[:, t.odd, ch, :], m.w_gate[:, ch, :], start=ch == 0, stop=ch == 1)
                    last.then_inc(l_mm, 1)

                pipelined(pe, TILES, [(6, add_squares), (3, mix_time), (9, turn), (10, route), (5, project_out), (1, decay_and_bc)], 12)

            @block.scalar
            def _(act):
                act.activation(col[:, 0, 7:8], c["ones"][:, 0:1], ACT.Exp)

                def decays(t):
                    act.wait_ge(d_mm, t.i + 1)
                    need(act, mix_done, t.i - 1)
                    act.activation(ex[:, t.odd, :, :].rearrange("p h t -> p (h t)"), ps_d, ACT.Exp).then_inc(exp_done, 1)

                def skips(t):
                    need(act, gate_done, t.i - 1)
                    for ch in range(3):
                        act.activation(xd[:, t.odd, ch, :], s.xbc[:, ch:ch + 1, bass.ds(t.i * P, P)].rearrange("p a t -> p (a t)"), ACT.Identity, scale=p["skip"][:, ch:ch + 1]).then_inc(xd_done, 1)

                def squares(t):
                    act.wait_ge(gate_done, t.i + 1)
                    need(act, sum3, t.i - 1)
                    act.activation(sq[:, t.odd, :, :], yg[:, t.odd, :, :], ACT.Square).then_inc(sq_done, 1)

                def take_turned(t):
                    act.wait_ge(u_mm, t.i + 1)
                    need(act, l_mm, t.i - 1)
                    act.activation(xft[:, t.odd, :, :], ps_u, ACT.Identity).then_inc(u_out, 1)

                pipelined(act, TILES, [(2, decays), (5, squares), (9, take_turned), (3, skips)], 12)

            @block.vector
            def _(dve):
                dve.wait_ge(m.w_out_loaded, 16)
                for ch in range(3):
                    nc.vector.tensor_scalar(m.w_out[:, ch, :], m.w_out[:, ch, :], p["norm_w"][:, ch:ch + 1], None, ALU.mult).then_inc(wo_ready, 1)

                def mask_bc(t):
                    dve.wait_ge(gx_mm, t.i + 1)
                    nc.vector.tensor_tensor(gm[:, t.odd, :], ps_g, c["upto_all"], ALU.mult).then_inc(g_done, 1)

                def times_dt(t):
                    need(dve, y_mm, t.i - 1)
                    nc.vector.tensor_tensor(xt[:, t.odd, :].rearrange("p (h c) -> p h c", h=NH), ps_x.rearrange("p (h c) -> p h c", h=NH),
                                            m.dt[:, bass.ds(t.i * NH, NH)].unsqueeze(2).to_broadcast([P, NH, HP]), ALU.mult).then_inc(x_done, 1)

                def mixing(t):
                    need(dve, y_mm, t.i - 1)
                    dve.wait_ge(exp_done, t.i + 1)
                    dve.wait_ge(g_done, t.i + 1)
                    wide = [P, NH, 4, BLK]
                    nc.vector.tensor_tensor(mix[:, t.odd, :, :, :], ex[:, t.odd, :, :].unsqueeze(2).to_broadcast(wide),
                                            gm[:, t.odd, :].rearrange("p (b t) -> p b t", b=4).unsqueeze(1).to_broadcast(wide), ALU.mult).then_inc(mix_done, 1)

                def add_skip(t):
                    dve.wait_ge(y_mm, t.i + 1)
                    dve.wait_ge(xd_done, 3 * (t.i + 1))
                    nc.vector.tensor_tensor(xd[:, t.odd, :, :], xd[:, t.odd, :, :], ps_y[t.odd], ALU.add).then_inc(skip_done, 1)

                def gate(t):
                    dve.wait_ge(skip_done, t.i + 1)
                    need(dve, o_mm, t.i - 1)
                    need(dve, sq_done, t.i - 1)
                    nc.vector.tensor_tensor(yg[:, t.odd, :, :], xd[:, t.odd, :, :], s.sz[:, :, bass.ds(t.i * P, P)], ALU.mult).then_inc(gate_done, 1)

                def mean_square(t):
                    dve.wait_ge(q_mm, t.i + 1)
                    need(dve, rms_done, t.i - 1)
                    nc.vector.tensor_scalar(col[:, t.odd, 0:1], ps_q[t.odd], 1.0 / DI, EPS, ALU.mult, ALU.add).then_inc(ms_done, 1)

                def residual(t):
                    dve.wait_ge(rms_done, t.i + 1)
                    need(dve, xf_done, t.i - 1)
                    nc.vector.scalar_tensor_tensor(row(m.h, t.i), ps_o[t.odd], col[:, t.odd, 1:2], row(m.h, t.i), ALU.mult, ALU.add).then_inc(h_done, 1)

                def sum_rows(t):
                    need_alone(dve, m, (h_done, t.i + 1))
                    nc.vector.bn_stats(st[:, t.odd, :], row(m.h, t.i)).then_inc(sums, 1)

                def moments(t):
                    need_alone(dve, m, (sums, t.i + 1))
                    nc.vector.bn_aggr(mv[:, t.odd, :], st[:, t.odd, :]).then_inc(mean_var, 1)

                def norm(t):
                    dve.wait_ge(rstd_done, t.i + 1)
                    need(dve, u_mm, t.i - 1)
                    need(dve, row_sent[t.odd], 16 * t.k)
                    nc.vector.tensor_scalar(xf[:, t.odd, :], row(m.h, t.i), mv[:, t.odd, 0:1], col[:, t.odd, 3:4], ALU.subtract, ALU.mult).then_inc(xf_done, 1)

                def take_logits(t):
                    dve.wait_ge(l_mm, t.i + 1)
                    need(dve, ix_done, t.i - 1)
                    need(dve, kept, t.i - 1)
                    need(dve, picked, t.i - 1)
                    nc.vector.tensor_copy(lg[:, t.odd, :], ps_l).then_inc(l_out, 1)

                def best(t):
                    need_alone(dve, m, (l_out, t.i + 1))
                    nc.vector.max(top[:, t.odd, :], lg[:, t.odd, :]).then_inc(top_done, 1)

                def best_index(t):
                    need_alone(dve, m, (top_done, t.i + 1))
                    nc.vector.max_index(ix[:, t.odd, :], top[:, t.odd, :], lg[:, t.odd, :]).then_inc(ix_done, 1)

                def keep_top(t):
                    nc.vector.tensor_copy(m.top[:, bass.ds(t.i * 2, 2)], top[:, t.odd, 0:2]).then_inc(kept, 1)

                def keep_index(t):
                    dve.wait_ge(ix_done, t.i + 1)
                    nc.vector.tensor_copy(m.pick[:, bass.ds(t.i * 2, 2)], ix[:, t.odd, 0:2]).then_inc(picked, 1)

                pipelined(dve, TILES, [(2, mask_bc), (7, residual), (11, take_logits), (2, times_dt), (6, mean_square), (11, best), (7, sum_rows), (2, mixing),
                                       (11, best_index), (11, keep_top), (7, moments), (4, add_skip), (11, keep_index), (8, norm), (4, gate)], 12)

            @block.gpsimd
            def _(pool):
                def spread(t):
                    need(pool, d_mm, t.i - 1)
                    nc.gpsimd.tensor_tensor(a_upto[:, t.odd, :, :], c["upto"].unsqueeze(1).to_broadcast([P, NH, BLK]),
                                            m.dt_a[:, bass.ds(t.i * NH, NH)].unsqueeze(2).to_broadcast([P, NH, BLK]), ALU.mult).then_inc(upto_done, 1)

                def root_of_mean_square(t):
                    pool.wait_ge(ms_done, t.i + 1)
                    need(pool, h_done, t.i - 1)
                    nc.gpsimd.tensor_tensor(col[:, t.odd, 1:2], col[:, t.odd, 0:1], c["minus_half"], ALU.pow).then_inc(rms_done, 1)

                def root_of_variance(t):
                    pool.wait_ge(mean_var, t.i + 1)
                    need(pool, xf_done, t.i - 1)
                    nc.gpsimd.tensor_tensor(col[:, t.odd, 2:3], mv[:, t.odd, 1:2], c["eps"], ALU.add).then_inc(eps_done, 1)
                    pool.wait_ge(eps_done, t.i + 1)
                    nc.gpsimd.tensor_tensor(col[:, t.odd, 3:4], col[:, t.odd, 2:3], c["minus_half"], ALU.pow).then_inc(rstd_done, 1)

                def sum_squares(t):
                    pool.wait_ge(sq_done, t.i + 1)
                    need(pool, q_mm, t.i - 1)
                    nc.gpsimd.tensor_tensor(sqs[:, t.odd, 0, :], sq[:, t.odd, 0, :], sq[:, t.odd, 1, :], ALU.add).then_inc(sum2, 1)
                    pool.wait_ge(sum2, t.i + 1)
                    nc.gpsimd.tensor_tensor(sqs[:, t.odd, 1, :], sqs[:, t.odd, 0, :], sq[:, t.odd, 2, :], ALU.add).then_inc(sum3, 1)

                pipelined(pool, TILES, [(0, spread), (5, sum_squares), (6, root_of_mean_square), (7, root_of_variance)], 12)


def dispatch(nc, m, banks, tag, n_exp, cols, pick, slot, tile_expert, tile_token, n_tiles, logits_to_gates):
    with ExitStack() as ctx:
        def sb(name, shape, dt=F32):
            return ctx.enter_context(nc.sbuf_tensor(f"{name}_{tag}", shape, dt))

        def sem(name):
            return ctx.enter_context(nc.semaphore(f"{name}_{tag}"))

        c = m.c
        n = n_exp * cols
        one_hot = sb("one_hot", [P, n_exp, cols])
        counts = sb("counts", [P, n_exp, cols + 1])
        run = sb("running", [P, n_exp, cols + 1])
        ones = sb("scan_ones", [P, n_exp * (cols + 1)])
        total = sb("totals", [P, 4, n_exp])
        total_i = sb("totals_int", [P, 2, n_exp], I32)
        place = sb("places", [P, n_exp, cols])
        slot_f = sb("slots", [P, cols])
        ended = sb("ended", [P, n_tiles, n_exp])
        expert_f = sb("tile_experts", [P, n_tiles])
        slot_i = sb("slots_int", [P, 3, cols], I32)
        tile_row = sb("tile_and_row", [P, 2, cols])
        in_tile = sb("in_tile", [P, cols, n_tiles], BF16)
        tile_id = sb("in_tile_times_id", [P, cols, 2, n_tiles], BF16)
        in_row = sb("in_row", [P, cols, P], BF16)
        token_f = sb("tokens", [P, n_tiles])
        chunk = 8
        picked, counted, step, gate_exp, in_tile_set, row_id_set, tile_id_set, in_row_set, tokens_mm = (sem(n) for n in (
            "picked", "counted", "dispatch_step", "gate_exp", "in_tile_set", "row_id_set", "tile_id_set", "in_row_set", "tokens_product"))
        flat = "p e a -> p (e a)"
        ps_before, ps_count = banks[0][:, 0:n], banks[1][:, 0:n]
        ps_token = banks[2][:, 0:2 * n_tiles].rearrange("p (w t) -> p w t", w=2)

        with nc.Block() as block:
            @block.tensor
            def _(pe):
                pe.wait_ge(picked, 1)
                nc.tensor.matmul(ps_before, c["before"], one_hot[:, :, :].rearrange(flat), start=True, stop=True)
                nc.tensor.matmul(ps_count, c["ones"], one_hot[:, :, :].rearrange(flat), start=True, stop=True).then_inc(counted, 1)
                pe.wait_ge(row_id_set, 1)
                pe.wait_ge(tile_id_set, 1)
                for a in range(cols):
                    if a % chunk == 0:
                        pe.wait_ge(in_row_set, a // chunk + 1)
                    last = nc.tensor.matmul(ps_token, in_row[:, a, :], tile_id[:, a, :, :], start=a == 0, stop=a == cols - 1)
                last.then_inc(tokens_mm, 1)

            @block.scalar
            def _(act):
                if logits_to_gates:
                    act.wait_ge(step, 1)
                    act.activation(m.gate[:, :, 1], m.gate[:, :, 1], ACT.Exp).then_inc(gate_exp, 1)
                act.wait_ge(in_tile_set, 1)
                act.activation(tile_id[:, :, 0, :], in_tile[:, :, :], ACT.Identity, scale=c["row_index"]).then_inc(row_id_set, 1)

            @block.vector
            def _(dve):
                done = [0]

                def then(ins):
                    done[0] += 1
                    ins.then_inc(step, 1)
                    dve.wait_ge(step, done[0])

                if logits_to_gates:
                    top = m.top[:, :].rearrange("p (i k) -> p i k", k=2)
                    then(nc.vector.tensor_tensor(m.gate[:, :, 1], top[:, :, 1], top[:, :, 0], ALU.subtract))
                nc.vector.tensor_tensor(one_hot[:, :, :], pick.unsqueeze(1).to_broadcast([P, n_exp, cols]),
                                        c["iota"][:, 0:n_exp].unsqueeze(2).to_broadcast([P, n_exp, cols]), ALU.is_equal).then_inc(picked, 1)
                then(nc.vector.memset(ones[:, :], 1.0))
                dve.wait_ge(counted, 1)
                then(nc.vector.tensor_copy(counts[:, :, 0:cols], ps_count.rearrange("p (e a) -> p e a", e=n_exp)))
                then(nc.vector.reduce_sum(total[:, 0, :], counts[:, :, 0:cols], AX_X))
                then(nc.vector.tensor_scalar(total_i[:, 0, :], total[:, 0, :], float(P - 1), None, ALU.add))
                then(nc.vector.tensor_scalar(total_i[:, 1, :], total_i[:, 0, :], 7, None, ALU.logical_shift_right))
                then(nc.vector.tensor_copy(total[:, 1, :], total_i[:, 1, :]))
                then(nc.vector.scalar_tensor_tensor(counts[:, :, cols], total[:, 1, :], float(P), total[:, 0, :], ALU.mult, ALU.subtract))
                then(nc.vector.tensor_tensor_scan(run[:, :, :].rearrange(flat), ones[:, :], counts[:, :, :].rearrange(flat), 0.0, ALU.mult, ALU.add))
                then(nc.vector.tensor_tensor(place[:, :, :], run[:, :, 0:cols], counts[:, :, 0:cols], ALU.subtract))
                then(nc.vector.tensor_tensor(place[:, :, :], place[:, :, :], ps_before.rearrange("p (e a) -> p e a", e=n_exp), ALU.add))
                then(nc.vector.tensor_tensor(place[:, :, :], place[:, :, :], one_hot[:, :, :], ALU.mult))
                then(nc.vector.reduce_sum(slot_f[:, :], place[:, :, :].rearrange("p e a -> p a e"), AX_X))
                then(nc.vector.tensor_copy(slot_i[:, 0, :], slot_f[:, :]))
                nc.vector.tensor_copy(slot[:, :], slot_f[:, :]).then_inc(step, 1)
                nc.vector.tensor_scalar(slot_i[:, 1, :], slot_i[:, 0, :], 7, None, ALU.logical_shift_right).then_inc(step, 1)
                done[0] += 2
                then(nc.vector.tensor_scalar(slot_i[:, 2, :], slot_i[:, 0, :], P - 1, None, ALU.bitwise_and))
                then(nc.vector.tensor_copy(tile_row[:, :, :], slot_i[:, 1:3, :]))
                nc.vector.tensor_tensor(in_tile[:, :, :], tile_row[:, 0, :].unsqueeze(2).to_broadcast([P, cols, n_tiles]),
                                        c["iota"][:, 0:n_tiles].unsqueeze(1).to_broadcast([P, cols, n_tiles]), ALU.is_equal).then_inc(in_tile_set, 1)

                def mark_rows(a):
                    nc.vector.tensor_tensor(in_row[:, a:a + chunk, :], tile_row[:, 1, a:a + chunk].unsqueeze(2).to_broadcast([P, chunk, P]),
                                            c["iota"].unsqueeze(1).to_broadcast([P, chunk, P]), ALU.is_equal).then_inc(in_row_set, 1)

                mark_rows(0)
                dve.wait_ge(in_tile_set, 1)
                per_token = cols // TILES
                nc.vector.tensor_tensor(tile_id[:, :, 1, :].rearrange("p (i k) t -> p i k t", k=per_token),
                                        in_tile[:, :, :].rearrange("p (i k) t -> p i k t", k=per_token),
                                        c["iota"][:, 0:TILES].unsqueeze(2).unsqueeze(3).to_broadcast([P, TILES, per_token, n_tiles]), ALU.mult).then_inc(tile_id_set, 1)
                for a in range(chunk, cols, chunk):
                    mark_rows(a)
                then(nc.vector.tensor_scalar(total[:, 2, :], run[:, :, cols], 1.0 / P, None, ALU.mult))
                then(nc.vector.tensor_tensor(ended[:, :, :], c["iota"][:, 0:n_tiles].unsqueeze(2).to_broadcast([P, n_tiles, n_exp]),
                                             total[:, 2, :].unsqueeze(1).to_broadcast([P, n_tiles, n_exp]), ALU.is_ge))
                then(nc.vector.reduce_sum(expert_f[:, :], ended[:, :, :], AX_X))
                then(nc.vector.tensor_scalar(expert_f[:, :], expert_f[:, :], float(n_exp - 1), None, ALU.min))
                then(nc.vector.tensor_copy(tile_expert[:, :], expert_f[:, :]))
                dve.wait_ge(tokens_mm, 1)
                then(nc.vector.tensor_copy(token_f[:, :], ps_token[:, 0, :]))
                then(nc.vector.scalar_tensor_tensor(token_f[:, :], ps_token[:, 1, :], float(P), token_f[:, :], ALU.mult, ALU.add))
                then(nc.vector.tensor_copy(tile_token[:, :], token_f[:, :]))
                if logits_to_gates:
                    dve.wait_ge(gate_exp, 1)
                    then(nc.vector.tensor_scalar(m.gate[:, :, 0], m.gate[:, :, 1], 1.0, None, ALU.add))
                    then(nc.vector.reciprocal(m.gate[:, :, 0], m.gate[:, :, 0]))
                    then(nc.vector.tensor_tensor(m.gate[:, :, 1], m.gate[:, :, 1], m.gate[:, :, 0], ALU.mult))


def experts(nc, m, ps, tag, n_exp, n_tiles, tile_expert, tile_token, src, dst, w_up, w_down, b_down, gelu, weights_in):
    kx = w_up.shape[0]
    with ExitStack() as ctx:
        def sb(name, shape, dt=F32):
            return ctx.enter_context(nc.sbuf_tensor(f"{name}_{tag}", shape, dt))

        def sem(name):
            return ctx.enter_context(nc.semaphore(f"{name}_{tag}"))

        c = m.c
        x = sb("rows_in", [P, 2, D])
        xt = sb("rows_turned", [kx, 2, 2, P])
        hid = sb("hidden", [P, 2, 2, HID // 2])
        ht = sb("hidden_turned", [P, 2, HC, P])
        y = sb("rows_out", [P, 2, D])
        x_in = [sem("rows_in_even"), sem("rows_in_odd")]
        y_sent = [sem("rows_sent_even"), sem("rows_sent_odd")]
        x_mm, x_out, up_mm, act_done, t_mm, t_out, down_mm, y_out, ones_set = (sem(n) for n in (
            "rows_turned_mm", "rows_turned_out", "up_product", "gelu_ready", "hidden_turned_mm", "hidden_turned_out", "down_product", "rows_ready", "ones_set"))
        ps_x = ps[0:HD, 0, 0:256].rearrange("p (c t) -> p c t", c=2)
        ps_h = [ps[:, 1:3, 0:HID // 2], ps[:, 6:8, 0:HID // 2]]
        ps_t = [ps[:, 3, :], ps[:, 4, 0:256]]
        ps_y = ps[:, 5, 0:D]

        def rows(t, i):
            return t[bass.ds(i * P, P), :]

        with nc.Block() as block:
            @block.sync
            def _(sp):
                def store(t):
                    sp.wait_ge(y_out, t.i + 1)
                    sp.dma_start(rows(dst, t.i), y[:, t.odd, :]).then_inc(y_sent[t.odd], 16)

                pipelined(sp, n_tiles, [(4, store)], 5)
                sp.wait_ge(y_sent[0], 16 * ((n_tiles + 1) // 2))
                sp.wait_ge(y_sent[1], 16 * (n_tiles // 2))

            @block.gpsimd
            def _(pool):
                def gather(t):
                    need(pool, x_mm, t.i - 1)
                    nc.gpsimd.indirect_dma_start(out=x[:, t.odd, :], out_offset=None, in_=src,
                                                 in_offset=bass.IndirectOffsetOnAxis(ap=tile_token[:, t.i:t.i + 1], axis=0)).then_inc(x_in[t.odd], 16)

                pipelined(pool, n_tiles, [(0, gather)], 1, straight=True)

            @block.tensor
            def _(pe):
                for s, value in weights_in:
                    pe.wait_ge(s, value)
                if kx > HD:
                    pe.wait_ge(ones_set, 1)

                def turn_rows(t):
                    pe.wait_ge(x_in[t.odd], 16 * (t.k + 1))
                    need(pe, x_out, t.i)
                    for ch in range(2):
                        last = nc.tensor.transpose(ps_x[:, ch, :], x[:, t.odd, ch * HD:(ch + 1) * HD], c["ident"])
                    last.then_inc(x_mm, 1)

                def expert_of(t):
                    return pe.value_load(tile_expert[0:1, bass.ds(t.i, 1)], min_val=0, max_val=n_exp - 1)

                def up(t):
                    e = expert_of(t)
                    pe.wait_ge(x_out, t.i + 1)
                    need(pe, act_done, t.i - 1)
                    for half in range(2):
                        for ch in range(2):
                            k = kx if ch == 0 else HD
                            last = nc.tensor.matmul(ps_h[t.odd][:, half, :], xt[0:k, t.odd, ch, :], w_up[0:k, bass.ds((e * 2 + ch) * HID + half * (HID // 2), HID // 2)],
                                                    start=ch == 0, stop=ch == 1)
                    last.then_inc(up_mm, 1)

                def turn_hidden(t):
                    pe.wait_ge(act_done, t.i + 1)
                    need(pe, t_out, 2 * t.i)
                    for ch in range(HC):
                        half, at = ch // 3, ch % 3
                        last = nc.tensor.transpose(ps_t[ch // 4][:, (ch % 4) * P:(ch % 4 + 1) * P], hid[:, t.odd, half, at * P:(at + 1) * P], c["ident"])
                        if ch in (3, 5):
                            last.then_inc(t_mm, 1)

                def down(t):
                    e = expert_of(t)
                    pe.wait_ge(t_out, 2 * (t.i + 1))
                    need(pe, y_out, t.i)
                    if b_down is not None:
                        nc.tensor.matmul(ps_y, c["ones"][0:1, :], b_down[0:1, bass.ds(e * D, D)], start=True, stop=False)
                    for ch in range(HC):
                        last = nc.tensor.matmul(ps_y, ht[:, t.odd, ch, :], w_down[:, bass.ds((e * HC + ch) * D, D)], start=ch == 0 and b_down is None, stop=ch == HC - 1)
                    last.then_inc(down_mm, 1)

                pipelined(pe, n_tiles, [(4, down), (3, turn_hidden), (2, up), (1, turn_rows)], 5)

            @block.scalar
            def _(act):
                act.activation(y[:, 0, 0:1], c["ones"][:, 0:1], gelu).then_inc(m.tables, 1)

                def take_rows(t):
                    act.wait_ge(x_mm, t.i + 1)
                    need(act, up_mm, t.i - 1)
                    act.activation(xt[0:HD, t.odd, :, :], ps_x, ACT.Identity).then_inc(x_out, 1)

                def activate(t):
                    act.wait_ge(up_mm, t.i + 1)
                    need(act, t_mm, 2 * (t.i - 1))
                    act.activation(hid[:, t.odd, :, :], ps_h[t.odd], gelu).then_inc(act_done, 1)

                pipelined(act, n_tiles, [(2, activate), (1, take_rows)], 5)

            @block.vector
            def _(dve):
                dve.wait_ge(m.tables, tag)
                if kx > HD:
                    nc.vector.memset(xt[HD:kx, :, :, :], 1.0).then_inc(ones_set, 1)

                def take_hidden(t):
                    need(dve, down_mm, t.i - 1)
                    dve.wait_ge(t_mm, 2 * t.i + 1)
                    nc.vector.tensor_copy(ht[:, t.odd, 0:4, :], ps_t[0]).then_inc(t_out, 1)
                    dve.wait_ge(t_mm, 2 * t.i + 2)
                    nc.vector.tensor_copy(ht[:, t.odd, 4:6, :], ps_t[1]).then_inc(t_out, 1)

                def take_rows(t):
                    need(dve, y_sent[t.odd], 16 * t.k)
                    dve.wait_ge(down_mm, t.i + 1)
                    nc.vector.tensor_copy(y[:, t.odd, :], ps_y).then_inc(y_out, 1)

                pipelined(dve, n_tiles, [(4, take_rows), (3, take_hidden)], 5)


def linear_attention(nc, dram, m, ps):
    with ExitStack() as ctx:
        def sb(name, shape, dt=F32):
            return ctx.enter_context(nc.sbuf_tensor(name, shape, dt))

        def sem(name):
            return ctx.enter_context(nc.semaphore(name))

        c, p = m.c, m.p
        gate = sb("gate_tile", [P, 2, 2])
        y = sb("expert_rows", [P, 2, 2, D])
        st = sb("bn_sums4", [P, 2, 2, 6])
        mv = sb("bn_mean_var4", [P, 2, 2, 2])
        col = sb("columns4", [P, 2, 4])
        xn = sb("xn", [P, 2, 2, D])
        xt = sb("xn_turned", [HD, 2, 2, 2, P])
        qk = sb("qk_turned", [HD, 2, 4, P])
        v = sb("v_rows", [P, 2, D])
        w = sb("weights_t", [P, 2, P])
        ps_t = [ps[0:HD, b, 0:256].rearrange("p (c t) -> p c t", c=2) for b in (0, 5)]
        ps_qk = ps[0:HD, 1, :].rearrange("p (n t) -> p n t", n=4)
        ps_v, ps_s, ps_o, ps_l = ps[:, 2, 0:D], ps[:, 3, 0:P], ps[:, 4, 0:D], ps[:, 6, 0:E2]

        y_in = [sem("expert_rows_even"), sem("expert_rows_odd")]
        row_sent = [sem("xn_b_sent_even"), sem("xn_b_sent_odd")]
        (gate_set, first_added, h3, sums_a, mv_a, eps_a, rstd_a, xn_a, t_mm_a, t_out_a, qk_mm, v_mm, qk_out, v_out, s_mm, w_out, o_mm, h4,
         sums_b, mv_b, eps_b, rstd_b, xn_b, t_mm_b, t_out_b, l_mm, l_out) = (sem(n) for n in (
            "gate_set", "first_expert_added", "h3_ready", "sums_a", "mean_var_a", "var_eps_a", "rstd_a", "xn_a_ready", "turned_a_mm",
            "turned_a_out", "qk2_product", "v2_product", "qk2_out", "v2_out", "score2_product", "weights_ready", "attended2", "h4_ready", "sums_b",
            "mean_var_b", "var_eps_b", "rstd_b", "xn_b_ready", "turned_b_mm", "turned_b_out", "logit2_product", "logits2_out"))

        def row(t, i):
            return t[:, bass.ds(i, 1), :].rearrange("p a d -> p (a d)")

        with nc.Block() as block:
            @block.sync
            def _(sp):
                def store(t):
                    sp.wait_ge(xn_b, t.i + 1)
                    sp.dma_start(dram["x2"][bass.ds(t.i * P, P), :], xn[:, t.odd, 1, :]).then_inc(row_sent[t.odd], 16)

                pipelined(sp, TILES, [(9, store)], 12)
                for sent in row_sent:
                    sp.wait_ge(sent, 16 * TILES // 2)

            @block.gpsimd
            def _(pool):
                def gather(t):
                    need(pool, h3, t.i - 1)
                    for k in range(2):
                        nc.gpsimd.indirect_dma_start(out=y[:, t.odd, k, :], out_offset=None, in_=dram["y1"],
                                                     in_offset=bass.IndirectOffsetOnAxis(ap=m.slot1[:, 2 * t.i + k:2 * t.i + k + 1], axis=0)).then_inc(y_in[t.odd], 16)

                def root(t, n, known, eps_done, done, used):
                    pool.wait_ge(known, t.i + 1)
                    need(pool, used, t.i - 1)
                    nc.gpsimd.tensor_tensor(col[:, t.odd, 2 * n:2 * n + 1], mv[:, t.odd, n, 1:2], c["eps"], ALU.add).then_inc(eps_done, 1)
                    pool.wait_ge(eps_done, t.i + 1)
                    nc.gpsimd.tensor_tensor(col[:, t.odd, 2 * n + 1:2 * n + 2], col[:, t.odd, 2 * n:2 * n + 1], c["minus_half"], ALU.pow).then_inc(done, 1)

                def root_a(t):
                    root(t, 0, mv_a, eps_a, rstd_a, xn_a)

                def root_b(t):
                    root(t, 1, mv_b, eps_b, rstd_b, xn_b)

                pipelined(pool, TILES, [(0, gather), (2, root_a), (8, root_b)], 12, straight=True)

            @block.vector
            def _(dve):
                def set_gate(t):
                    need(dve, h3, t.i - 1)
                    nc.vector.tensor_copy(gate[:, t.odd, :], m.gate[:, bass.ds(t.i, 1), :].rearrange("p a k -> p (a k)")).then_inc(gate_set, 1)

                def add_first(t):
                    dve.wait_ge(y_in[t.odd], 32 * (t.k + 1))
                    dve.wait_ge(gate_set, t.i + 1)
                    nc.vector.scalar_tensor_tensor(row(m.h, t.i), y[:, t.odd, 0, :], gate[:, t.odd, 0:1], row(m.h, t.i), ALU.mult, ALU.add).then_inc(first_added, 1)

                def add_second(t):
                    dve.wait_ge(first_added, t.i + 1)
                    nc.vector.scalar_tensor_tensor(row(m.h, t.i), y[:, t.odd, 1, :], gate[:, t.odd, 1:2], row(m.h, t.i), ALU.mult, ALU.add).then_inc(h3, 1)

                def sum_a(t):
                    need_alone(dve, m, (h3, t.i + 1))
                    nc.vector.bn_stats(st[:, t.odd, 0, :], row(m.h, t.i)).then_inc(sums_a, 1)

                def moments_a(t):
                    need_alone(dve, m, (sums_a, t.i + 1))
                    nc.vector.bn_aggr(mv[:, t.odd, 0, :], st[:, t.odd, 0, :]).then_inc(mv_a, 1)

                def norm_a(t):
                    dve.wait_ge(rstd_a, t.i + 1)
                    need(dve, t_mm_a, t.i - 1)
                    nc.vector.tensor_scalar(xn[:, t.odd, 0, :], row(m.h, t.i), mv[:, t.odd, 0, 0:1], col[:, t.odd, 1:2], ALU.subtract, ALU.mult).then_inc(xn_a, 1)

                def take_qkv(t):
                    dve.wait_ge(qk_mm, t.i + 1)
                    need(dve, s_mm, t.i - 1)
                    nc.vector.tensor_tensor(qk[:, t.odd, :, :], ps_qk, p["b_qk"][0:HD, :].unsqueeze(2).to_broadcast([HD, 4, P]), ALU.add).then_inc(qk_out, 1)
                    dve.wait_ge(v_mm, t.i + 1)
                    need(dve, o_mm, t.i - 1)
                    nc.vector.tensor_tensor(v[:, t.odd, :], ps_v, p["b_v"], ALU.add).then_inc(v_out, 1)

                def decay(t):
                    dve.wait_ge(s_mm, t.i + 1)
                    need(dve, o_mm, t.i - 1)
                    nc.vector.tensor_tensor(w[:, t.odd, :], ps_s, c["decay"], ALU.mult).then_inc(w_out, 1)

                def residual(t):
                    dve.wait_ge(o_mm, t.i + 1)
                    need(dve, xn_b, t.i - 1)
                    nc.vector.tensor_tensor(row(m.h, t.i), row(m.h, t.i), ps_o, ALU.add).then_inc(h4, 1)

                def sum_b(t):
                    need_alone(dve, m, (h4, t.i + 1))
                    nc.vector.bn_stats(st[:, t.odd, 1, :], row(m.h, t.i)).then_inc(sums_b, 1)

                def moments_b(t):
                    need_alone(dve, m, (sums_b, t.i + 1))
                    nc.vector.bn_aggr(mv[:, t.odd, 1, :], st[:, t.odd, 1, :]).then_inc(mv_b, 1)

                def norm_b(t):
                    dve.wait_ge(rstd_b, t.i + 1)
                    need(dve, t_mm_b, t.i - 1)
                    need(dve, row_sent[t.odd], 16 * t.k)
                    nc.vector.tensor_scalar(xn[:, t.odd, 1, :], row(m.h, t.i), mv[:, t.odd, 1, 0:1], col[:, t.odd, 3:4], ALU.subtract, ALU.mult).then_inc(xn_b, 1)

                def take_logits(t):
                    dve.wait_ge(l_mm, t.i + 1)
                    nc.vector.tensor_copy(m.logits2[:, bass.ds(t.i * E2, E2)], ps_l).then_inc(l_out, 1)

                pipelined(dve, TILES, [(2, add_first), (6, take_qkv), (2, add_second), (7, decay), (2, sum_a), (8, residual), (2, moments_a),
                                       (3, norm_a), (8, sum_b), (9, norm_b), (8, moments_b), (11, take_logits), (1, set_gate)], 12)

            @block.scalar
            def _(act):
                def take_a(t):
                    act.wait_ge(t_mm_a, t.i + 1)
                    need(act, v_mm, t.i - 1)
                    act.activation(xt[:, t.odd, 0, :, :], ps_t[0], ACT.Identity).then_inc(t_out_a, 1)

                def take_b(t):
                    act.wait_ge(t_mm_b, t.i + 1)
                    need(act, l_mm, t.i - 1)
                    act.activation(xt[:, t.odd, 1, :, :], ps_t[1], ACT.Identity).then_inc(t_out_b, 1)

                pipelined(act, TILES, [(4, take_a), (10, take_b)], 12)

            @block.tensor
            def _(pe):
                pe.wait_ge(m.w_qkv_loaded, 16)
                pe.wait_ge(m.wg_loaded, 16)

                def turn(t, n, ready, freed, done):
                    pe.wait_ge(ready, t.i + 1)
                    need(pe, freed, t.i)
                    for ch in range(2):
                        last = nc.tensor.transpose(ps_t[n][:, ch, :], xn[:, t.odd, n, ch * HD:(ch + 1) * HD], c["ident"])
                    last.then_inc(done, 1)

                def turn_a(t):
                    turn(t, 0, xn_a, t_out_a, t_mm_a)

                def turn_b(t):
                    turn(t, 1, xn_b, t_out_b, t_mm_b)

                def project(t):
                    pe.wait_ge(t_out_a, t.i + 1)
                    need(pe, qk_out, t.i)
                    for n in range(4):
                        for ch in range(2):
                            last = nc.tensor.matmul(ps_qk[:, n, :], m.w_qkv[:, ch, n * HD:(n + 1) * HD], xt[:, t.odd, 0, ch, :], start=ch == 0, stop=ch == 1)
                    last.then_inc(qk_mm, 1)
                    need(pe, v_out, t.i)
                    for ch in range(2):
                        last = nc.tensor.matmul(ps_v, xt[:, t.odd, 0, ch, :], m.w_qkv[:, ch, 2 * D:3 * D], start=ch == 0, stop=ch == 1)
                    last.then_inc(v_mm, 1)

                def score(t):
                    pe.wait_ge(qk_out, t.i + 1)
                    need(pe, w_out, t.i)
                    for ch in range(2):
                        last = nc.tensor.matmul(ps_s, qk[:, t.odd, 2 + ch, :], qk[:, t.odd, ch, :], start=ch == 0, stop=ch == 1)
                    last.then_inc(s_mm, 1)

                def attend(t):
                    pe.wait_ge(w_out, t.i + 1)
                    pe.wait_ge(v_out, t.i + 1)
                    need(pe, h4, t.i)
                    nc.tensor.matmul(ps_o, w[:, t.odd, :], v[:, t.odd, :], start=True, stop=True).then_inc(o_mm, 1)

                def route(t):
                    pe.wait_ge(t_out_b, t.i + 1)
                    need(pe, l_out, t.i)
                    for ch in range(2):
                        last = nc.tensor.matmul(ps_l, xt[:, t.odd, 1, ch, :], m.wg[:, ch, :], start=ch == 0, stop=ch == 1)
                    last.then_inc(l_mm, 1)

                pipelined(pe, TILES, [(7, score), (8, attend), (4, turn_a), (10, turn_b), (11, route), (5, project)], 12)


def choose_one(nc, m, banks):
    with ExitStack() as ctx:
        def sb(name, shape, dt=F32):
            return ctx.enter_context(nc.sbuf_tensor(name, shape, dt))

        z = sb("seq_logits", [P, TILES, E2])
        e = sb("seq_exp", [P, TILES, E2])
        best = sb("seq_best", [P, TILES])
        mean_mm = ctx.enter_context(nc.semaphore("logits_averaged"))
        exp_done = ctx.enter_context(nc.semaphore("seq_exp_ready"))
        step = ctx.enter_context(nc.semaphore("choice_step"))
        wide = [P, TILES, E2]
        with nc.Block() as block:
            @block.tensor
            def _(pe):
                nc.tensor.matmul(banks[0][:, 0:TILES * E2], m.c["seq_mean"], m.logits2[:, :], start=True, stop=True).then_inc(mean_mm, 1)

            @block.scalar
            def _(act):
                act.wait_ge(step, 3)
                act.activation(e[:, :, :], e[:, :, :], ACT.Exp).then_inc(exp_done, 1)

            @block.vector
            def _(dve):
                done = [0]

                def then(ins):
                    done[0] += 1
                    ins.then_inc(step, 1)
                    dve.wait_ge(step, done[0])

                dve.wait_ge(mean_mm, 1)
                then(nc.vector.tensor_copy(z[:, :, :].rearrange("p i e -> p (i e)"), banks[0][:, 0:TILES * E2]))
                then(nc.vector.reduce_max(best[:, :], z[:, :, :], AX_X))
                then(nc.vector.tensor_tensor(e[:, :, :], z[:, :, :], best[:, :].unsqueeze(2).to_broadcast(wide), ALU.subtract))
                then(nc.vector.tensor_tensor(z[:, :, :], z[:, :, :], best[:, :].unsqueeze(2).to_broadcast(wide), ALU.is_equal))
                then(nc.vector.scalar_tensor_tensor(z[:, :, :], z[:, :, :], -float(E2), m.c["iota"][:, 0:E2].unsqueeze(1).to_broadcast(wide), ALU.mult, ALU.add))
                then(nc.vector.tensor_reduce(best[:, :], z[:, :, :], AX_X, ALU.min))
                then(nc.vector.tensor_scalar(m.pick2[:, :], best[:, :], float(E2), None, ALU.add))
                dve.wait_ge(exp_done, 1)
                then(nc.vector.reduce_sum(best[:, :], e[:, :, :], AX_X))
                then(nc.vector.reciprocal(m.score2[:, :], best[:, :]))


def finish(nc, dram, m):
    deep = 4
    with ExitStack() as ctx:
        y = ctx.enter_context(nc.sbuf_tensor("expert_rows_last", [P, deep, D], F32))
        o = ctx.enter_context(nc.sbuf_tensor("out_rows", [P, deep, D], F32))
        added = ctx.enter_context(nc.semaphore("out_ready"))
        y_in = [ctx.enter_context(nc.semaphore(f"expert_rows_last_{n}")) for n in range(deep)]
        sent = [ctx.enter_context(nc.semaphore(f"out_sent_{n}")) for n in range(deep)]
        with nc.Block() as block:
            @block.gpsimd
            def _(pool):
                for i in range(TILES):
                    need(pool, added, i - deep + 1)
                    nc.gpsimd.indirect_dma_start(out=y[:, i % deep, :], out_offset=None, in_=dram["y2"],
                                                 in_offset=bass.IndirectOffsetOnAxis(ap=m.slot2[:, i:i + 1], axis=0)).then_inc(y_in[i % deep], 16)

            @block.vector
            def _(dve):
                for i in range(TILES):
                    dve.wait_ge(y_in[i % deep], 16 * (i // deep + 1))
                    need(dve, sent[i % deep], 16 * (i // deep))
                    nc.vector.scalar_tensor_tensor(o[:, i % deep, :], y[:, i % deep, :], m.score2[:, i:i + 1], m.h[:, i, :], ALU.mult, ALU.add).then_inc(added, 1)

            @block.sync
            def _(sp):
                for i in range(TILES):
                    sp.wait_ge(added, i + 1)
                    sp.dma_start(dram["out"][i * P:(i + 1) * P, :], o[:, i % deep, :]).then_inc(sent[i % deep], 16)
                for n in range(deep):
                    sp.wait_ge(sent[n], 16 * TILES // deep)


def host_layout(v):
    def chunks(a, n):
        a = np.asarray(a).reshape(n, -1).T
        return np.concatenate([a, np.zeros((P - a.shape[0], n), a.dtype)]) if a.shape[0] < P else a

    wkv = v["L0_tok_Wkv"]
    rows = {
        "bq": np.tile(v["L0_tok_bq"], 16)[:, None], "bkv": np.tile(v["L0_tok_bkv"], 16)[:, None],
        "ln_w": chunks(v["L0_attn_ln_w"], 2), "ln_b": chunks(v["L0_attn_ln_b"], 2),
        "conv_w": v["L0_attn_conv_w"].reshape(5, P, KC).transpose(1, 0, 2).reshape(P, 20),
        "conv_b": chunks(v["L0_attn_conv_b"], 5), "skip": chunks(np.repeat(v["L0_attn_D"], HP), 3),
        "norm_w": chunks(v["L0_attn_norm_w"], 3), "b_qk": chunks(v["L1_attn_b_qkv"][:2 * D], 4),
        "A_log": np.tile(v["L0_attn_A_log"], (P, 1)), "dt_bias": np.tile(v["L0_attn_dt_bias"], (P, 1)),
        "bq_row": np.tile(v["L0_tok_bq"], (P, 16)), "b_v": np.tile(v["L1_attn_b_qkv"][2 * D:], (P, 1)),
        "wq": np.tile(v["L0_tok_Wq"].T, (8, 8)), "wk": np.tile(wkv[:8].T, (8, 8)), "wv": np.tile(wkv[8:].T, (8, 8)),
    }
    return {
        "x": v["x"].reshape(2 * N_TOK, D),
        "param": np.concatenate([rows[n] for n, _ in PARAMS], axis=1),
        "const": constant_table()[0],
        "w_in": v["L0_attn_W_in"],
        "w_out": v["L0_attn_W_out"],
        "w_fc": v["L0_ffn_w_fc"].reshape(2, HD, HID, E1).transpose(1, 3, 0, 2).reshape(HD, E1 * 2 * HID),
        "w_proj": v["L0_ffn_w_proj"].reshape(HC, P, D, E1).transpose(1, 3, 0, 2).reshape(P, E1 * HC * D),
        "w_gate": v["L0_ffn_w_gate"],
        "w_qkv": v["L1_attn_W_qkv"],
        "wg": v["L1_ffn_Wg"].T,
        "w1": np.concatenate([v["L1_ffn_W1"].reshape(E2, 2, HD, HID).transpose(2, 0, 1, 3).reshape(HD, E2 * 2 * HID),
                              np.stack([v["L1_ffn_b1"], np.zeros_like(v["L1_ffn_b1"])], axis=1).reshape(1, E2 * 2 * HID)]),
        "w2": v["L1_ffn_W2"].reshape(E2, HC, P, D).transpose(2, 0, 1, 3).reshape(P, E2 * HC * D),
        "b2": v["L1_ffn_b2"].reshape(1, E2 * D),
    }


OUTPUTS = {"out": (N_TOK, D)}
DEBUG = {}
SCRATCH = {"x1": (N_TOK, D), "y1": (T1 * P, D), "x2": (N_TOK, D), "y2": (T2 * P, D)}


def kernel(**inputs):
    import concourse.bacc as bacc
    from concourse.bass_utils import run_bass_kernel_spmd

    arrays = {n: np.ascontiguousarray(a) for n, a in host_layout({n: np.asarray(a) for n, a in inputs.items()}).items()}
    nc = bacc.Bacc("TRN2", target_bir_lowering=False, num_devices=1)
    dram = {n: nc.dram_tensor("in_" + n, a.shape, F32, kind="ExternalInput").ap() for n, a in arrays.items()}
    for n, shape in {**OUTPUTS, **DEBUG}.items():
        dram[n] = nc.dram_tensor(n, shape, F32, kind="ExternalOutput").ap()
    for n, shape in SCRATCH.items():
        dram[n] = nc.dram_tensor(n, shape, F32, kind="Internal").ap()
    build(nc, dram)
    got = run_bass_kernel_spmd(nc, [{"in_" + n: a for n, a in arrays.items()}], core_ids=[0]).results[0]
    return got["out"].reshape(64, BLK, D)
```

```python
from contextlib import ExitStack

import concourse.bass as bass
import numpy as np
from concourse import mybir

F32 = mybir.dt.float32
BF16 = mybir.dt.bfloat16
F32R = mybir.dt.float32r
I32 = mybir.dt.int32
U32 = mybir.dt.uint32
ALU = mybir.AluOpType
ACT = mybir.ActivationFunctionType
AX_X = mybir.AxisListType.X

P = 128
BLK = 32
D = 192
HD = 96
N_TOK = 2048
TILES = N_TOK // P
FR, FR2 = 16, 8
NH, HP = 6, 64
DI = NH * HP
DS = 128
CONV = DI + 2 * DS
KC = 4
NIN = 2 * DI + 2 * DS + NH
SB = 512
HID = 768
HC = HID // P
E1, E2 = 8, 3
T1 = (2 * N_TOK + E1 * (P - 1)) // P
T2 = (N_TOK + E2 * (P - BLK)) // P
EPS = 1e-5
SC = float(1.0 / np.sqrt(np.float32(D)))


def constant_table():
    p = np.arange(P)
    same32 = p[:, None] // BLK == p[None, :] // BLK
    diff = p[None, :] - p[:, None]
    decay = np.where(same32 & (diff >= 0), np.float32(0.99) ** np.maximum(diff, 0).astype(np.float32), 0) / np.sqrt(np.float32(D))
    parts = {
        "ident": np.eye(P),
        "group_bar": np.where(p[:, None] // FR2 == p[None, :] // FR2, 0.0, -1e30),
        "frame_sel": np.tile((p[:, None] // FR == np.arange(64)[None, :] // FR2), (1, 3)),
        "after": same32 & (p[:, None] > p[None, :]),
        "upto_all": same32 & (p[:, None] <= p[None, :]),
        "upto": (p[:, None] % BLK) <= np.arange(BLK)[None, :],
        "before": p[:, None] < p[None, :],
        "ones": np.ones((P, P)),
        "decay": decay,
        "seq_mean": same32 / float(BLK),
        "iota": np.tile(p[None, :], (P, 1)),
        "row_index": p[:, None],
        "minus_half": np.full((P, 1), -0.5),
        "eps": np.full((P, 1), EPS),
    }
    at, n = {}, 0
    for name, a in parts.items():
        at[name] = (n, a.shape[1])
        n += a.shape[1]
    return np.concatenate([a.astype(np.float32) for a in parts.values()], axis=1), at


PARAMS = [("bq", 1), ("bkv", 1), ("ln_w", 2), ("ln_b", 2), ("conv_w", 20), ("conv_b", 5), ("skip", 3), ("norm_w", 3),
          ("b_qk", 4), ("A_log", NH), ("dt_bias", NH), ("bq_row", P), ("b_v", D), ("wq", 64), ("wk", 64), ("wv", 64)]


def param_places():
    at, n = {}, 0
    for name, w in PARAMS:
        at[name] = (n, w)
        n += w
    return at, n


class Tile:
    def __init__(self, k, odd):
        self.k, self.odd, self.i = k, odd, k * 2 + odd


def pipelined(eng, n, stages, depth, straight=False, steps=2):
    first = depth + 1
    first += (n - first) % steps

    def step(t, turn=0):
        for lag, stage in stages:
            i = t - lag
            if 0 <= i and (i < n or not isinstance(turn, int)):
                stage(Tile(turn * (steps // 2) + i // 2, i % 2))

    if straight or first >= n:
        for t in range(n + depth - 1):
            step(t)
        return
    for t in range(first):
        step(t)
    with eng.Fori(0, (n - first) // steps) as turn:
        for t in range(first, first + steps):
            step(t, turn)
    for t in range(n, n + depth - 1):
        step(t)


def need(eng, sem, value):
    if not (isinstance(value, int) and value <= 0):
        eng.wait_ge(sem, value)


def need_alone(eng, m, *counts):
    counts = [(sem, value if isinstance(value, int) else eng.snap(value)) for sem, value in counts]
    if not all(isinstance(value, int) for _, value in counts):
        eng.wait_ge(m.loaded, 32)
    for sem, value in counts:
        need(eng, sem, value)


def after_first(eng, sem, turn, value):
    if not (isinstance(turn, int) and turn == 0):
        eng.wait_ge(sem, value)


def build(nc, dram):
    with ExitStack() as ctx:
        def sb(name, shape, dt=F32):
            return ctx.enter_context(nc.sbuf_tensor(name, shape, dt))

        m = Memory(nc, ctx, sb)
        ps = ctx.enter_context(nc.psum_tensor("psum", [P, 8, 512], F32))
        banks = [ps[:, n, :] for n in range(8)]
        with ExitStack() as early:
            s = SsmMemory(nc, early)
            with ExitStack() as inputs:
                s.hold_inputs(inputs)
                merge_frames(nc, dram, m, s, banks)
                project_in(nc, dram, m, s, banks)
            state_space(nc, dram, m, s, ps)
            nc.clear_and_free_semaphores(s.semaphores)
            nc.all_engine_barrier()
        with ExitStack() as late:
            w = ExpertMemory(nc, late)
            w.load(nc, dram)
            with ExitStack() as first:
                w.hold_first(nc, first)
                dispatch(nc, m, banks, 1, E1, 2 * TILES, m.pick[:, :], m.slot1, m.expert1, m.token1, T1, w)
                experts(nc, m, ps, 1, E1, T1, m.expert1, m.token1, dram["x1"], dram["y1"], [w.w_fc_high, m.w_fc_low], w.w_proj, None,
                        ACT.Gelu_apprx_tanh, (w.w_proj_loaded, 16))
            w.hold_second(nc, late)
            linear_attention(nc, dram, m, w, ps)
            choose_one(nc, m, banks)
            dispatch(nc, m, banks, 2, E2, TILES, m.pick2[:, :], None, m.expert2, m.token2, T2, None, m.score2, m.score_slot, m.out_row)
            experts(nc, m, ps, 2, E2, T2, m.expert2, m.token2, dram["x2"], dram["out"], [w.w1_high, w.w1_low], w.w2, w.b2, ACT.Gelu,
                    (w.w2_loaded, 32), (dram["h4"], m.score_slot, m.out_row))


class Memory:

    def __init__(self, nc, ctx, sb):
        table, at = constant_table()
        places, width = param_places()
        self.const = sb("const", [P, table.shape[1]])
        self.param = sb("param", [P, width])
        self.c = {n: self.const[:, a:a + w] for n, (a, w) in at.items()}
        self.p = {n: self.param[:, a:a + w] for n, (a, w) in places.items()}
        self.h = sb("h", [P, TILES, D])
        self.dt = sb("dt", [P, TILES * NH])
        self.dt_a = sb("dt_a", [P, TILES * NH])
        self.top = sb("top", [P, TILES * 2])
        self.pick = sb("pick", [P, TILES * 2])
        self.w_out = sb("w_out", [P, 3, D])
        self.w_gate = sb("w_gate", [HD, 2, E1])
        self.w_fc_low = sb("w_fc_low", [HD, E1 * 2 * HID], F32R)
        self.w_fc = self.w_fc_low[:, :].bitcast(F32)
        self.w_qkv = sb("w_qkv", [HD, 2, 3 * D])
        self.wg = sb("wg", [HD, 2, E2])
        self.gate = sb("gate", [P, TILES, 2])
        self.slot1 = sb("slot1", [P, 2 * TILES], U32)
        self.expert1 = sb("expert1", [P, T1], I32)
        self.token1 = sb("token1", [P, T1], U32)
        self.logits2 = sb("logits2", [P, TILES * E2])
        self.pick2 = sb("pick2", [P, TILES])
        self.score2 = sb("score2", [P, TILES])
        self.expert2 = sb("expert2", [P, T2], I32)
        self.token2 = sb("token2", [P, T2], U32)
        self.score_slot = sb("score_by_slot", [P, T2])
        self.out_row = sb("out_row", [P, T2], U32)
        self.loaded = ctx.enter_context(nc.semaphore("constants_loaded"))
        self.w_in_loaded = ctx.enter_context(nc.semaphore("w_in_loaded"))
        self.w_out_loaded = ctx.enter_context(nc.semaphore("w_out_loaded"))
        self.w_gate_loaded = ctx.enter_context(nc.semaphore("w_gate_loaded"))
        self.w_fc_loaded = ctx.enter_context(nc.semaphore("w_fc_loaded"))
        self.w_qkv_loaded = ctx.enter_context(nc.semaphore("w_qkv_loaded"))
        self.wg_loaded = ctx.enter_context(nc.semaphore("wg_loaded"))
        self.tables = ctx.enter_context(nc.semaphore("gelu_table_loaded"))


class ExpertMemory:

    def __init__(self, nc, ctx):
        self.w_proj = ctx.enter_context(nc.sbuf_tensor("w_proj", [P, E1 * HC * D], F32))
        self.w1_low = ctx.enter_context(nc.sbuf_tensor("w1_low", [HD + 1, E2 * 2 * HID], F32R))
        self.w1 = self.w1_low[:, :].bitcast(F32)
        self.w_proj_loaded = ctx.enter_context(nc.semaphore("w_proj_loaded"))
        self.w1_loaded = ctx.enter_context(nc.semaphore("w1_loaded"))
        self.w2_loaded = ctx.enter_context(nc.semaphore("w2_loaded"))

    def load(self, nc, dram):
        with nc.Block() as block:
            @block.sync
            def _(sp):
                sp.dma_start(self.w_proj[:, :], dram["w_proj"]).then_inc(self.w_proj_loaded, 16)
                sp.dma_start(self.w1, dram["w1"]).then_inc(self.w1_loaded, 16)

    def hold_first(self, nc, ctx):
        self.w_fc_high = ctx.enter_context(nc.sbuf_tensor("w_fc_high", [HD, E1 * 2 * HID], F32R))

    def hold_second(self, nc, ctx):
        self.w1_high = ctx.enter_context(nc.sbuf_tensor("w1_high", [HD + 1, E2 * 2 * HID], F32R))
        self.w2 = ctx.enter_context(nc.sbuf_tensor("w2", [P, E2 * HC * D], F32))
        self.b2 = ctx.enter_context(nc.sbuf_tensor("b2", [1, E2 * D], F32))


class SsmMemory:

    def __init__(self, nc, ctx):
        def sb(name, shape):
            return ctx.enter_context(nc.sbuf_tensor(name, shape, F32))

        self.nc, self.semaphores = nc, []
        self.xbc = sb("xbc", [P, 5, N_TOK])
        self.sz = sb("sz", [P, 3, N_TOK])

    def hold_inputs(self, ctx):
        def sb(name, shape):
            return ctx.enter_context(self.nc.sbuf_tensor(name, shape, F32R))

        self.w_parts = sb("w_in_parts", [HD, 2, 2, NIN - NH])
        self.ut_parts = sb("ut_parts", [HD, 2, 2, N_TOK])

    def semaphore(self, name):
        self.semaphores.append(self.nc.alloc_semaphore(name))
        return self.semaphores[-1]


def merge_frames(nc, dram, m, s, banks):
    with ExitStack() as ctx:
        def sb(name, shape, dt=F32):
            return ctx.enter_context(nc.sbuf_tensor(name, shape, dt))

        def sem(name):
            return s.semaphore(name)

        c, p = m.c, m.p
        x = sb("x_frames", [P, 2, 2, D])
        w_tok = sb("w_tok", [P, 3, 64])
        bq_sc = sb("bq_scaled", [P, 1])
        ones_row = c["ones"][0:1, 0:HD]
        qk = sb("qk", [HD, 2, 2, 2, P])
        s_m = sb("scores", [P, 2, P])
        mx = sb("row_max", [P, 2, 2])
        pr = sb("probs", [P, 2, P])
        rs = sb("row_sum", [P, 2, 2])
        pt = sb("probs_t", [P, 2, P])
        v = s.sz[:, :, :].rearrange("p c t -> p (c t)")[:, 0:TILES * D].rearrange("p (i d) -> p i d", d=D)
        w_in = s.xbc[0:HD, :, :].rearrange("p c t -> p (c t)")[:, 0:2 * NIN].rearrange("p (c n) -> p c n", c=2)
        st = sb("bn_sums", [P, 2, 2, 6])
        mv = sb("bn_mean_var", [P, 2, 2, 2])
        ve = sb("var_eps", [P, 2, 2])
        rstd = sb("rstd", [P, 2, 2])
        a = sb("normed", [P, 2, D])
        u = sb("normed_twice", [P, 2, D])
        ut = sb("ut_tile", [HD, 2, 2, P])
        ps_qk = [banks[o][0:HD, :].rearrange("p (w c t) -> p w c t", w=2, c=2) for o in range(2)]
        ps_qv = banks[2][:, 0:2 * D].rearrange("p (w d) -> p w d", w=2)
        ps_s, ps_pt, ps_o = banks[3][:, 0:P], banks[4][:, 0:P], banks[5][:, 0:D]
        ps_u = banks[6][0:HD, 0:256].rearrange("p (c t) -> p c t", c=2)
        ps_dt = banks[7][:, 0:NH]

        x_in = [sem("x_in_even"), sem("x_in_odd")]
        w_ready, b_ready = sem("w_tok_ready"), sem("bq_scaled_ready")
        qk_mm, qv_mm, s_mm, pt_mm, o_mm, u_mm, dt_mm = (sem(n) for n in (
            "qk_product", "qv_product", "score_product", "probs_transposed", "attended", "u_transposed", "dt_product"))
        qk_ev, qn_ev, vn_ev = sem("qk_out"), sem("q_rows_out"), sem("v_rows_out")
        s_bar, s_max, n_max, p_exp, pt_ev = sem("scores_barred"), sem("scores_maxed"), sem("neg_max_ready"), sem("probs_ready"), sem("probs_t_out")
        r_inv, h_out, st1, mv1, ve1, rstd1 = (sem(n) for n in ("sum_inverted", "h_ready", "sums1", "mean_var1", "var_eps1", "rstd1"))
        a_out, st2, mv2, ve2, rstd2, ha = (sem(n) for n in ("a_ready", "sums2", "mean_var2", "var_eps2", "rstd2", "h_plus_a"))
        u_out, ut_ev, ut_kept, ut_low, dt_out, w_high = (sem(n) for n in ("u_ready", "ut_out", "ut_high_ready", "ut_low_ready", "dt_out", "w_in_high_ready"))

        x_rows = dram["x"].rearrange("(i h p) d -> i p h d", h=2, p=P)

        def row(t, i):
            return t[:, bass.ds(i, 1), :].rearrange("p a d -> p (a d)")

        with nc.Block() as block:
            @block.sync
            def _(sp):
                sp.dma_start(m.const[:, :], dram["const"]).then_inc(m.loaded, 16)
                sp.dma_start(m.param[:, :], dram["param"]).then_inc(m.loaded, 16)

                def load(t):
                    need(sp, qk_mm, t.i - 1)
                    need(sp, qv_mm, t.i - 1)
                    sp.dma_start(x[:, t.odd, :, :], x_rows[bass.ds(t.i, 1), :, :, :].rearrange("a p h d -> (a p) h d")).then_inc(x_in[t.odd], 16)

                pipelined(sp, TILES, [(0, load)], 1)
                sp.dma_start(m.w_fc, dram["w_fc"]).then_inc(m.w_fc_loaded, 16)
                sp.dma_start(m.w_qkv[:, :, :], dram["w_qkv"].rearrange("(c p) n -> p c n", p=HD)).then_inc(m.w_qkv_loaded, 16)
                sp.dma_start(m.wg[:, :, :], dram["wg"].rearrange("(c p) e -> p c e", p=HD)).then_inc(m.wg_loaded, 16)

            @block.tensor
            def _(pe):
                pe.wait_ge(m.loaded, 32)
                pe.wait_ge(w_ready, 1)

                def project(t):
                    pe.wait_ge(x_in[t.odd], 16 * (t.k + 1))
                    need(pe, qk_ev, t.i - 1)
                    for ch in range(2):
                        nc.tensor.matmul(ps_qk[t.odd][:, 0, ch, :], ones_row, p["bq_row"][0:1, :], start=True, stop=False)
                        for half in range(2):
                            nc.tensor.matmul(ps_qk[t.odd][:, 0, ch, half * 64:half * 64 + 64], x[:, t.odd, half, ch * HD:(ch + 1) * HD],
                                             w_tok[:, 0, :], start=False, stop=half == 1)
                    for ch in range(2):
                        for half in range(2):
                            last = nc.tensor.matmul(ps_qk[t.odd][:, 1, ch, half * 64:half * 64 + 64], x[:, t.odd, half, ch * HD:(ch + 1) * HD],
                                                    w_tok[:, 1, :], start=True, stop=True)
                    last.then_inc(qk_mm, 1)
                    need(pe, qn_ev, t.i)
                    need(pe, vn_ev, t.i)
                    for w, col in ((0, 0), (1, 2)):
                        for half in range(2):
                            last = nc.tensor.matmul(ps_qv[half * 64:half * 64 + 64, w, :], w_tok[:, col, :],
                                                    x[:, t.odd, half, :], start=True, stop=True)
                    last.then_inc(qv_mm, 1)

                def score(t):
                    pe.wait_ge(qk_ev, t.i + 1)
                    need(pe, s_bar, t.i)
                    for ch in range(2):
                        last = nc.tensor.matmul(ps_s, qk[:, t.odd, 0, ch, :], qk[:, t.odd, 1, ch, :], start=ch == 0, stop=ch == 1)
                    last.then_inc(s_mm, 1)

                def turn_probs(t):
                    pe.wait_ge(p_exp, t.i + 1)
                    need(pe, pt_ev, t.i)
                    nc.tensor.transpose(ps_pt, pr[:, t.odd, :], c["ident"]).then_inc(pt_mm, 1)

                def attend(t):
                    pe.wait_ge(pt_ev, t.i + 1)
                    pe.wait_ge(vn_ev, t.i + 1)
                    need(pe, h_out, t.i)
                    nc.tensor.matmul(ps_o, pt[:, t.odd, :], row(v, t.i), start=True, stop=True).then_inc(o_mm, 1)

                def turn_u(t):
                    pe.wait_ge(u_out, t.i + 1)
                    need(pe, ut_kept, 2 * t.i)
                    for ch in range(2):
                        last = nc.tensor.transpose(ps_u[:, ch, :], u[:, t.odd, ch * HD:(ch + 1) * HD], c["ident"])
                    last.then_inc(u_mm, 1)

                def steps(t):
                    if isinstance(t.i, int) and t.i == 0:
                        pe.wait_ge(m.w_in_loaded, 16)
                    pe.wait_ge(ut_ev, 2 * (t.i + 1))
                    need(pe, dt_out, t.i)
                    for ch in range(2):
                        last = nc.tensor.matmul(ps_dt, ut[:, t.odd, ch, :], w_in[:, ch, NIN - NH:NIN], start=ch == 0, stop=ch == 1)
                    last.then_inc(dt_mm, 1)

                pipelined(pe, TILES, [(2, score), (3, turn_probs), (4, attend), (8, steps), (7, turn_u), (0, project)], 9)

            @block.scalar
            def _(act):
                act.dma_start(w_in, dram["w_in"].rearrange("(c p) n -> p c n", p=HD)).then_inc(m.w_in_loaded, 16)
                act.dma_start(m.w_out[:, :, :], dram["w_out"].rearrange("(c p) n -> p c n", p=P)).then_inc(m.w_out_loaded, 16)
                act.dma_start(m.w_gate[:, :, :], dram["w_gate"].rearrange("(c p) e -> p c e", p=HD)).then_inc(m.w_gate_loaded, 16)
                act.wait_ge(m.loaded, 32)
                act.wait_ge(b_ready, 1)
                act.activation(rs[:, 0, 1:2], c["ones"][:, 0:1], ACT.Exp)
                act.wait_ge(m.w_in_loaded, 16)
                act.activation(s.w_parts[:, 0, :, :], w_in[:, :, 0:NIN - NH], ACT.Identity).then_inc(w_high, 1)

                def take_rows(t):
                    act.wait_ge(qv_mm, t.i + 1)
                    act.activation(row(m.h, t.i), ps_qv[:, 0, :], ACT.Identity, bias=bq_sc[:, 0:1], scale=SC).then_inc(qn_ev, 1)
                    act.activation(row(v, t.i), ps_qv[:, 1, :], ACT.Identity, bias=p["bkv"]).then_inc(vn_ev, 1)

                def exponent(t):
                    act.wait_ge(n_max, t.i + 1)
                    need(act, pt_mm, t.i - 1)
                    act.activation(pr[:, t.odd, :], s_m[:, t.odd, :], ACT.Exp, bias=mx[:, t.odd, 1:2], scale=SC,
                                   accum_out=rs[:, t.odd, 0:1]).then_inc(p_exp, 1)

                def take_u(t):
                    act.wait_ge(u_mm, t.i + 1)
                    need(act, dt_mm, t.i - 1)
                    need(act, ut_low, t.i - 1)
                    for to, done in ((ut[:, t.odd, :, :], ut_ev), (s.ut_parts[:, 0, :, bass.ds(t.i * P, P)], ut_kept)):
                        for ch in range(2):
                            act.activation(to[:, ch, :], ps_u[:, ch, :], ACT.Identity, bias=p["ln_b"][0:HD, ch:ch + 1],
                                           scale=p["ln_w"][0:HD, ch:ch + 1]).then_inc(done, 1)

                pipelined(act, TILES, [(1, take_rows), (2, exponent), (7, take_u)], 9)

            @block.vector
            def _(dve):
                dve.wait_ge(m.loaded, 32)
                for w, name in enumerate(("wq", "wk", "wv")):
                    last = nc.vector.tensor_tensor(w_tok[:, w, :], p[name], c["frame_sel"][:, w * 64:(w + 1) * 64], ALU.mult)
                last.then_inc(w_ready, 1)
                nc.vector.tensor_scalar(bq_sc[:, :], p["bq"], SC, None, ALU.mult).then_inc(b_ready, 1)
                dve.wait_ge(m.w_in_loaded, 16)
                dve.wait_ge(w_high, 1)
                nc.vector.tensor_tensor(s.w_parts[:, 1, :, :], w_in[:, :, 0:NIN - NH], s.w_parts[:, 0, :, :], ALU.subtract)

                def take_qk(t):
                    dve.wait_ge(qk_mm, t.i + 1)
                    need(dve, s_mm, t.i - 1)
                    nc.vector.tensor_copy(qk[:, t.odd, :, :, :], ps_qk[t.odd]).then_inc(qk_ev, 1)

                def bar(t):
                    dve.wait_ge(s_mm, t.i + 1)
                    need(dve, p_exp, t.i - 1)
                    nc.vector.tensor_tensor(s_m[:, t.odd, :], ps_s, c["group_bar"], ALU.add).then_inc(s_bar, 1)

                def maxima(t):
                    dve.wait_ge(s_bar, t.i + 1)
                    nc.vector.reduce_max(mx[:, t.odd, 0:1], s_m[:, t.odd, :], AX_X).then_inc(s_max, 1)

                def negate(t):
                    dve.wait_ge(s_max, t.i + 1)
                    nc.vector.tensor_scalar(mx[:, t.odd, 1:2], mx[:, t.odd, 0:1], -SC, None, ALU.mult).then_inc(n_max, 1)

                def take_probs(t):
                    dve.wait_ge(pt_mm, t.i + 1)
                    need(dve, o_mm, t.i - 1)
                    nc.vector.tensor_copy(pt[:, t.odd, :], ps_pt).then_inc(pt_ev, 1)
                    nc.vector.reciprocal(rs[:, t.odd, 1:2], rs[:, t.odd, 0:1]).then_inc(r_inv, 1)

                def merge(t):
                    dve.wait_ge(o_mm, t.i + 1)
                    dve.wait_ge(r_inv, t.i + 1)
                    need(dve, a_out, t.i - 1)
                    dve.wait_ge(qn_ev, t.i + 1)
                    nc.vector.scalar_tensor_tensor(row(m.h, t.i), ps_o, rs[:, t.odd, 1:2], row(m.h, t.i), ALU.mult, ALU.add).then_inc(h_out, 1)

                def sums_once(t):
                    need_alone(dve, m, (h_out, t.i + 1))
                    nc.vector.bn_stats(st[:, t.odd, 0, :], row(m.h, t.i)).then_inc(st1, 1)

                def moments_once(t):
                    need_alone(dve, m, (st1, t.i + 1))
                    nc.vector.bn_aggr(mv[:, t.odd, 0, :], st[:, t.odd, 0, :]).then_inc(mv1, 1)

                def norm_once(t):
                    dve.wait_ge(rstd1, t.i + 1)
                    need(dve, ha, t.i - 1)
                    need(dve, u_out, t.i - 1)
                    nc.vector.tensor_scalar(a[:, t.odd, :], row(m.h, t.i), mv[:, t.odd, 0, 0:1], rstd[:, t.odd, 0:1], ALU.subtract, ALU.mult).then_inc(a_out, 1)

                def sums_twice(t):
                    need_alone(dve, m, (a_out, t.i + 1))
                    nc.vector.bn_stats(st[:, t.odd, 1, :], a[:, t.odd, :]).then_inc(st2, 1)

                def moments_twice(t):
                    need_alone(dve, m, (st2, t.i + 1))
                    nc.vector.bn_aggr(mv[:, t.odd, 1, :], st[:, t.odd, 1, :]).then_inc(mv2, 1)

                def norm_twice(t):
                    dve.wait_ge(rstd2, t.i + 1)
                    need(dve, u_mm, t.i - 1)
                    nc.vector.tensor_scalar(u[:, t.odd, :], a[:, t.odd, :], mv[:, t.odd, 1, 0:1], rstd[:, t.odd, 1:2], ALU.subtract, ALU.mult).then_inc(u_out, 1)

                def take_dt(t):
                    dve.wait_ge(dt_mm, t.i + 1)
                    nc.vector.tensor_tensor(m.dt[:, bass.ds(t.i * NH, NH)], ps_dt, p["dt_bias"], ALU.add).then_inc(dt_out, 1)

                pipelined(dve, TILES, [(2, bar), (1, take_qk), (2, maxima), (6, norm_twice), (2, negate), (5, norm_once), (3, take_probs), (5, sums_twice),
                                       (4, merge), (5, moments_twice), (4, sums_once), (8, take_dt), (4, moments_once)], 9)

            @block.gpsimd
            def _(pool):
                pool.wait_ge(m.loaded, 32)

                def low_part(t):
                    pool.wait_ge(ut_kept, 2 * (t.i + 1))
                    at = bass.ds(t.i * P, P)
                    nc.gpsimd.tensor_tensor(s.ut_parts[:, 1, :, at], ut[:, t.odd, :, :], s.ut_parts[:, 0, :, at], ALU.subtract).then_inc(ut_low, 1)

                def inverse_root(t, n, known, eps_done, done):
                    pool.wait_ge(known, t.i + 1)
                    nc.gpsimd.tensor_tensor(ve[:, t.odd, n:n + 1], mv[:, t.odd, n, 1:2], c["eps"], ALU.add).then_inc(eps_done, 1)
                    pool.wait_ge(eps_done, t.i + 1)
                    nc.gpsimd.tensor_tensor(rstd[:, t.odd, n:n + 1], ve[:, t.odd, n:n + 1], c["minus_half"], ALU.pow).then_inc(done, 1)

                def roots(t):
                    inverse_root(t, 0, mv1, ve1, rstd1)

                def roots_and_residual(t):
                    inverse_root(t, 1, mv2, ve2, rstd2)
                    nc.gpsimd.tensor_tensor(row(m.h, t.i), row(m.h, t.i), a[:, t.odd, :], ALU.add).then_inc(ha, 1)

                pipelined(pool, TILES, [(8, low_part), (5, roots_and_residual), (4, roots)], 9)


def project_in(nc, dram, m, s, banks):
    with ExitStack() as ctx:
        def sb(name, shape, dt=F32):
            return ctx.enter_context(nc.sbuf_tensor(name, shape, dt))

        def sem(name):
            return s.semaphore(name)

        p = m.p
        n_dt = TILES * NH
        mag, ex, one_ex, ln1, back = (sb(n, [P, n_dt]) for n in ("dt_mag", "dt_exp", "dt_one_exp", "dt_log", "dt_back"))
        e_a = sb("exp_A", [P, NH])
        pre = sb("conv_out", [P, 5, SB])
        mag_done, exp_done, one_done, log_done, back1, back2, back3, sp_done, ea_done, a_done = (sem(n) for n in (
            "dt_mag_ready", "dt_exp_ready", "dt_one_exp_ready", "dt_log_ready", "dt_rounded", "dt_lost_ready",
            "dt_log_mended", "dt_softplus_ready", "exp_A_ready", "dt_A_ready"))
        proj, gate_out, tap3, taps, conv_silu = (sem(n) for n in ("projected", "gate_ready", "last_tap_done", "taps_done", "conv_ready"))

        chunks = [("conv", 0, 3), ("conv", 1, 4), ("gate", 0, 0), ("conv", 2, 5), ("conv", 3, 6), ("gate", 1, 1), ("conv", 4, 7), ("gate", 2, 2)]
        at = {(kind, c): n for n, (kind, c, _) in enumerate(chunks)}
        bank_of = {"conv": banks[0:5], "gate": banks[5:8]}

        with nc.Block() as block:
            @block.tensor
            def _(pe):
                def superblock(j):
                    for kind, c, ch in chunks:
                        if kind == "conv":
                            after_first(pe, taps, j, 3 * (5 * (j - 1) + c + 1))
                        else:
                            after_first(pe, gate_out, j, 3 * (j - 1) + c + 1)
                        terms = [(half, w, u) for w, u in ((0, 1), (1, 0), (0, 0)) for half in range(2)]
                        for half, w, u in terms:
                            last = nc.tensor.matmul(bank_of[kind][c][:, :], s.w_parts[:, w, half, ch * P:(ch + 1) * P], s.ut_parts[:, u, half, bass.ds(j * SB, SB)],
                                                    start=(half, w, u) == terms[0], stop=(half, w, u) == terms[-1])
                        last.then_inc(proj, 1)

                superblock(0)
                with pe.Fori(1, N_TOK // SB) as j:
                    superblock(j)

            @block.scalar
            def _(act):
                act.activation(e_a[:, :], p["A_log"], ACT.Exp).then_inc(ea_done, 1)
                act.wait_ge(mag_done, 1)
                act.activation(ex[:, :], mag[:, :], ACT.Exp, scale=-1.0).then_inc(exp_done, 1)
                act.wait_ge(one_done, 1)
                act.activation(ln1[:, :], one_ex[:, :], ACT.Ln).then_inc(log_done, 1)
                act.wait_ge(ea_done, 1)
                act.wait_ge(a_done, 1)
                act.activation(e_a[:, :], p["A_log"], ACT.Silu).then_inc(ea_done, 1)

                def first_tap(j, c):
                    act.wait_ge(proj, 8 * j + at["conv", c] + 1)
                    after_first(act, conv_silu, j, 5 * (j - 1) + c + 1)
                    act.activation(pre[:, c, :], banks[c][:, :], ACT.Identity, bias=p["conv_b"][:, c:c + 1],
                                   scale=p["conv_w"][:, 4 * c + 3:4 * c + 4]).then_inc(tap3, 1)

                def silu(j, c):
                    act.wait_ge(taps, 3 * (5 * j + c + 1))
                    act.activation(s.xbc[:, c, bass.ds(j * SB, SB)], pre[:, c, :], ACT.Silu).then_inc(conv_silu, 1)

                def gate(j, c):
                    act.wait_ge(proj, 8 * j + at["gate", c] + 1)
                    act.activation(s.sz[:, c, bass.ds(j * SB, SB)], banks[5 + c][:, :], ACT.Silu).then_inc(gate_out, 1)

                def superblock(j):
                    first_tap(j, 0)
                    first_tap(j, 1)
                    silu(j, 0)
                    gate(j, 0)
                    first_tap(j, 2)
                    silu(j, 1)
                    first_tap(j, 3)
                    silu(j, 2)
                    gate(j, 1)
                    first_tap(j, 4)
                    silu(j, 3)
                    gate(j, 2)
                    silu(j, 4)

                superblock(0)
                with act.Fori(1, N_TOK // SB) as j:
                    superblock(j)

            @block.vector
            def _(dve):
                nc.vector.scalar_tensor_tensor(mag[:, :], m.dt[:, :], -1.0, m.dt[:, :], ALU.mult, ALU.max).then_inc(mag_done, 1)
                dve.wait_ge(exp_done, 1)
                nc.vector.tensor_scalar(one_ex[:, :], ex[:, :], 1.0, None, ALU.add).then_inc(one_done, 1)
                dve.wait_ge(one_done, 1)
                nc.vector.tensor_scalar(back[:, :], one_ex[:, :], -1.0, None, ALU.add).then_inc(back1, 1)
                dve.wait_ge(back1, 1)
                nc.vector.tensor_tensor(mag[:, :], ex[:, :], back[:, :], ALU.subtract).then_inc(back2, 1)
                dve.wait_ge(back2, 1)
                dve.wait_ge(log_done, 1)
                nc.vector.tensor_tensor(one_ex[:, :], ln1[:, :], mag[:, :], ALU.add).then_inc(back3, 1)
                dve.wait_ge(back3, 1)
                nc.vector.scalar_tensor_tensor(m.dt[:, :], m.dt[:, :], 0.0, one_ex[:, :], ALU.max, ALU.add).then_inc(sp_done, 1)
                dve.wait_ge(sp_done, 1)
                dve.wait_ge(ea_done, 1)
                nc.vector.scalar_tensor_tensor(m.dt_a[:, :].rearrange("p (i h) -> p i h", h=NH), m.dt[:, :].rearrange("p (i h) -> p i h", h=NH), -1.0,
                                               e_a[:, :].unsqueeze(1).to_broadcast([P, TILES, NH]), ALU.mult, ALU.mult).then_inc(a_done, 1)

                def superblock(j):
                    for c in range(5):
                        full = pre[:, c, :].rearrange("p (b t) -> p b t", t=BLK)
                        src = banks[c][:, :].rearrange("p (b t) -> p b t", t=BLK)
                        for back_by in range(1, KC):
                            if back_by == 1:
                                dve.wait_ge(tap3, 5 * j + c + 1)
                            else:
                                dve.wait_ge(taps, 3 * (5 * j + c) + back_by - 1)
                            nc.vector.scalar_tensor_tensor(full[:, :, back_by:], src[:, :, :BLK - back_by], p["conv_w"][:, 4 * c + 3 - back_by:4 * c + 4 - back_by],
                                                           full[:, :, back_by:], ALU.mult, ALU.add).then_inc(taps, 1)

                superblock(0)
                with dve.Fori(1, N_TOK // SB) as j:
                    superblock(j)


def state_space(nc, dram, m, s, ps):
    with ExitStack() as ctx:
        def sb(name, shape, dt=F32):
            return ctx.enter_context(nc.sbuf_tensor(name, shape, dt))

        def sem(name):
            return s.semaphore(name)

        c, p = m.c, m.p
        xb = sb("xbc_tile", [P, 2, 5, P])
        a_upto = sb("dt_a_upto", [P, 2, NH, BLK])
        ex = sb("decays", [P, 2, NH, BLK])
        gm = sb("bc_masked", [P, 2, P])
        mix = sb("mix", [P, 2, NH, 4, BLK])
        xt = sb("x_dt", [P, 2, DI])
        xd = sb("x_skip", [P, 2, 3, P])
        yg = sb("y_gated", [P, 2, 3, P])
        sq = sb("y_squares", [P, 2, 3, P])
        sqs = sb("y_squares_summed", [P, 2, 2, P])
        col = sb("columns", [P, 2, 8])
        st = sb("bn_sums2", [P, 2, 6])
        mv = sb("bn_mean_var2", [P, 2, 2])
        xf = sb("xf_tile", [P, 2, D])
        xft = sb("xf_turned", [HD, 2, 2, P])
        lg = sb("logits", [P, 2, E1])
        top = sb("top8", [P, 2, 8])
        ix = sb("top8_index", [P, 2, 8], U32)
        ps_d = ps[:, 0, 0:NH * BLK]
        ps_g = ps[:, 1, 0:P]
        ps_x = ps[:, 1, P:P + DI]
        ps_y = [ps[:, 2 + o, 0:DI].rearrange("p (c t) -> p c t", c=3) for o in range(2)]
        ps_o = [ps[:, 4 + o, 0:D] for o in range(2)]
        ps_q = [ps[:, 4 + o, D:D + 1] for o in range(2)]
        ps_u = ps[0:HD, 6, 0:256].rearrange("p (c t) -> p c t", c=2)
        ps_l = ps[:, 7, 0:E1]

        xb_in = [sem("xbc_in_even"), sem("xbc_in_odd")]
        (wo_ready, upto_done, d_mm, gx_mm, exp_done, g_done, x_done, mix_done, y_mm, xd_done, skip_done, gate_done, sq_done, sum2, sum3, q_mm, ms_done, rms_done,
         o_mm, h_done, sums, mean_var, eps_done, rstd_done, xf_done, u_mm, u_out, l_mm, l_out, top_done, ix_done, kept, picked) = (sem(n) for n in (
            "w_out_scaled", "dt_a_spread", "decay_sums", "bc_and_x_turned", "decays_ready", "bc_masked_ready", "x_dt_ready", "mix_ready", "y_product",
            "skip_ready", "skip_added", "y_gated_ready", "squares_ready", "two_squares_summed", "squares_summed",
            "mean_square_product", "mean_square_ready", "rms_ready", "y_out_product", "h2_ready", "sums3", "mean_var3", "var_eps3",
            "rstd3", "xf_ready", "xf_turned_mm", "xf_turned_out", "logit_product", "logits_out", "top_ready", "index_ready", "top_kept", "index_kept"))
        row_sent = [sem("xf_sent_even"), sem("xf_sent_odd")]

        def row(t, i):
            return t[:, bass.ds(i, 1), :].rearrange("p a d -> p (a d)")

        with nc.Block() as block:
            @block.sync
            def _(sp):
                def copy_tile(t):
                    need(sp, gx_mm, t.i - 1)
                    sp.dma_start(xb[:, t.odd, :, :], s.xbc[:, :, bass.ds(t.i * P, P)]).then_inc(xb_in[t.odd], 16)

                def store(t):
                    sp.wait_ge(xf_done, t.i + 1)
                    sp.dma_start(dram["x1"][bass.ds(t.i * P, P), :], xf[:, t.odd, :]).then_inc(row_sent[t.odd], 16)

                pipelined(sp, TILES, [(8, store), (0, copy_tile)], 12)
                for sent in row_sent:
                    sp.wait_ge(sent, 16 * TILES // 2)

            @block.tensor
            def _(pe):
                pe.wait_ge(wo_ready, 3)
                pe.wait_ge(m.w_gate_loaded, 16)

                def decay_and_bc(t):
                    pe.wait_ge(upto_done, t.i + 1)
                    need(pe, exp_done, t.i)
                    nc.tensor.matmul(ps_d, c["after"], a_upto[:, t.odd, :, :].rearrange("p h t -> p (h t)"), start=True, stop=True).then_inc(d_mm, 1)
                    pe.wait_ge(xb_in[t.odd], 16 * (t.k + 1))
                    need(pe, g_done, t.i)
                    need(pe, x_done, t.i)
                    nc.tensor.matmul(ps_g, xb[:, t.odd, 3, :], xb[:, t.odd, 4, :], start=True, stop=True)
                    for ch in range(3):
                        last = nc.tensor.transpose(ps_x[:, ch * P:(ch + 1) * P], xb[:, t.odd, ch, :], c["ident"])
                    last.then_inc(gx_mm, 1)

                def mix_time(t):
                    pe.wait_ge(mix_done, t.i + 1)
                    pe.wait_ge(x_done, t.i + 1)
                    need(pe, skip_done, t.i - 1)
                    for h in range(NH):
                        last = nc.tensor.matmul(ps_y[t.odd][(h % 2) * HP:(h % 2 + 1) * HP, h // 2, :], xt[:, t.odd, h * HP:(h + 1) * HP],
                                                mix[:, t.odd, h, :, :].rearrange("p b t -> p (b t)"), start=True, stop=True)
                    last.then_inc(y_mm, 1)

                def project_out(t):
                    pe.wait_ge(gate_done, t.i + 1)
                    need(pe, h_done, t.i - 1)
                    need(pe, ms_done, t.i - 1)
                    for ch in range(3):
                        last = nc.tensor.matmul(ps_o[t.odd], yg[:, t.odd, ch, :], m.w_out[:, ch, :], start=ch == 0, stop=ch == 2)
                    last.then_inc(o_mm, 1)

                def add_squares(t):
                    pe.wait_ge(sum3, t.i + 1)
                    nc.tensor.matmul(ps_q[t.odd], sqs[:, t.odd, 1, :], c["ones"][:, 0:1], start=True, stop=True).then_inc(q_mm, 1)

                def turn(t):
                    pe.wait_ge(xf_done, t.i + 1)
                    need(pe, u_out, t.i)
                    for ch in range(2):
                        last = nc.tensor.transpose(ps_u[:, ch, :], xf[:, t.odd, ch * HD:(ch + 1) * HD], c["ident"])
                    last.then_inc(u_mm, 1)

                def route(t):
                    pe.wait_ge(u_out, t.i + 1)
                    need(pe, l_out, t.i)
                    for ch in range(2):
                        last = nc.tensor.matmul(ps_l, xft[:, t.odd, ch, :], m.w_gate[:, ch, :], start=ch == 0, stop=ch == 1)
                    last.then_inc(l_mm, 1)

                pipelined(pe, TILES, [(6, add_squares), (3, mix_time), (9, turn), (10, route), (5, project_out), (1, decay_and_bc)], 12)

            @block.scalar
            def _(act):
                act.activation(col[:, 0, 7:8], c["ones"][:, 0:1], ACT.Exp)

                def decays(t):
                    act.wait_ge(d_mm, t.i + 1)
                    need(act, mix_done, t.i - 1)
                    act.activation(ex[:, t.odd, :, :].rearrange("p h t -> p (h t)"), ps_d, ACT.Exp).then_inc(exp_done, 1)

                def skips(t):
                    need(act, gate_done, t.i - 1)
                    for ch in range(3):
                        act.activation(xd[:, t.odd, ch, :], s.xbc[:, ch:ch + 1, bass.ds(t.i * P, P)].rearrange("p a t -> p (a t)"), ACT.Identity,
                                       scale=p["skip"][:, ch:ch + 1]).then_inc(xd_done, 1)

                def squares(t):
                    act.wait_ge(gate_done, t.i + 1)
                    need(act, sum3, t.i - 1)
                    act.activation(sq[:, t.odd, :, :], yg[:, t.odd, :, :], ACT.Square).then_inc(sq_done, 1)

                def take_turned(t):
                    act.wait_ge(u_mm, t.i + 1)
                    need(act, l_mm, t.i - 1)
                    act.activation(xft[:, t.odd, :, :], ps_u, ACT.Identity).then_inc(u_out, 1)

                pipelined(act, TILES, [(2, decays), (5, squares), (9, take_turned), (3, skips)], 12)

            @block.vector
            def _(dve):
                dve.wait_ge(m.w_out_loaded, 16)
                for ch in range(3):
                    nc.vector.tensor_scalar(m.w_out[:, ch, :], m.w_out[:, ch, :], p["norm_w"][:, ch:ch + 1], None, ALU.mult).then_inc(wo_ready, 1)

                def mask_bc(t):
                    dve.wait_ge(gx_mm, t.i + 1)
                    nc.vector.tensor_tensor(gm[:, t.odd, :], ps_g, c["upto_all"], ALU.mult).then_inc(g_done, 1)

                def times_dt(t):
                    need(dve, y_mm, t.i - 1)
                    nc.vector.tensor_tensor(xt[:, t.odd, :].rearrange("p (h c) -> p h c", h=NH), ps_x.rearrange("p (h c) -> p h c", h=NH),
                                            m.dt[:, bass.ds(t.i * NH, NH)].unsqueeze(2).to_broadcast([P, NH, HP]), ALU.mult).then_inc(x_done, 1)

                def mixing(t):
                    need(dve, y_mm, t.i - 1)
                    dve.wait_ge(exp_done, t.i + 1)
                    dve.wait_ge(g_done, t.i + 1)
                    wide = [P, NH, 4, BLK]
                    nc.vector.tensor_tensor(mix[:, t.odd, :, :, :], ex[:, t.odd, :, :].unsqueeze(2).to_broadcast(wide),
                                            gm[:, t.odd, :].rearrange("p (b t) -> p b t", b=4).unsqueeze(1).to_broadcast(wide), ALU.mult).then_inc(mix_done, 1)

                def add_skip(t):
                    dve.wait_ge(y_mm, t.i + 1)
                    dve.wait_ge(xd_done, 3 * (t.i + 1))
                    nc.vector.tensor_tensor(xd[:, t.odd, :, :], xd[:, t.odd, :, :], ps_y[t.odd], ALU.add).then_inc(skip_done, 1)

                def gate(t):
                    dve.wait_ge(skip_done, t.i + 1)
                    need(dve, o_mm, t.i - 1)
                    need(dve, sq_done, t.i - 1)
                    nc.vector.tensor_tensor(yg[:, t.odd, :, :], xd[:, t.odd, :, :], s.sz[:, :, bass.ds(t.i * P, P)], ALU.mult).then_inc(gate_done, 1)

                def mean_square(t):
                    dve.wait_ge(q_mm, t.i + 1)
                    need(dve, rms_done, t.i - 1)
                    nc.vector.tensor_scalar(col[:, t.odd, 0:1], ps_q[t.odd], 1.0 / DI, EPS, ALU.mult, ALU.add).then_inc(ms_done, 1)

                def residual(t):
                    dve.wait_ge(rms_done, t.i + 1)
                    need(dve, xf_done, t.i - 1)
                    nc.vector.scalar_tensor_tensor(row(m.h, t.i), ps_o[t.odd], col[:, t.odd, 1:2], row(m.h, t.i), ALU.mult, ALU.add).then_inc(h_done, 1)

                def sum_rows(t):
                    need_alone(dve, m, (h_done, t.i + 1))
                    nc.vector.bn_stats(st[:, t.odd, :], row(m.h, t.i)).then_inc(sums, 1)

                def moments(t):
                    need_alone(dve, m, (sums, t.i + 1))
                    nc.vector.bn_aggr(mv[:, t.odd, :], st[:, t.odd, :]).then_inc(mean_var, 1)

                def norm(t):
                    dve.wait_ge(rstd_done, t.i + 1)
                    need(dve, u_mm, t.i - 1)
                    need(dve, row_sent[t.odd], 16 * t.k)
                    nc.vector.tensor_scalar(xf[:, t.odd, :], row(m.h, t.i), mv[:, t.odd, 0:1], col[:, t.odd, 3:4], ALU.subtract, ALU.mult).then_inc(xf_done, 1)

                def take_logits(t):
                    dve.wait_ge(l_mm, t.i + 1)
                    need(dve, ix_done, t.i - 1)
                    need(dve, kept, t.i - 1)
                    need(dve, picked, t.i - 1)
                    nc.vector.tensor_copy(lg[:, t.odd, :], ps_l).then_inc(l_out, 1)

                def best(t):
                    need_alone(dve, m, (l_out, t.i + 1))
                    nc.vector.max(top[:, t.odd, :], lg[:, t.odd, :]).then_inc(top_done, 1)

                def best_index(t):
                    need_alone(dve, m, (top_done, t.i + 1))
                    nc.vector.max_index(ix[:, t.odd, :], top[:, t.odd, :], lg[:, t.odd, :]).then_inc(ix_done, 1)

                def keep_top(t):
                    nc.vector.tensor_copy(m.top[:, bass.ds(t.i * 2, 2)], top[:, t.odd, 0:2]).then_inc(kept, 1)

                def keep_index(t):
                    dve.wait_ge(ix_done, t.i + 1)
                    nc.vector.tensor_copy(m.pick[:, bass.ds(t.i * 2, 2)], ix[:, t.odd, 0:2]).then_inc(picked, 1)

                pipelined(dve, TILES, [(2, mask_bc), (7, residual), (11, take_logits), (2, times_dt), (6, mean_square), (11, best), (7, sum_rows), (2, mixing),
                                       (11, best_index), (11, keep_top), (7, moments), (4, add_skip), (11, keep_index), (8, norm), (4, gate)], 12)

            @block.gpsimd
            def _(pool):
                def spread(t):
                    need(pool, d_mm, t.i - 1)
                    nc.gpsimd.tensor_tensor(a_upto[:, t.odd, :, :], c["upto"].unsqueeze(1).to_broadcast([P, NH, BLK]),
                                            m.dt_a[:, bass.ds(t.i * NH, NH)].unsqueeze(2).to_broadcast([P, NH, BLK]), ALU.mult).then_inc(upto_done, 1)

                def root_of_mean_square(t):
                    pool.wait_ge(ms_done, t.i + 1)
                    need(pool, h_done, t.i - 1)
                    nc.gpsimd.tensor_tensor(col[:, t.odd, 1:2], col[:, t.odd, 0:1], c["minus_half"], ALU.pow).then_inc(rms_done, 1)

                def root_of_variance(t):
                    pool.wait_ge(mean_var, t.i + 1)
                    need(pool, xf_done, t.i - 1)
                    nc.gpsimd.tensor_tensor(col[:, t.odd, 2:3], mv[:, t.odd, 1:2], c["eps"], ALU.add).then_inc(eps_done, 1)
                    pool.wait_ge(eps_done, t.i + 1)
                    nc.gpsimd.tensor_tensor(col[:, t.odd, 3:4], col[:, t.odd, 2:3], c["minus_half"], ALU.pow).then_inc(rstd_done, 1)

                def sum_squares(t):
                    pool.wait_ge(sq_done, t.i + 1)
                    need(pool, q_mm, t.i - 1)
                    nc.gpsimd.tensor_tensor(sqs[:, t.odd, 0, :], sq[:, t.odd, 0, :], sq[:, t.odd, 1, :], ALU.add).then_inc(sum2, 1)
                    pool.wait_ge(sum2, t.i + 1)
                    nc.gpsimd.tensor_tensor(sqs[:, t.odd, 1, :], sqs[:, t.odd, 0, :], sq[:, t.odd, 2, :], ALU.add).then_inc(sum3, 1)

                pipelined(pool, TILES, [(0, spread), (5, sum_squares), (6, root_of_mean_square), (7, root_of_variance)], 12)


def dispatch(nc, m, banks, tag, n_exp, cols, pick, slot, tile_expert, tile_token, n_tiles, first=None, score=None, score_slot=None,
             out_row=None):
    with ExitStack() as ctx:
        def sb(name, shape, dt=F32):
            return ctx.enter_context(nc.sbuf_tensor(f"{name}_{tag}", shape, dt))

        def sem(name):
            return ctx.enter_context(nc.semaphore(f"{name}_{tag}"))

        c = m.c
        n = n_exp * cols
        one_hot = sb("one_hot", [P, n_exp, cols])
        counts = sb("counts", [P, n_exp, cols + 1])
        run = sb("running", [P, n_exp, cols + 1])
        ones = sb("scan_ones", [P, n_exp * (cols + 1)])
        total = sb("totals", [P, 4, n_exp])
        total_i = sb("totals_int", [P, 2, n_exp], I32)
        place = sb("places", [P, n_exp, cols])
        slot_f = sb("slots", [P, cols])
        ended = sb("ended", [P, n_tiles, n_exp])
        expert_f = sb("tile_experts", [P, n_tiles])
        slot_i = sb("slots_int", [P, 3, cols], I32)
        tile_row = sb("tile_and_row", [P, 2, cols])
        in_tile = sb("in_tile", [P, cols, n_tiles], BF16)
        kinds = 2 if score is None else 6
        tile_id = sb("in_tile_times_id", [P, cols, kinds, n_tiles], BF16)
        score_part = sb("score_parts", [P, 3, cols], BF16)
        score_rest = sb("score_rests", [P, 2, cols])
        pad_row = sb("pad_rows", [P, 2, n_tiles])
        parted, marked = sem("score_parted"), sem("scores_marked")
        in_row = sb("in_row", [P, cols, P], BF16)
        token_f = sb("tokens", [P, n_tiles])
        chunk = 8
        high_ready = sem("w_fc_high_ready")
        on_pool = 6

        def of_expert(t, e):
            return t[:, e * 2 * HID:(e + 1) * 2 * HID]

        def low_weights(eng, which, e):
            eng.wait_ge(high_ready, e + 1)
            which.tensor_tensor(of_expert(m.w_fc_low, e), of_expert(m.w_fc, e), of_expert(first.w_fc_high, e), ALU.subtract)

        picked, counted, step, gate_exp, in_tile_set, row_id_set, tile_id_set, in_row_set, tokens_mm = (sem(n) for n in (
            "picked", "counted", "dispatch_step", "gate_exp", "in_tile_set", "row_id_set", "tile_id_set", "in_row_set", "tokens_product"))
        flat = "p e a -> p (e a)"
        ps_before, ps_count = banks[0][:, 0:n], banks[1][:, 0:n]
        ps_token = banks[2][:, 0:kinds * n_tiles].rearrange("p (w t) -> p w t", w=kinds)

        with nc.Block() as block:
            @block.tensor
            def _(pe):
                pe.wait_ge(picked, 1)
                nc.tensor.matmul(ps_before, c["before"], one_hot[:, :, :].rearrange(flat), start=True, stop=True)
                nc.tensor.matmul(ps_count, c["ones"], one_hot[:, :, :].rearrange(flat), start=True, stop=True).then_inc(counted, 1)
                pe.wait_ge(row_id_set, 1)
                pe.wait_ge(tile_id_set, 1)
                if score is not None:
                    pe.wait_ge(marked, 4)
                for a in range(cols):
                    if a % chunk == 0:
                        pe.wait_ge(in_row_set, a // chunk + 1)
                    last = nc.tensor.matmul(ps_token, in_row[:, a, :], tile_id[:, a, :, :], start=a == 0, stop=a == cols - 1)
                last.then_inc(tokens_mm, 1)

            @block.scalar
            def _(act):
                def times_row():
                    act.wait_ge(in_tile_set, 1)
                    act.activation(tile_id[:, :, 0, :], in_tile[:, :, :], ACT.Identity, scale=c["row_index"]).then_inc(row_id_set, 1)

                if first:
                    act.wait_ge(step, 1)
                    act.activation(m.gate[:, :, 1], m.gate[:, :, 1], ACT.Exp).then_inc(gate_exp, 1)
                    act.wait_ge(m.w_fc_loaded, 16)
                    for e in range(E1):
                        if e == 6:
                            times_row()
                        act.activation(of_expert(first.w_fc_high, e), of_expert(m.w_fc, e), ACT.Identity).then_inc(high_ready, 1)
                else:
                    times_row()

            @block.gpsimd
            def _(pool):
                if first:
                    for e in range(on_pool):
                        low_weights(pool, nc.gpsimd, e)
                if score is not None:
                    pool.wait_ge(in_tile_set, 1)
                    nc.gpsimd.tensor_copy(tile_id[:, :, 2, :], in_tile[:, :, :]).then_inc(marked, 1)
                    pool.wait_ge(parted, 5)
                    for n in range(3):
                        nc.gpsimd.tensor_tensor(tile_id[:, :, 3 + n, :], in_tile[:, :, :], score_part[:, n, :].unsqueeze(2).to_broadcast([P, cols, n_tiles]),
                                                ALU.mult).then_inc(marked, 1)

            @block.vector
            def _(dve):
                done = [0]

                def then(ins):
                    done[0] += 1
                    ins.then_inc(step, 1)
                    dve.wait_ge(step, done[0])

                if first:
                    top = m.top[:, :].rearrange("p (i k) -> p i k", k=2)
                    then(nc.vector.tensor_tensor(m.gate[:, :, 1], top[:, :, 1], top[:, :, 0], ALU.subtract))
                nc.vector.tensor_tensor(one_hot[:, :, :], pick.unsqueeze(1).to_broadcast([P, n_exp, cols]),
                                        c["iota"][:, 0:n_exp].unsqueeze(2).to_broadcast([P, n_exp, cols]), ALU.is_equal).then_inc(picked, 1)
                then(nc.vector.memset(ones[:, :], 1.0))
                if score is not None:
                    rest = score[:, :]
                    for n in range(3):
                        nc.vector.tensor_copy(score_part[:, n, :], rest).then_inc(parted, 1)
                        if n < 2:
                            dve.wait_ge(parted, 2 * n + 1)
                            nc.vector.tensor_tensor(score_rest[:, n, :], rest, score_part[:, n, :], ALU.subtract).then_inc(parted, 1)
                            dve.wait_ge(parted, 2 * n + 2)
                            rest = score_rest[:, n, :]
                    then(nc.vector.tensor_scalar(pad_row[:, 0, :], c["iota"][:, 0:n_tiles], float(P), c["row_index"], ALU.mult, ALU.add))
                dve.wait_ge(counted, 1)
                then(nc.vector.tensor_copy(counts[:, :, 0:cols], ps_count.rearrange("p (e a) -> p e a", e=n_exp)))
                then(nc.vector.reduce_sum(total[:, 0, :], counts[:, :, 0:cols], AX_X))
                then(nc.vector.tensor_scalar(total_i[:, 0, :], total[:, 0, :], float(P - 1), None, ALU.add))
                then(nc.vector.tensor_scalar(total_i[:, 1, :], total_i[:, 0, :], 7, None, ALU.logical_shift_right))
                then(nc.vector.tensor_copy(total[:, 1, :], total_i[:, 1, :]))
                then(nc.vector.scalar_tensor_tensor(counts[:, :, cols], total[:, 1, :], float(P), total[:, 0, :], ALU.mult, ALU.subtract))
                then(nc.vector.tensor_tensor_scan(run[:, :, :].rearrange(flat), ones[:, :], counts[:, :, :].rearrange(flat), 0.0, ALU.mult, ALU.add))
                then(nc.vector.tensor_tensor(place[:, :, :], run[:, :, 0:cols], counts[:, :, 0:cols], ALU.subtract))
                then(nc.vector.tensor_tensor(place[:, :, :], place[:, :, :], ps_before.rearrange("p (e a) -> p e a", e=n_exp), ALU.add))
                then(nc.vector.tensor_tensor(place[:, :, :], place[:, :, :], one_hot[:, :, :], ALU.mult))
                then(nc.vector.reduce_sum(slot_f[:, :], place[:, :, :].rearrange("p e a -> p a e"), AX_X))
                then(nc.vector.tensor_copy(slot_i[:, 0, :], slot_f[:, :]))
                if slot is not None:
                    nc.vector.tensor_copy(slot[:, :], slot_f[:, :])
                nc.vector.tensor_scalar(slot_i[:, 1, :], slot_i[:, 0, :], 7, None, ALU.logical_shift_right).then_inc(step, 1)
                done[0] += 1
                then(nc.vector.tensor_scalar(slot_i[:, 2, :], slot_i[:, 0, :], P - 1, None, ALU.bitwise_and))
                then(nc.vector.tensor_copy(tile_row[:, :, :], slot_i[:, 1:3, :]))
                nc.vector.tensor_tensor(in_tile[:, :, :], tile_row[:, 0, :].unsqueeze(2).to_broadcast([P, cols, n_tiles]),
                                        c["iota"][:, 0:n_tiles].unsqueeze(1).to_broadcast([P, cols, n_tiles]), ALU.is_equal).then_inc(in_tile_set, 1)

                def mark_rows(a):
                    nc.vector.tensor_tensor(in_row[:, a:a + chunk, :], tile_row[:, 1, a:a + chunk].unsqueeze(2).to_broadcast([P, chunk, P]),
                                            c["iota"].unsqueeze(1).to_broadcast([P, chunk, P]), ALU.is_equal).then_inc(in_row_set, 1)

                mark_rows(0)
                dve.wait_ge(in_tile_set, 1)
                per_token = cols // TILES
                nc.vector.tensor_tensor(tile_id[:, :, 1, :].rearrange("p (i k) t -> p i k t", k=per_token),
                                        in_tile[:, :, :].rearrange("p (i k) t -> p i k t", k=per_token),
                                        c["iota"][:, 0:TILES].unsqueeze(2).unsqueeze(3).to_broadcast([P, TILES, per_token, n_tiles]), ALU.mult).then_inc(tile_id_set, 1)
                for a in range(chunk, cols, chunk):
                    mark_rows(a)
                then(nc.vector.tensor_scalar(total[:, 2, :], run[:, :, cols], 1.0 / P, None, ALU.mult))
                then(nc.vector.tensor_tensor(ended[:, :, :], c["iota"][:, 0:n_tiles].unsqueeze(2).to_broadcast([P, n_tiles, n_exp]),
                                             total[:, 2, :].unsqueeze(1).to_broadcast([P, n_tiles, n_exp]), ALU.is_ge))
                then(nc.vector.reduce_sum(expert_f[:, :], ended[:, :, :], AX_X))
                then(nc.vector.tensor_scalar(expert_f[:, :], expert_f[:, :], float(n_exp - 1), None, ALU.min))
                then(nc.vector.tensor_copy(tile_expert[:, :], expert_f[:, :]))
                if first:
                    for e in range(on_pool, E1):
                        low_weights(dve, nc.vector, e)
                dve.wait_ge(tokens_mm, 1)
                then(nc.vector.tensor_copy(token_f[:, :], ps_token[:, 0, :]))
                then(nc.vector.scalar_tensor_tensor(token_f[:, :], ps_token[:, 1, :], float(P), token_f[:, :], ALU.mult, ALU.add))
                then(nc.vector.tensor_copy(tile_token[:, :], token_f[:, :]))
                if score is not None:
                    then(nc.vector.tensor_scalar(pad_row[:, 1, :], ps_token[:, 2, :], -1.0, 1.0, ALU.mult, ALU.add))
                    then(nc.vector.scalar_tensor_tensor(pad_row[:, 1, :], pad_row[:, 0, :], float(N_TOK), pad_row[:, 1, :], ALU.add, ALU.mult))
                    then(nc.vector.tensor_tensor(pad_row[:, 1, :], pad_row[:, 1, :], token_f[:, :], ALU.add))
                    then(nc.vector.tensor_copy(out_row[:, :], pad_row[:, 1, :]))
                    then(nc.vector.tensor_copy(score_slot[:, :], ps_token[:, 5, :]))
                    for n in (4, 3):
                        then(nc.vector.tensor_tensor(score_slot[:, :], score_slot[:, :], ps_token[:, n, :], ALU.add))
                if first:
                    dve.wait_ge(gate_exp, 1)
                    then(nc.vector.tensor_scalar(m.gate[:, :, 0], m.gate[:, :, 1], 1.0, None, ALU.add))
                    then(nc.vector.reciprocal(m.gate[:, :, 0], m.gate[:, :, 0]))
                    then(nc.vector.tensor_tensor(m.gate[:, :, 1], m.gate[:, :, 1], m.gate[:, :, 0], ALU.mult))


def experts(nc, m, ps, tag, n_exp, n_tiles, tile_expert, tile_token, src, dst, w_up, w_down, b_down, gelu, down_loaded, merge=None):
    kx = w_up[0].shape[0]
    groups = [(ch, x_part, w_part) for x_part, w_part in ((1, 0), (0, 1), (0, 0)) for ch in range(2)]
    with ExitStack() as ctx:
        def sb(name, shape, dt=F32):
            return ctx.enter_context(nc.sbuf_tensor(f"{name}_{tag}", shape, dt))

        def sem(name):
            return ctx.enter_context(nc.semaphore(f"{name}_{tag}"))

        c = m.c
        x = sb("rows_in", [P, 2, D])
        xt = sb("rows_turned", [kx, 2, 2, 2, P], F32R)
        hid = sb("hidden", [P, 2, 2, HID // 2])
        ht = sb("hidden_turned", [P, 2, HC, P])
        y = sb("rows_out", [P, 2, D])
        x_in = [sem("rows_in_even"), sem("rows_in_odd")]
        y_sent = [sem("rows_sent_even"), sem("rows_sent_odd")]
        y_scaled = sem("rows_scaled")
        if merge:
            h_rows, score_slot, out_row = merge
            h = sb("residual_rows", [P, n_tiles, D])
        x_mm, x_out, x_low, up_mm, act_done, t_mm, t_out, down_mm, y_out, ones_set = (sem(n) for n in (
            "rows_turned_mm", "rows_turned_out", "rows_low_ready", "up_product", "gelu_ready",
            "hidden_turned_mm", "hidden_turned_out", "down_product", "rows_ready", "ones_set"))
        ps_x = ps[0:HD, 0, 0:256].rearrange("p (c t) -> p c t", c=2)
        ps_h = [ps[:, 1:3, 0:HID // 2], ps[:, 6:8, 0:HID // 2]]
        ps_t = [ps[:, 3, :], ps[:, 4, 0:256]]
        ps_y = ps[:, 5, 0:D]
        hidden_chunks = (slice(0, 4), slice(4, HC))

        def rows(t, i):
            return t[bass.ds(i * P, P), :]

        with nc.Block() as block:
            @block.sync
            def _(sp):
                def store(t):
                    sp.wait_ge(y_out, t.i + 1)
                    sp.dma_start(rows(dst, t.i), y[:, t.odd, :]).then_inc(y_sent[t.odd], 16)

                if not merge:
                    pipelined(sp, n_tiles, [(4, store)], 5, steps=4)
                sp.wait_ge(y_sent[0], 16 * ((n_tiles + 1) // 2))
                sp.wait_ge(y_sent[1], 16 * (n_tiles // 2))

            @block.gpsimd
            def _(pool):
                def gather(t):
                    need(pool, x_mm, t.i - 1)
                    nc.gpsimd.indirect_dma_start(out=x[:, t.odd, :], out_offset=None, in_=src,
                                                 in_offset=bass.IndirectOffsetOnAxis(ap=tile_token[:, t.i:t.i + 1], axis=0)).then_inc(x_in[t.odd], 16)

                    if merge:
                        nc.gpsimd.indirect_dma_start(out=h[:, t.i, :], out_offset=None, in_=h_rows,
                                                     in_offset=bass.IndirectOffsetOnAxis(ap=tile_token[:, t.i:t.i + 1], axis=0)).then_inc(x_in[t.odd], 16)

                def scatter(t):
                    pool.wait_ge(y_out, t.i + 1)
                    nc.gpsimd.indirect_dma_start(out=dst, out_offset=bass.IndirectOffsetOnAxis(ap=out_row[:, t.i:t.i + 1], axis=0),
                                                 in_=y[:, t.odd, :], in_offset=None).then_inc(y_sent[t.odd], 16)

                pipelined(pool, n_tiles, [(0, gather)] + ([(4, scatter)] if merge else []), 5 if merge else 1, straight=True)

            @block.tensor
            def _(pe):
                if kx > HD:
                    pe.wait_ge(ones_set, 2)

                def turn_rows(t):
                    pe.wait_ge(x_in[t.odd], (32 if merge else 16) * (t.k + 1))
                    need(pe, x_out, t.i)
                    need(pe, x_low, t.i)
                    for ch in range(2):
                        last = nc.tensor.transpose(ps_x[:, ch, :], x[:, t.odd, ch * HD:(ch + 1) * HD], c["ident"])
                    last.then_inc(x_mm, 1)

                def expert_of(t):
                    return pe.value_load(tile_expert[0:1, bass.ds(t.i, 1)], min_val=0, max_val=n_exp - 1)

                def up(t):
                    e = expert_of(t)
                    pe.wait_ge(x_out, t.i + 1)
                    pe.wait_ge(x_low, t.i + 1)
                    need(pe, act_done, t.i - 1)
                    for half in range(2):
                        for ch, x_part, w_part in groups:
                            k = kx if ch == 0 else HD
                            last = nc.tensor.matmul(ps_h[t.odd][:, half, :], xt[0:k, t.odd, x_part, ch, :],
                                                    w_up[w_part][0:k, bass.ds((e * 2 + ch) * HID + half * (HID // 2), HID // 2)],
                                                    start=(ch, x_part, w_part) == groups[0], stop=(ch, x_part, w_part) == groups[-1])
                    last.then_inc(up_mm, 1)

                def turn_hidden(t):
                    pe.wait_ge(act_done, t.i + 1)
                    need(pe, t_out, 2 * t.i)
                    for ch in range(HC):
                        half, at = ch // 3, ch % 3
                        last = nc.tensor.transpose(ps_t[ch // 4][:, (ch % 4) * P:(ch % 4 + 1) * P], hid[:, t.odd, half, at * P:(at + 1) * P], c["ident"])
                        if ch in (3, 5):
                            last.then_inc(t_mm, 1)

                def down(t):
                    if isinstance(t.i, int) and t.i == 0:
                        pe.wait_ge(*down_loaded)
                    e = expert_of(t)
                    pe.wait_ge(t_out, 2 * (t.i + 1))
                    need(pe, y_out, t.i)
                    if b_down is not None:
                        nc.tensor.matmul(ps_y, c["ones"][0:1, :], b_down[0:1, bass.ds(e * D, D)], start=True, stop=False)
                    for ch in range(HC):
                        last = nc.tensor.matmul(ps_y, ht[:, t.odd, ch, :], w_down[:, bass.ds((e * HC + ch) * D, D)], start=ch == 0 and b_down is None, stop=ch == HC - 1)
                    last.then_inc(down_mm, 1)

                pipelined(pe, n_tiles, [(4, down), (3, turn_hidden), (2, up), (1, turn_rows)], 5, steps=4)

            @block.scalar
            def _(act):
                act.activation(y[:, 0, 0:1], c["ones"][:, 0:1], gelu).then_inc(m.tables, 1)

                def take_rows(t):
                    act.wait_ge(x_mm, t.i + 1)
                    need(act, up_mm, t.i - 1)
                    act.activation(xt[0:HD, t.odd, 0, :, :], ps_x, ACT.Identity).then_inc(x_out, 1)

                def activate(t):
                    act.wait_ge(up_mm, t.i + 1)
                    need(act, t_mm, 2 * (t.i - 1))
                    act.activation(hid[:, t.odd, :, :], ps_h[t.odd], gelu).then_inc(act_done, 1)

                pipelined(act, n_tiles, [(2, activate), (1, take_rows)], 5, steps=4)

            @block.vector
            def _(dve):
                dve.wait_ge(m.tables, tag)
                if kx > HD:
                    for part in range(2):
                        nc.vector.memset(xt[HD:kx, :, part, :, :].bitcast(F32), float(part == 0)).then_inc(ones_set, 1)

                def take_hidden(t):
                    need(dve, down_mm, t.i - 1)
                    for n, chunks in enumerate(hidden_chunks):
                        dve.wait_ge(t_mm, 2 * t.i + n + 1)
                        nc.vector.tensor_copy(ht[:, t.odd, chunks, :], ps_t[n]).then_inc(t_out, 1)

                def low_rows(t):
                    need(dve, up_mm, t.i - 1)
                    dve.wait_ge(x_out, t.i + 1)
                    nc.vector.tensor_tensor(xt[0:HD, t.odd, 1, :, :], ps_x, xt[0:HD, t.odd, 0, :, :], ALU.subtract).then_inc(x_low, 1)

                def take_rows(t):
                    need(dve, y_sent[t.odd], 16 * t.k)
                    dve.wait_ge(down_mm, t.i + 1)
                    if not merge:
                        nc.vector.tensor_copy(y[:, t.odd, :], ps_y).then_inc(y_out, 1)
                        return
                    nc.vector.tensor_tensor(y[:, t.odd, :], ps_y, score_slot[:, bass.ds(t.i, 1)].to_broadcast([P, D]), ALU.mult).then_inc(y_scaled, 1)
                    dve.wait_ge(y_scaled, t.i + 1)
                    nc.vector.tensor_tensor(y[:, t.odd, :], y[:, t.odd, :], h[:, bass.ds(t.i, 1), :].rearrange("p a d -> p (a d)"), ALU.add).then_inc(y_out, 1)

                pipelined(dve, n_tiles, [(4, take_rows), (3, take_hidden), (1, low_rows)], 5, steps=4)


def linear_attention(nc, dram, m, weights, ps):
    with ExitStack() as ctx:
        def sb(name, shape, dt=F32):
            return ctx.enter_context(nc.sbuf_tensor(name, shape, dt))

        def sem(name):
            return ctx.enter_context(nc.semaphore(name))

        c, p = m.c, m.p
        gate = sb("gate_tile", [P, 2, 2])
        y = sb("expert_rows", [P, 2, 2, D])
        st = sb("bn_sums4", [P, 2, 2, 6])
        mv = sb("bn_mean_var4", [P, 2, 2, 2])
        col = sb("columns4", [P, 2, 4])
        xn = sb("xn", [P, 2, 2, D])
        xt = sb("xn_turned", [HD, 2, 2, 2, P])
        qk = sb("qk_turned", [HD, 2, 4, P])
        v = sb("v_rows", [P, 2, D])
        w = sb("weights_t", [P, 2, P])
        ps_t = [ps[0:HD, b, 0:256].rearrange("p (c t) -> p c t", c=2) for b in (0, 5)]
        ps_qk = ps[0:HD, 1, :].rearrange("p (n t) -> p n t", n=4)
        ps_v, ps_s, ps_o, ps_l = ps[:, 2, 0:D], ps[:, 3, 0:P], ps[:, 4, 0:D], ps[:, 6, 0:E2]

        y_in = [sem("expert_rows_even"), sem("expert_rows_odd")]
        w1_high_ready, h_sent = sem("w1_high_ready"), sem("h4_sent")
        row_sent = [sem("xn_b_sent_even"), sem("xn_b_sent_odd")]
        (gate_set, first_added, h3, sums_a, mv_a, eps_a, rstd_a, xn_a, t_mm_a, t_out_a, qk_mm, v_mm, qk_out, v_out, s_mm, w_out, o_mm, h4,
         sums_b, mv_b, eps_b, rstd_b, xn_b, t_mm_b, t_out_b, l_mm, l_out) = (sem(n) for n in (
            "gate_set", "first_expert_added", "h3_ready", "sums_a", "mean_var_a", "var_eps_a", "rstd_a", "xn_a_ready", "turned_a_mm",
            "turned_a_out", "qk2_product", "v2_product", "qk2_out", "v2_out", "score2_product", "weights_ready", "attended2", "h4_ready", "sums_b",
            "mean_var_b", "var_eps_b", "rstd_b", "xn_b_ready", "turned_b_mm", "turned_b_out", "logit2_product", "logits2_out"))

        def row(t, i):
            return t[:, bass.ds(i, 1), :].rearrange("p a d -> p (a d)")

        def of_expert(t, e):
            return t[:, e * 2 * HID:(e + 1) * 2 * HID]

        with nc.Block() as block:
            @block.sync
            def _(sp):
                def store(t):
                    sp.wait_ge(xn_b, t.i + 1)
                    sp.dma_start(dram["x2"][bass.ds(t.i * P, P), :], xn[:, t.odd, 1, :]).then_inc(row_sent[t.odd], 16)

                sp.dma_start(weights.w2[:, :], dram["w2"]).then_inc(weights.w2_loaded, 16)
                sp.dma_start(weights.b2[:, :], dram["b2"]).then_inc(weights.w2_loaded, 16)
                def store_h(t):
                    sp.wait_ge(h4, t.i + 1)
                    sp.dma_start(dram["h4"][bass.ds(t.i * P, P), :], row(m.h, t.i)).then_inc(h_sent, 16)

                pipelined(sp, TILES, [(9, store), (9, store_h)], 12)
                for sent in row_sent:
                    sp.wait_ge(sent, 16 * TILES // 2)
                sp.wait_ge(h_sent, 16 * TILES)

            @block.gpsimd
            def _(pool):
                def gather(t):
                    need(pool, h3, t.i - 1)
                    for k in range(2):
                        nc.gpsimd.indirect_dma_start(out=y[:, t.odd, k, :], out_offset=None, in_=dram["y1"],
                                                     in_offset=bass.IndirectOffsetOnAxis(ap=m.slot1[:, 2 * t.i + k:2 * t.i + k + 1], axis=0)).then_inc(y_in[t.odd], 16)

                def root(t, n, known, eps_done, done, used):
                    pool.wait_ge(known, t.i + 1)
                    need(pool, used, t.i - 1)
                    nc.gpsimd.tensor_tensor(col[:, t.odd, 2 * n:2 * n + 1], mv[:, t.odd, n, 1:2], c["eps"], ALU.add).then_inc(eps_done, 1)
                    pool.wait_ge(eps_done, t.i + 1)
                    nc.gpsimd.tensor_tensor(col[:, t.odd, 2 * n + 1:2 * n + 2], col[:, t.odd, 2 * n:2 * n + 1], c["minus_half"], ALU.pow).then_inc(done, 1)

                def root_a(t):
                    root(t, 0, mv_a, eps_a, rstd_a, xn_a)

                def root_b(t):
                    root(t, 1, mv_b, eps_b, rstd_b, xn_b)

                pipelined(pool, TILES, [(0, gather), (2, root_a), (8, root_b)], 12, straight=True)

            @block.vector
            def _(dve):
                for e in range(E2):
                    dve.wait_ge(w1_high_ready, e + 1)
                    nc.vector.tensor_tensor(of_expert(weights.w1_low, e), of_expert(weights.w1, e), of_expert(weights.w1_high, e), ALU.subtract)

                def set_gate(t):
                    need(dve, h3, t.i - 1)
                    nc.vector.tensor_copy(gate[:, t.odd, :], m.gate[:, bass.ds(t.i, 1), :].rearrange("p a k -> p (a k)")).then_inc(gate_set, 1)

                def add_first(t):
                    dve.wait_ge(y_in[t.odd], 32 * (t.k + 1))
                    dve.wait_ge(gate_set, t.i + 1)
                    nc.vector.scalar_tensor_tensor(row(m.h, t.i), y[:, t.odd, 0, :], gate[:, t.odd, 0:1], row(m.h, t.i), ALU.mult, ALU.add).then_inc(first_added, 1)

                def add_second(t):
                    dve.wait_ge(first_added, t.i + 1)
                    nc.vector.scalar_tensor_tensor(row(m.h, t.i), y[:, t.odd, 1, :], gate[:, t.odd, 1:2], row(m.h, t.i), ALU.mult, ALU.add).then_inc(h3, 1)

                def sum_a(t):
                    need_alone(dve, m, (h3, t.i + 1))
                    nc.vector.bn_stats(st[:, t.odd, 0, :], row(m.h, t.i)).then_inc(sums_a, 1)

                def moments_a(t):
                    need_alone(dve, m, (sums_a, t.i + 1))
                    nc.vector.bn_aggr(mv[:, t.odd, 0, :], st[:, t.odd, 0, :]).then_inc(mv_a, 1)

                def norm_a(t):
                    dve.wait_ge(rstd_a, t.i + 1)
                    need(dve, t_mm_a, t.i - 1)
                    nc.vector.tensor_scalar(xn[:, t.odd, 0, :], row(m.h, t.i), mv[:, t.odd, 0, 0:1], col[:, t.odd, 1:2], ALU.subtract, ALU.mult).then_inc(xn_a, 1)

                def take_qkv(t):
                    dve.wait_ge(qk_mm, t.i + 1)
                    need(dve, s_mm, t.i - 1)
                    nc.vector.tensor_tensor(qk[:, t.odd, :, :], ps_qk, p["b_qk"][0:HD, :].unsqueeze(2).to_broadcast([HD, 4, P]), ALU.add).then_inc(qk_out, 1)
                    dve.wait_ge(v_mm, t.i + 1)
                    need(dve, o_mm, t.i - 1)
                    nc.vector.tensor_tensor(v[:, t.odd, :], ps_v, p["b_v"], ALU.add).then_inc(v_out, 1)

                def decay(t):
                    dve.wait_ge(s_mm, t.i + 1)
                    need(dve, o_mm, t.i - 1)
                    nc.vector.tensor_tensor(w[:, t.odd, :], ps_s, c["decay"], ALU.mult).then_inc(w_out, 1)

                def residual(t):
                    dve.wait_ge(o_mm, t.i + 1)
                    need(dve, xn_b, t.i - 1)
                    nc.vector.tensor_tensor(row(m.h, t.i), row(m.h, t.i), ps_o, ALU.add).then_inc(h4, 1)

                def sum_b(t):
                    need_alone(dve, m, (h4, t.i + 1))
                    nc.vector.bn_stats(st[:, t.odd, 1, :], row(m.h, t.i)).then_inc(sums_b, 1)

                def moments_b(t):
                    need_alone(dve, m, (sums_b, t.i + 1))
                    nc.vector.bn_aggr(mv[:, t.odd, 1, :], st[:, t.odd, 1, :]).then_inc(mv_b, 1)

                def norm_b(t):
                    dve.wait_ge(rstd_b, t.i + 1)
                    need(dve, t_mm_b, t.i - 1)
                    need(dve, row_sent[t.odd], 16 * t.k)
                    nc.vector.tensor_scalar(xn[:, t.odd, 1, :], row(m.h, t.i), mv[:, t.odd, 1, 0:1], col[:, t.odd, 3:4], ALU.subtract, ALU.mult).then_inc(xn_b, 1)

                def take_logits(t):
                    dve.wait_ge(l_mm, t.i + 1)
                    nc.vector.tensor_copy(m.logits2[:, bass.ds(t.i * E2, E2)], ps_l).then_inc(l_out, 1)

                pipelined(dve, TILES, [(2, add_first), (6, take_qkv), (2, add_second), (7, decay), (2, sum_a), (8, residual), (2, moments_a),
                                       (3, norm_a), (8, sum_b), (9, norm_b), (8, moments_b), (11, take_logits), (1, set_gate)], 12)

            @block.scalar
            def _(act):
                def take_a(t):
                    act.wait_ge(t_mm_a, t.i + 1)
                    need(act, v_mm, t.i - 1)
                    act.activation(xt[:, t.odd, 0, :, :], ps_t[0], ACT.Identity).then_inc(t_out_a, 1)

                def take_b(t):
                    act.wait_ge(t_mm_b, t.i + 1)
                    need(act, l_mm, t.i - 1)
                    act.activation(xt[:, t.odd, 1, :, :], ps_t[1], ACT.Identity).then_inc(t_out_b, 1)

                act.wait_ge(weights.w1_loaded, 16)
                for e in range(E2):
                    act.activation(of_expert(weights.w1_high, e), of_expert(weights.w1, e), ACT.Identity).then_inc(w1_high_ready, 1)
                pipelined(act, TILES, [(4, take_a), (10, take_b)], 12)

            @block.tensor
            def _(pe):
                pe.wait_ge(m.w_qkv_loaded, 16)
                pe.wait_ge(m.wg_loaded, 16)

                def turn(t, n, ready, freed, done):
                    pe.wait_ge(ready, t.i + 1)
                    need(pe, freed, t.i)
                    for ch in range(2):
                        last = nc.tensor.transpose(ps_t[n][:, ch, :], xn[:, t.odd, n, ch * HD:(ch + 1) * HD], c["ident"])
                    last.then_inc(done, 1)

                def turn_a(t):
                    turn(t, 0, xn_a, t_out_a, t_mm_a)

                def turn_b(t):
                    turn(t, 1, xn_b, t_out_b, t_mm_b)

                def project(t):
                    pe.wait_ge(t_out_a, t.i + 1)
                    need(pe, qk_out, t.i)
                    for n in range(4):
                        for ch in range(2):
                            last = nc.tensor.matmul(ps_qk[:, n, :], m.w_qkv[:, ch, n * HD:(n + 1) * HD], xt[:, t.odd, 0, ch, :], start=ch == 0, stop=ch == 1)
                    last.then_inc(qk_mm, 1)
                    need(pe, v_out, t.i)
                    for ch in range(2):
                        last = nc.tensor.matmul(ps_v, xt[:, t.odd, 0, ch, :], m.w_qkv[:, ch, 2 * D:3 * D], start=ch == 0, stop=ch == 1)
                    last.then_inc(v_mm, 1)

                def score(t):
                    pe.wait_ge(qk_out, t.i + 1)
                    need(pe, w_out, t.i)
                    for ch in range(2):
                        last = nc.tensor.matmul(ps_s, qk[:, t.odd, 2 + ch, :], qk[:, t.odd, ch, :], start=ch == 0, stop=ch == 1)
                    last.then_inc(s_mm, 1)

                def attend(t):
                    pe.wait_ge(w_out, t.i + 1)
                    pe.wait_ge(v_out, t.i + 1)
                    need(pe, h4, t.i)
                    nc.tensor.matmul(ps_o, w[:, t.odd, :], v[:, t.odd, :], start=True, stop=True).then_inc(o_mm, 1)

                def route(t):
                    pe.wait_ge(t_out_b, t.i + 1)
                    need(pe, l_out, t.i)
                    for ch in range(2):
                        last = nc.tensor.matmul(ps_l, xt[:, t.odd, 1, ch, :], m.wg[:, ch, :], start=ch == 0, stop=ch == 1)
                    last.then_inc(l_mm, 1)

                pipelined(pe, TILES, [(7, score), (8, attend), (4, turn_a), (10, turn_b), (11, route), (5, project)], 12)


def choose_one(nc, m, banks):
    with ExitStack() as ctx:
        def sb(name, shape, dt=F32):
            return ctx.enter_context(nc.sbuf_tensor(name, shape, dt))

        z = sb("seq_logits", [P, TILES, E2])
        e = sb("seq_exp", [P, TILES, E2])
        best = sb("seq_best", [P, TILES])
        mean_mm = ctx.enter_context(nc.semaphore("logits_averaged"))
        exp_done = ctx.enter_context(nc.semaphore("seq_exp_ready"))
        step = ctx.enter_context(nc.semaphore("choice_step"))
        wide = [P, TILES, E2]
        with nc.Block() as block:
            @block.tensor
            def _(pe):
                nc.tensor.matmul(banks[0][:, 0:TILES * E2], m.c["seq_mean"], m.logits2[:, :], start=True, stop=True).then_inc(mean_mm, 1)

            @block.scalar
            def _(act):
                act.wait_ge(step, 3)
                act.activation(e[:, :, :], e[:, :, :], ACT.Exp).then_inc(exp_done, 1)

            @block.vector
            def _(dve):
                done = [0]

                def then(ins):
                    done[0] += 1
                    ins.then_inc(step, 1)
                    dve.wait_ge(step, done[0])

                dve.wait_ge(mean_mm, 1)
                then(nc.vector.tensor_copy(z[:, :, :].rearrange("p i e -> p (i e)"), banks[0][:, 0:TILES * E2]))
                then(nc.vector.reduce_max(best[:, :], z[:, :, :], AX_X))
                then(nc.vector.tensor_tensor(e[:, :, :], z[:, :, :], best[:, :].unsqueeze(2).to_broadcast(wide), ALU.subtract))
                then(nc.vector.tensor_tensor(z[:, :, :], z[:, :, :], best[:, :].unsqueeze(2).to_broadcast(wide), ALU.is_equal))
                then(nc.vector.scalar_tensor_tensor(z[:, :, :], z[:, :, :], -float(E2), m.c["iota"][:, 0:E2].unsqueeze(1).to_broadcast(wide), ALU.mult, ALU.add))
                then(nc.vector.tensor_reduce(best[:, :], z[:, :, :], AX_X, ALU.min))
                then(nc.vector.tensor_scalar(m.pick2[:, :], best[:, :], float(E2), None, ALU.add))
                dve.wait_ge(exp_done, 1)
                then(nc.vector.reduce_sum(best[:, :], e[:, :, :], AX_X))
                then(nc.vector.reciprocal(m.score2[:, :], best[:, :]))


def host_layout(v):
    def chunks(a, n):
        a = np.asarray(a).reshape(n, -1).T
        return np.concatenate([a, np.zeros((P - a.shape[0], n), a.dtype)]) if a.shape[0] < P else a

    wkv = v["L0_tok_Wkv"]
    rows = {
        "bq": np.tile(v["L0_tok_bq"], 16)[:, None], "bkv": np.tile(v["L0_tok_bkv"], 16)[:, None],
        "ln_w": chunks(v["L0_attn_ln_w"], 2), "ln_b": chunks(v["L0_attn_ln_b"], 2),
        "conv_w": v["L0_attn_conv_w"].reshape(5, P, KC).transpose(1, 0, 2).reshape(P, 20),
        "conv_b": chunks(v["L0_attn_conv_b"], 5), "skip": chunks(np.repeat(v["L0_attn_D"], HP), 3),
        "norm_w": chunks(v["L0_attn_norm_w"], 3), "b_qk": chunks(v["L1_attn_b_qkv"][:2 * D], 4),
        "A_log": np.tile(v["L0_attn_A_log"], (P, 1)), "dt_bias": np.tile(v["L0_attn_dt_bias"], (P, 1)),
        "bq_row": np.tile(v["L0_tok_bq"], (P, 16)), "b_v": np.tile(v["L1_attn_b_qkv"][2 * D:], (P, 1)),
        "wq": np.tile(v["L0_tok_Wq"].T, (8, 8)), "wk": np.tile(wkv[:8].T, (8, 8)), "wv": np.tile(wkv[8:].T, (8, 8)),
    }
    return {
        "x": v["x"].reshape(2 * N_TOK, D),
        "param": np.concatenate([rows[n] for n, _ in PARAMS], axis=1),
        "const": constant_table()[0],
        "w_in": v["L0_attn_W_in"],
        "w_out": v["L0_attn_W_out"],
        "w_fc": v["L0_ffn_w_fc"].reshape(2, HD, HID, E1).transpose(1, 3, 0, 2).reshape(HD, E1 * 2 * HID),
        "w_proj": v["L0_ffn_w_proj"].reshape(HC, P, D, E1).transpose(1, 3, 0, 2).reshape(P, E1 * HC * D),
        "w_gate": v["L0_ffn_w_gate"],
        "w_qkv": v["L1_attn_W_qkv"],
        "wg": v["L1_ffn_Wg"].T,
        "w1": np.concatenate([v["L1_ffn_W1"].reshape(E2, 2, HD, HID).transpose(2, 0, 1, 3).reshape(HD, E2 * 2 * HID),
                              np.stack([v["L1_ffn_b1"], np.zeros_like(v["L1_ffn_b1"])], axis=1).reshape(1, E2 * 2 * HID)]),
        "w2": v["L1_ffn_W2"].reshape(E2, HC, P, D).transpose(2, 0, 1, 3).reshape(P, E2 * HC * D),
        "b2": v["L1_ffn_b2"].reshape(1, E2 * D),
    }


OUTPUTS = {"out": (N_TOK + T2 * P, D)}
DEBUG = {}
SCRATCH = {"x1": (N_TOK, D), "y1": (T1 * P, D), "x2": (N_TOK, D), "h4": (N_TOK, D)}


def kernel(**inputs):
    import concourse.bacc as bacc
    from concourse.bass_utils import run_bass_kernel_spmd

    arrays = {n: np.ascontiguousarray(a) for n, a in host_layout({n: np.asarray(a) for n, a in inputs.items()}).items()}
    nc = bacc.Bacc("TRN2", target_bir_lowering=False, num_devices=1)
    dram = {n: nc.dram_tensor("in_" + n, a.shape, F32, kind="ExternalInput").ap() for n, a in arrays.items()}
    for n, shape in {**OUTPUTS, **DEBUG}.items():
        dram[n] = nc.dram_tensor(n, shape, F32, kind="ExternalOutput").ap()
    for n, shape in SCRATCH.items():
        dram[n] = nc.dram_tensor(n, shape, F32, kind="Internal").ap()
    build(nc, dram)
    got = run_bass_kernel_spmd(nc, [{"in_" + n: a for n, a in arrays.items()}], core_ids=[0]).results[0]
    return got["out"][:N_TOK].reshape(64, BLK, D)
```
